# Optimizing a Trainium2 kernel written in Bass

```python
import numpy as np
import jax
import jax.numpy as jnp

def _softmax(x, axis=-1):
    return jax.nn.softmax(x, axis=axis)

def _gelu(x):
    return jax.nn.gelu(x, approximate=True)

def _silu(x):
    return jax.nn.silu(x)

def _sigmoid(x):
    return jax.nn.sigmoid(x)

def _layernorm(x, axis=-1, eps=1e-05):
    m = jnp.mean(x, axis=axis, keepdims=True)
    v = jnp.var(x, axis=axis, keepdims=True)
    return (x - m) / jnp.sqrt(v + eps)

def _scatter_add(tgt, idx, src, axis=0):
    return tgt.at[idx].add(src)

def _segment_sum(src, seg, n):
    return jax.ops.segment_sum(src, seg, n)
kernel_name = 'mk_prb_d1_jaxref_r4_a04eaa'

def setup_inputs(seed: int=0):
    np.random.seed(seed)
    _w = jnp.asarray

    def _L0_attn_setup():
        import jax, jax.numpy as jnp
        import numpy as np
        B, L, E, H, WINDOW = (4, 256, 256, 16, 4)
        D = E // H
        SCALING = D ** (-0.5)

        def _get_relative_embeddings(emb, length):
            pad_length = max(length - (WINDOW + 1), 0)
            if pad_length > 0:
                emb = jnp.pad(emb, ((0, 0), (pad_length, pad_length), (0, 0)))
            start = max(WINDOW + 1 - length, 0)
            return emb[:, start:start + 2 * length - 1]

        def _rel_to_abs(x):
            bh, length, _ = x.shape
            x = jnp.pad(x, ((0, 0), (0, 0), (0, 1)))
            xf = x.reshape(bh, length * 2 * length)
            xf = jnp.pad(xf, ((0, 0), (0, length - 1)))
            xfin = xf.reshape(bh, length + 1, 2 * length - 1)
            return xfin[:, :length, length - 1:]

        def _abs_to_rel(x):
            bh, length, _ = x.shape
            x = jnp.pad(x, ((0, 0), (0, 0), (0, length - 1)))
            xf = x.reshape(bh, length * (2 * length - 1))
            xf = jnp.pad(xf, ((0, 0), (length, 0)))
            xfin = xf.reshape(bh, length, 2 * length)
            return xfin[:, :, 1:]
        key = jax.random.key(seed)
        ks = jax.random.split(key, 12)
        s = E ** (-0.5)
        return {'hidden_states': jax.random.normal(ks[0], (B, L, E), dtype=jnp.float32), 'Wq': jax.random.normal(ks[1], (E, E), dtype=jnp.float32) * s, 'bq': jnp.zeros((E,), dtype=jnp.float32), 'Wk': jax.random.normal(ks[2], (E, E), dtype=jnp.float32) * s, 'bk': jnp.zeros((E,), dtype=jnp.float32), 'Wv': jax.random.normal(ks[3], (E, E), dtype=jnp.float32) * s, 'bv': jnp.zeros((E,), dtype=jnp.float32), 'Wo': jax.random.normal(ks[4], (E, E), dtype=jnp.float32) * s, 'bo': jnp.zeros((E,), dtype=jnp.float32), 'emb_rel_k': jax.random.normal(ks[5], (1, 2 * WINDOW + 1, D), dtype=jnp.float32) * SCALING, 'emb_rel_v': jax.random.normal(ks[6], (1, 2 * WINDOW + 1, D), dtype=jnp.float32) * SCALING}
    _L0_attn_in = _L0_attn_setup()

    def _L0_ffn_setup():
        import jax, jax.numpy as jnp
        import numpy as np
        HIDDEN = 256
        FFN = 1024
        NUM_EXPERTS = 8
        TOP_K = 2
        BATCH, SEQ = (2, 512)
        key = jax.random.key(seed)
        ks = jax.random.split(key, 6)
        s_h = 1.0 / np.sqrt(HIDDEN)
        s_f = 1.0 / np.sqrt(FFN)
        return {'hidden_states': jax.random.normal(ks[0], (BATCH, SEQ, HIDDEN), jnp.float32), 'gate_w': jax.random.uniform(ks[1], (HIDDEN, NUM_EXPERTS), jnp.float32, -s_h, s_h), 'gate_b': jax.random.uniform(ks[2], (NUM_EXPERTS,), jnp.float32, -s_h, s_h), 'w1': jax.random.uniform(ks[3], (NUM_EXPERTS, HIDDEN, FFN), jnp.float32, -s_h, s_h), 'w3': jax.random.uniform(ks[4], (NUM_EXPERTS, HIDDEN, FFN), jnp.float32, -s_h, s_h), 'w2': jax.random.uniform(ks[5], (NUM_EXPERTS, FFN, HIDDEN), jnp.float32, -s_f, s_f)}
    _L0_ffn_in = _L0_ffn_setup()
    _d = {'L0_attn_hidden_states': _L0_attn_in['hidden_states'], 'L0_attn_Wq': _L0_attn_in['Wq'], 'L0_attn_bq': _L0_attn_in['bq'], 'L0_attn_Wk': _L0_attn_in['Wk'], 'L0_attn_bk': _L0_attn_in['bk'], 'L0_attn_Wv': _L0_attn_in['Wv'], 'L0_attn_bv': _L0_attn_in['bv'], 'L0_attn_Wo': _L0_attn_in['Wo'], 'L0_attn_bo': _L0_attn_in['bo'], 'L0_attn_emb_rel_k': _L0_attn_in['emb_rel_k'], 'L0_attn_emb_rel_v': _L0_attn_in['emb_rel_v'], 'L0_ffn_gate_w': _L0_ffn_in['gate_w'], 'L0_ffn_gate_b': _L0_ffn_in['gate_b'], 'L0_ffn_w1': _L0_ffn_in['w1'], 'L0_ffn_w3': _L0_ffn_in['w3'], 'L0_ffn_w2': _L0_ffn_in['w2']}
    _x0 = _d['L0_attn_hidden_states']
    _d['L0_attn_hidden_states'] = jax.random.normal(jax.random.fold_in(jax.random.key(seed), 1), (4, 1024, 256), dtype=_x0.dtype)
    del _x0
    return _d

def reference(L0_attn_hidden_states, L0_attn_Wq, L0_attn_bq, L0_attn_Wk, L0_attn_bk, L0_attn_Wv, L0_attn_bv, L0_attn_Wo, L0_attn_bo, L0_attn_emb_rel_k, L0_attn_emb_rel_v, L0_ffn_gate_w, L0_ffn_gate_b, L0_ffn_w1, L0_ffn_w3, L0_ffn_w2):

    def _L0_attn_ref(hidden_states, Wq, bq, Wk, bk, Wv, bv, Wo, bo, emb_rel_k, emb_rel_v):
        import jax, jax.numpy as jnp
        import numpy as np
        B, L, E, H, WINDOW = (4, 256, 256, 16, 4)
        D = E // H
        SCALING = D ** (-0.5)

        def _get_relative_embeddings(emb, length):
            pad_length = max(length - (WINDOW + 1), 0)
            if pad_length > 0:
                emb = jnp.pad(emb, ((0, 0), (pad_length, pad_length), (0, 0)))
            start = max(WINDOW + 1 - length, 0)
            return emb[:, start:start + 2 * length - 1]

        def _rel_to_abs(x):
            bh, length, _ = x.shape
            x = jnp.pad(x, ((0, 0), (0, 0), (0, 1)))
            xf = x.reshape(bh, length * 2 * length)
            xf = jnp.pad(xf, ((0, 0), (0, length - 1)))
            xfin = xf.reshape(bh, length + 1, 2 * length - 1)
            return xfin[:, :length, length - 1:]

        def _abs_to_rel(x):
            bh, length, _ = x.shape
            x = jnp.pad(x, ((0, 0), (0, 0), (0, length - 1)))
            xf = x.reshape(bh, length * (2 * length - 1))
            xf = jnp.pad(xf, ((0, 0), (length, 0)))
            xfin = xf.reshape(bh, length, 2 * length)
            return xfin[:, :, 1:]
        bsz, tgt_len, _ = hidden_states.shape

        def shape(t):
            return t.reshape(bsz, tgt_len, H, D).transpose(0, 2, 1, 3).reshape(bsz * H, tgt_len, D)
        q = shape((hidden_states @ Wq + bq) * SCALING)
        k = shape(hidden_states @ Wk + bk)
        v = shape(hidden_states @ Wv + bv)
        src_len = k.shape[1]
        attn_weights = jnp.einsum('btd,bsd->bts', q, k)
        rel_k = _get_relative_embeddings(emb_rel_k, src_len)
        rel_logits = jnp.einsum('btd,md->btm', q, rel_k[0])
        attn_weights = attn_weights + _rel_to_abs(rel_logits)
        attn_probs = jax.nn.softmax(attn_weights, axis=-1)
        attn_output = jnp.einsum('bts,bsd->btd', attn_probs, v)
        rel_v = _get_relative_embeddings(emb_rel_v, src_len)
        rel_weights = _abs_to_rel(attn_probs)
        attn_output = attn_output + jnp.einsum('btm,md->btd', rel_weights, rel_v[0])
        out = attn_output.reshape(bsz, H, tgt_len, D).transpose(0, 2, 1, 3).reshape(bsz, tgt_len, E)
        return out @ Wo + bo

    def _L0_ffn_ref(hidden_states, gate_w, gate_b, w1, w3, w2):
        import jax, jax.numpy as jnp
        import numpy as np
        HIDDEN = 256
        FFN = 1024
        NUM_EXPERTS = 8
        TOP_K = 2
        BATCH, SEQ = (2, 512)
        B, S, D = hidden_states.shape
        T = B * S
        x = hidden_states.reshape(T, D)
        logits = x @ gate_w + gate_b
        probs = jax.nn.softmax(logits.astype(jnp.float32), axis=-1)
        top_w, top_idx = jax.lax.top_k(probs, TOP_K)
        top_w = top_w / jnp.sum(top_w, axis=-1, keepdims=True)
        combine = jnp.zeros((T, NUM_EXPERTS), jnp.float32)
        combine = combine.at[jnp.arange(T)[:, None], top_idx].set(top_w)
        combine = combine.astype(x.dtype)
        h = jax.nn.silu(jnp.einsum('td,edf->tef', x, w1)) * jnp.einsum('td,edf->tef', x, w3)
        out_e = jnp.einsum('tef,efd->ted', h, w2)
        out = jnp.einsum('ted,te->td', out_e, combine)
        return out.reshape(B, S, D)
    x = L0_attn_hidden_states
    xn = _layernorm(x, axis=-1)
    x = x + _L0_attn_ref(xn, L0_attn_Wq, L0_attn_bq, L0_attn_Wk, L0_attn_bk, L0_attn_Wv, L0_attn_bv, L0_attn_Wo, L0_attn_bo, L0_attn_emb_rel_k, L0_attn_emb_rel_v) + _L0_ffn_ref(xn, L0_ffn_gate_w, L0_ffn_gate_b, L0_ffn_w1, L0_ffn_w3, L0_ffn_w2)
    return x

_drawn_inputs = setup_inputs


def setup_inputs(seed=0):
    import zlib

    import numpy as np

    out = dict(_drawn_inputs(seed))
    spreads = {'L0_attn_bq': (0.0, 0.8),
     'L0_attn_bk': (0.0, 0.8),
     'L0_attn_bv': (0.0, 0.1),
     'L0_attn_bo': (0.0, 0.1)}
    factors = {'L0_attn_emb_rel_k': 8.0, 'L0_attn_emb_rel_v': 8.0, 'L0_ffn_gate_b': 3.805}
    for name, (base, spread) in spreads.items():
        noise = np.random.default_rng([zlib.crc32(name.encode()), seed]).standard_normal(out[name].shape)
        drawn = base * np.exp(spread * noise) if base else spread * noise
        out[name] = jnp.asarray(drawn.astype(out[name].dtype))
    for name, factor in factors.items():
        out[name] = (out[name] * factor).astype(out[name].dtype)
    return out
```

```python
import concourse.bass as bass
from concourse import mybir
from contextlib import ExitStack

F32 = mybir.dt.float32
BF16 = mybir.dt.bfloat16
ALU = mybir.AluOpType
ACT = mybir.ActivationFunctionType
AX = mybir.AxisListType

P = 128
NB, L, E = 4, 1024, 256
H, D = 16, 16
T = NB * L
NT = T // P
TB = L // P
KC = E // P
CH = 512
NC = T // CH
CT = CH // P
W = 4
NM = 2 * W + 1
HG = 4
NG = NB * H // HG
VW = 32
ROWS = 6 * D
MROWS = 2
BW = P + 2 * W
X = 8
F = 1024
FC = F // P
TS = 2 * P
NS = 2 * T // TS + X - 1
FAR = -1e30
EPS = 1e-5
Q_PARTS = (0, 0, 0, 1, 1, 2)
K_PARTS = (0, 1, 2, 0, 1, 0)


def after(eng, sem, value):
    if not (isinstance(value, int) and value <= 0):
        eng.wait_ge(sem, value)


def scratch(nc):
    def dram(name, shape, dt):
        return nc.dram_tensor(name, shape, dt, kind="Internal").ap()
    return dict(
        xn=dram("xn_rows", [T, E], F32),
        q=dram("q_rows", [T, E], F32),
        k=dram("k_rows", [W + T + W, E], F32),
        v=dram("v_rows", [W + T + W, E], F32),
        vx=dram("vx_rows", [T, H * VW], F32),
        sq=dram("q_stack", [NB, H // HG, HG, ROWS, L], BF16),
        sk=dram("k_stack", [NB, H // HG, HG, ROWS, L], BF16),
        xs=dram("slot_rows", [NS * TS, E], F32),
        ys=dram("slot_outputs", [NS * TS, E], F32),
    )


def norm_and_project(nc, c, dr, x, Wq, bq, Wk, bk, Wv, bv, rel_k, gate_w, gate_b, band, logits):
    with ExitStack() as ctx:
        def sb(name, shape, dt=F32):
            return ctx.enter_context(nc.sbuf_tensor("a_" + name, shape, dt))

        def ps(name, shape, dt=F32):
            return ctx.enter_context(nc.psum_tensor("a_" + name, shape, dt))

        def sem(name):
            return ctx.enter_context(nc.semaphore("a_" + name))

        w = {n: sb("w" + n, [P, KC, E]) for n in "qkv"}
        bcol = sb("bcol", [P, 2, KC])
        gw = sb("gw", [P, KC, X])
        gb = sb("gb", [P, X])
        bvb = sb("bvb", [P, E])
        relk = sb("relk", [P, NM])
        hmask = sb("hmask", [P, 8])
        rk = sb("rk", [P, NM, 8])
        zpad = sb("zpad", [W, E])
        xt = sb("xt", [P, CT, E])
        st = sb("st", [P, CT, 6])
        mv = sb("mv", [P, 3, CT])
        std = sb("std", [P, CT])
        rstd = sb("rstd", [P, CT])
        xn = sb("xn", [P, CT, E])
        xnT = sb("xnT", [P, KC, CH])
        qkT = sb("qkT", [P, 2 * KC, CH])
        rest = sb("rest", [P, 2 * KC, CH])
        part = [sb(f"part{i}", [P, 2 * KC, CH], BF16) for i in range(3)]
        vrow = sb("vrow", [P, CT, E])
        vx = sb("vx", [P, CT, H, VW])
        qrow = sb("qrow", [P, CT, E])
        krow = sb("krow", [P, CT, E])
        pT = ps("pT", [P, 2, CH])
        pqk = ps("pqk", [P, 2 * KC, CH])
        pv = ps("pv", [P, 2, CH])

        w_in, const_ok, x_in = sem("w_in"), sem("const_ok"), sem("x_in")
        dchain, var_ok, std_ok, xn_ok = sem("dchain"), sem("var_ok"), sem("std_ok"), sem("xn_ok")
        tp_ok, xnT_ok, qk_ok, v_ok, qkT_ok = sem("tp_ok"), sem("xnT_ok"), sem("qk_ok"), sem("v_ok"), sem("qkT_ok")
        rows_ok, rel_ok, qrow_ok, krow_ok = sem("rows_ok"), sem("rel_ok"), sem("qrow_ok"), sem("krow_ok")
        v_out, parts_ok, rel_out = sem("v_out"), sem("parts_ok"), sem("rel_out")
        st_xn, st_parts, st_rows, st_v, st_pad = (
            sem("st_xn"), sem("st_parts"), sem("st_rows"), sem("st_v"), sem("st_pad"))
        achain, bias_ok = sem("achain"), sem("bias_ok")

        x_v = x.rearrange("(n i p) e -> n p i e", p=P, i=CT)

        def rows_view(a, off=0):
            return a[off:off + T, :].rearrange("(n i p) e -> n p i e", p=P, i=CT)
        N_LOAD = 3 + 2 + 1 + 8 + 2
        RELW = NM * H
        RG = RELW + X

        with nc.Block() as block:
            @block.sync
            def _(sp):
                for n, src in (("q", Wq), ("k", Wk), ("v", Wv)):
                    sp.dma_start(w[n][:], src.rearrange("(k p) e -> p k e", p=P)).then_inc(w_in, 16)
                for i, src in enumerate((bq, bk)):
                    sp.dma_start(bcol[:, i, :], src.rearrange("(k p) -> p k", p=P),
                                 allow_slow_non_contiguous=True).then_inc(w_in, 16)
                sp.dma_start(bvb[:], bv.rearrange("(o e) -> o e", o=1).broadcast_to([P, E])).then_inc(w_in, 16)
                for h in range(8):
                    sp.dma_start(relk[h * D:(h + 1) * D, :], rel_k[0].rearrange("m d -> d m"),
                                 allow_slow_non_contiguous=True).then_inc(w_in, 16)
                sp.dma_start(gw[:], gate_w.rearrange("(k p) e -> p k e", p=P)).then_inc(w_in, 16)
                sp.dma_start(gb[:], gate_b.rearrange("(o e) -> o e", o=1).broadcast_to([P, X])).then_inc(w_in, 16)
                sp.wait_ge(const_ok, 1)
                for a in (dr["k"], dr["v"]):
                    for r in (0, W + T):
                        sp.dma_start(a[r:r + W, :], zpad[:]).then_inc(st_pad, 16)
                sp.dma_start(xt[:], x_v[0]).then_inc(x_in, 16)

                def chunk(b, u, more=True):
                    n = 2 * b + u
                    sp.wait_ge(xn_ok, n + 1)
                    if more:
                        sp.dma_start(xt[:], x_v[n + 1]).then_inc(x_in, 16)
                    sp.dma_start(rows_view(dr["xn"])[n], xn[:]).then_inc(st_xn, 16)
                    sp.wait_ge(v_out, n + 1)
                    sp.dma_start(rows_view(dr["v"], W)[n], vrow[:]).then_inc(st_v, 16)
                    sp.dma_start(rows_view(dr["vx"])[n], vx[:].rearrange("p i h v -> p i (h v)")).then_inc(st_v, 16)
                    sp.wait_ge(parts_ok, n + 1)
                    for j in range(6):
                        for a, (stack, parts) in enumerate(((dr["sq"], Q_PARTS), (dr["sk"], K_PARTS))):
                            for k in range(KC):
                                dst = stack[b, 2 * k:2 * k + 2, :, j * D:(j + 1) * D, u * CH:(u + 1) * CH].rearrange(
                                    "g h d c -> (g h) d c")
                                sp.dma_start(dst, part[parts[j]][:, a * KC + k, :]).then_inc(st_parts, 16)
                    sp.wait_ge(krow_ok, n + 1)
                    sp.dma_start(rows_view(dr["k"], W)[n], krow[:]).then_inc(st_rows, 16)
                    sp.wait_ge(qrow_ok, n + 1)
                    sp.dma_start(rows_view(dr["q"])[n], qrow[:]).then_inc(st_rows, 16)
                with sp.Fori(0, NB - 1) as b:
                    chunk(b, 0)
                    chunk(b, 1)
                chunk(NB - 1, 0)
                chunk(NB - 1, 1, more=False)
                sp.wait_ge(st_pad, 64)
                sp.wait_ge(st_xn, 16 * NC)
                sp.wait_ge(st_v, 32 * NC)
                sp.wait_ge(st_parts, 16 * 24 * NC)
                sp.wait_ge(st_rows, 32 * NC)

            @block.gpsimd
            def _(pool):
                nc.gpsimd.memset(zpad[:], 0.0).then_inc(const_ok, 1)
                nc.gpsimd.memset(vx[:], 0.0).then_inc(const_ok, 1)
                pool.wait_ge(const_ok, 2)
                nc.gpsimd.memset(vx[:, :, :, D:D + 1], 1.0).then_inc(const_ok, 1)
                nc.gpsimd.memset(hmask[:], 1.0).then_inc(const_ok, 1)
                pool.wait_ge(const_ok, 4)
                nc.gpsimd.affine_select(out=hmask[:], in_=hmask[:], compare_op=ALU.is_ge, fill=0.0, base=0,
                                        pattern=[[-D, 8]], channel_multiplier=1).then_inc(const_ok, 1)
                pool.wait_ge(const_ok, 5)
                nc.gpsimd.affine_select(out=hmask[:], in_=hmask[:], compare_op=ALU.is_ge, fill=0.0, base=D - 1,
                                        pattern=[[D, 8]], channel_multiplier=-1).then_inc(const_ok, 1)
                pool.wait_ge(const_ok, 6)
                pool.wait_ge(w_in, 16 * N_LOAD)
                nc.gpsimd.tensor_tensor(rk[:], relk[:].rearrange("p (m o) -> p m o", o=1).broadcast_to([P, NM, 8]),
                                        hmask[:].rearrange("p (o h) -> p o h", o=1).broadcast_to([P, NM, 8]),
                                        ALU.mult).then_inc(const_ok, 1)

            @block.vector
            def _(dve):
                dve.wait_ge(w_in, 16 * N_LOAD)
                dve.wait_ge(const_ok, 3)
                with dve.Fori(0, NC) as n:
                    STEPS = 4

                    def link(ins, k):
                        ins.then_inc(dchain, 1)
                        dve.wait_ge(dchain, n * STEPS + k)
                    dve.wait_ge(x_in, 16 * n + 16)
                    for i in range(CT - 1):
                        nc.vector.bn_stats(st[:, i, :], xt[:, i, :])
                    link(nc.vector.bn_stats(st[:, CT - 1, :], xt[:, CT - 1, :]), 1)
                    nc.vector.tensor_tensor(mv[:, 0, :], st[:, :, 1], st[:, :, 4], ALU.add)
                    nc.vector.tensor_tensor(mv[:, 1, :], st[:, :, 1], st[:, :, 4], ALU.subtract)
                    link(nc.vector.tensor_tensor(mv[:, 2, :], st[:, :, 2], st[:, :, 5], ALU.add), 2)
                    nc.vector.tensor_scalar(mv[:, 0, :], mv[:, 0, :], 0.5, None, ALU.mult)
                    nc.vector.tensor_scalar(mv[:, 2, :], mv[:, 2, :], 1.0 / E, EPS, ALU.mult, ALU.add)
                    link(nc.vector.scalar_tensor_tensor(out=mv[:, 1, :], in0=mv[:, 1, :], scalar=0.25, in1=mv[:, 1, :],
                                                        op0=ALU.mult, op1=ALU.mult), 3)
                    nc.vector.tensor_tensor(std[:], mv[:, 1, :], mv[:, 2, :], ALU.add).then_inc(var_ok, 1)
                    dve.wait_ge(std_ok, n + 1)
                    link(nc.vector.reciprocal(rstd[:], std[:]), 4)
                    dve.wait_ge(tp_ok, n)
                    dve.wait_ge(st_xn, 16 * n)
                    for i in range(CT):
                        last = nc.vector.tensor_scalar(xn[:, i, :], xt[:, i, :], mv[:, 0, i:i + 1], rstd[:, i:i + 1],
                                                       ALU.subtract, ALU.mult)
                    last.then_inc(xn_ok, 1)
                    dve.wait_ge(v_ok, n + 1)
                    dve.wait_ge(st_v, 32 * n)
                    for u in range(2):
                        src = pv[:, u, :].rearrange("p (i e) -> p i e", i=2)
                        b = bvb[:].rearrange("p (o e) -> p o e", o=1).broadcast_to([P, 2, E])
                        nc.vector.tensor_tensor(vrow[:, 2 * u:2 * u + 2, :], src, b, ALU.add)
                        for i in range(2):
                            last = nc.vector.tensor_tensor(
                                vx[:, 2 * u + i, :, 0:D], src[:, i, :].rearrange("p (h d) -> p h d", d=D),
                                bvb[:].rearrange("p (h d) -> p h d", d=D), ALU.add)
                    last.then_inc(v_out, 1)
                    dve.wait_ge(qkT_ok, n + 1)
                    dve.wait_ge(st_parts, 16 * 24 * n)
                    nc.vector.tensor_copy(part[0][:], qkT[:]).then_inc(achain, 1)
                    dve.wait_ge(achain, 3 * n + 1)
                    nc.vector.tensor_tensor(rest[:], qkT[:], part[0][:], ALU.subtract).then_inc(achain, 1)
                    dve.wait_ge(achain, 3 * n + 2)
                    nc.vector.tensor_copy(part[1][:], rest[:]).then_inc(achain, 1)
                    dve.wait_ge(achain, 3 * n + 3)
                    nc.vector.tensor_tensor(part[2][:], rest[:], part[1][:], ALU.subtract).then_inc(parts_ok, 1)
                    dve.wait_ge(rel_ok, n + 1)
                    for i in range(CT):
                        o = (i % 2) * RG
                        nc.vector.tensor_tensor(logits[:, n * CT + i, :], pT[:, i // 2, o + RELW:o + RG], gb[:], ALU.add)
                        src = pT[:, i // 2, o:o + RELW].rearrange("p (c m h) -> p c m h", c=2, m=NM)
                        for k in range(KC):
                            last = nc.vector.tensor_tensor(
                                band[:, n * CT + i, :, k * 8:(k + 1) * 8], src[:, k, :, :],
                                c["edge"][:, n * CT + i, :].rearrange("p (m o) -> p m o", o=1).broadcast_to([P, NM, 8]),
                                ALU.add)
                    last.then_inc(rel_out, 1)
                    dve.wait_ge(rows_ok, n + 1)
                    dve.wait_ge(st_rows, 32 * n)
                    for u in range(2):
                        last = nc.vector.tensor_copy(krow[:, 2 * u:2 * u + 2, :],
                                                     pqk[:, 2 + u, :].rearrange("p (i e) -> p i e", i=2))
                    last.then_inc(krow_ok, 1)

            @block.scalar
            def _(act):
                act.wait_ge(w_in, 16 * N_LOAD)
                nc.scalar.mul(bcol[:, 0, :], bcol[:, 0, :], float(D) ** -0.5).then_inc(bias_ok, 1)
                act.wait_ge(bias_ok, 1)
                with act.Fori(0, NC) as n:
                    act.wait_ge(var_ok, n + 1)
                    nc.scalar.activation(std[:], std[:], ACT.Sqrt).then_inc(std_ok, 1)
                    act.wait_ge(tp_ok, n + 1)
                    act.wait_ge(rel_ok, n)
                    for k in range(KC):
                        last = nc.scalar.copy(xnT[:, k, :], pT[:, k, :])
                    last.then_inc(xnT_ok, 1)
                    act.wait_ge(qk_ok, n + 1)
                    act.wait_ge(parts_ok, n)
                    act.wait_ge(rel_ok, n)
                    for a in range(2 * KC):
                        last = nc.scalar.activation(qkT[:, a, :], pqk[:, a, :], ACT.Identity,
                                                    bias=bcol[:, a // KC, a % KC:a % KC + 1],
                                                    scale=float(D) ** -0.5 if a < KC else 1.0)
                    last.then_inc(qkT_ok, 1)
                    act.wait_ge(rows_ok, n + 1)
                    act.wait_ge(st_rows, 32 * n)
                    for u in range(2):
                        last = nc.scalar.copy(qrow[:, 2 * u:2 * u + 2, :],
                                              pqk[:, u, :].rearrange("p (i e) -> p i e", i=2))
                    last.then_inc(qrow_ok, 1)

            @block.tensor
            def _(pe):
                pe.wait_ge(w_in, 16 * N_LOAD)
                pe.wait_ge(const_ok, 7)
                with pe.Fori(0, NC) as n:
                    pe.wait_ge(xn_ok, n + 1)
                    pe.wait_ge(rel_out, n)
                    for k in range(KC):
                        for i in range(CT):
                            last = nc.tensor.transpose(pT[:, k, i * P:(i + 1) * P], xn[:, i, k * P:(k + 1) * P], c["ident"][:])
                    last.then_inc(tp_ok, 1)
                    pe.wait_ge(xnT_ok, n + 1)
                    pe.wait_ge(krow_ok, n)
                    pe.wait_ge(qrow_ok, n)
                    for a in range(2 * KC):
                        m = a % KC
                        for k in range(KC):
                            last = nc.tensor.matmul(pqk[:, a, :], w["qk"[a // KC]][:, k, m * P:(m + 1) * P], xnT[:, k, :],
                                                    start=(k == 0), stop=(k == KC - 1))
                    last.then_inc(qk_ok, 1)
                    pe.wait_ge(v_out, n)
                    for i in range(CT):
                        for k in range(KC):
                            last = nc.tensor.matmul(pv[:, i // 2, (i % 2) * E:(i % 2 + 1) * E], xnT[:, k, i * P:(i + 1) * P],
                                                    w["v"][:, k, :], start=(k == 0), stop=(k == KC - 1))
                    last.then_inc(v_ok, 1)
                    pe.wait_ge(qkT_ok, n + 1)
                    for a in range(2):
                        for i in range(CT):
                            for k in range(KC):
                                o = (i % 2) * E + k * P
                                last = nc.tensor.transpose(pqk[:, 2 * a + i // 2, o:o + P],
                                                           qkT[:, a * KC + k, i * P:(i + 1) * P], c["ident"][:])
                    last.then_inc(rows_ok, 1)
                    for i in range(CT):
                        for k in range(KC):
                            o = (i % 2) * RG + k * NM * 8
                            last = nc.tensor.matmul(pT[:, i // 2, o:o + NM * 8], qkT[:, k, i * P:(i + 1) * P],
                                                    rk[:].rearrange("p m h -> p (m h)"), start=True, stop=True)
                        o = (i % 2) * RG + RELW
                        for k in range(KC):
                            last = nc.tensor.matmul(pT[:, i // 2, o:o + X], xnT[:, k, i * P:(i + 1) * P], gw[:, k, :],
                                                    start=(k == 0), stop=(k == KC - 1))
                    last.then_inc(rel_ok, 1)


def band_scores(nc, c, dr, band, bmax):
    with ExitStack() as ctx:
        def sb(name, shape, dt=F32):
            return ctx.enter_context(nc.sbuf_tensor("b_" + name, shape, dt))

        def sem(name):
            return ctx.enter_context(nc.semaphore("b_" + name))
        BUF = 2
        q = sb("q", [P, BUF, E])
        ks = sb("ks", [P, BUF, NM * E])
        prod = sb("prod", [P, BUF, NM, H, D])
        dot = sb("dot", [P, BUF, NM * H])
        q_in = [sem(f"q_in{i}") for i in range(BUF)]
        mul_ok, sum_ok, chain = sem("mul_ok"), sem("sum_ok"), sem("chain")
        q_v = dr["q"].rearrange("(n p) e -> n p e", p=P)

        def windows(n):
            v = dr["k"][0:T, :].rearrange("(n p) e -> n p e", p=P)[n]
            return bass.AP(v.tensor, v.offset, [[E, P], [1, NM * E]])

        with nc.Block() as block:
            @block.sync
            def _(sp):
                def load(t, u):
                    sp.dma_start(q[:, u, :], q_v[t]).then_inc(q_in[u], 16)
                    sp.dma_start(ks[:, u, :], windows(t)).then_inc(q_in[u], 16)
                for u in range(BUF):
                    load(u, u)
                with sp.Fori(0, NT // BUF - 1) as r:
                    for u in range(BUF):
                        sp.wait_ge(mul_ok, BUF * r + u + 1)
                        load(BUF * r + BUF + u, u)

            @block.gpsimd
            def _(pool):
                with pool.Fori(0, NT // BUF) as r:
                    for u in range(BUF):
                        pool.wait_ge(q_in[u], 32 * r + 32)
                        pool.wait_ge(sum_ok, BUF * r)
                        nc.gpsimd.tensor_tensor(
                            prod[:, u].rearrange("p m h d -> p m (h d)"), ks[:, u, :].rearrange("p (m e) -> p m e", m=NM),
                            q[:, u:u + 1, :].broadcast_to([P, NM, E]), ALU.mult).then_inc(mul_ok, 1)

            @block.vector
            def _(dve):
                with dve.Fori(0, NT // BUF) as r:
                    for u in range(BUF):
                        t = r * BUF + u
                        dve.wait_ge(mul_ok, t + 1)
                        nc.vector.tensor_reduce(dot[:, u, :], prod[:, u].rearrange("p m h d -> p (m h) d"),
                                                AX.X, ALU.add).then_inc(sum_ok, 1)
                        dve.wait_ge(sum_ok, t + 1)
                        b = band[:, t, :, :].rearrange("p m h -> p (m h)")
                        nc.vector.tensor_tensor(b, b, dot[:, u, :], ALU.add).then_inc(chain, 1)
                        dve.wait_ge(chain, t + 1)
                        nc.vector.tensor_reduce(bmax[:, t, :], band[:, t, :, :].rearrange("p m h -> p h m"), AX.X, ALU.max)


def attention(nc, c, dr, band, bmax, neg, oa):
    XS = TB * HG
    PAIRS = TB // 2
    QUOTA = 24
    with ExitStack() as ctx:
        def sb(name, shape, dt=F32):
            return ctx.enter_context(nc.sbuf_tensor("t_" + name, shape, dt))

        def ps(name, shape, dt=F32):
            return ctx.enter_context(nc.psum_tensor("t_" + name, shape, dt))

        def sem(name):
            return ctx.enter_context(nc.semaphore("t_" + name))

        def sems(name):
            return [sem(f"{name}{i}") for i in range(2)]
        q1 = sb("q1", [P, 2, HG, L], BF16)
        k1 = sb("k1", [P, 2, HG, L], BF16)
        q2 = sb("q2", [P, 2, HG, L], BF16)
        k2 = sb("k2", [P, 2, HG, L], BF16)
        vx = sb("vx", [P, 2, TB, HG * VW])
        pr = sb("pr", [P, 2, HG, 2, CH])
        mx = sb("mx", [P, HG, TB, 2])
        ma = sb("ma", [P, HG, TB])
        mb = sb("mb", [P, HG, TB])
        mparts = sb("mparts", [P, 4, HG, TB], BF16)
        mt = sb("mt", [2 * HG * TB, P], BF16)
        ot = sb("ot", [P, CH])
        s1 = ps("s1", [P, 2, CH])
        s2 = ps("s2", [P, 2, 2, CH])
        po = ps("po", [P, CH])
        misc = ps("misc", [P, CH])
        in1, in2, vin, ones_ok = sems("in1_"), sems("in2_"), sems("vin"), sem("ones_ok")
        zeros_ok = sem("zeros_ok")
        s1_ok, mx_ok, chain, mparts_ok, mt_ps_ok, mt_ok, m_in = (
            sem("s1_ok"), sem("mx_ok"), sem("chain"), sem("mparts_ok"), sem("mt_ps_ok"), sem("mt_ok"), sem("m_in"))
        s2_ok, exp_ok, pv_ok, ot_ok, otT_ok, oa_ok = (
            sem("s2_ok"), sem("exp_ok"), sem("pv_ok"), sem("ot_ok"), sem("otT_ok"), sem("oa_ok"))
        sq = dr["sq"].rearrange("b g h r c -> (b g) r h c")
        sk = dr["sk"].rearrange("b g h r c -> (b g) r h c")
        vd = dr["vx"].rearrange("(b i p) (g v) -> b g p i v", p=P, i=TB, v=HG * VW)

        def far_pieces(tile, half):
            a, b = max(tile * P - W, half * CH), min(tile * P + P + W, half * CH + CH)
            return [(a - half * CH, b - a, a - (tile * P - W))] if a < b else []

        with nc.Block() as block:
            @block.sync
            def _(sp):
                def load1(g, u):
                    for dst, src in ((q1, sq), (k1, sk)):
                        sp.dma_start(dst[0:ROWS, u], src[g]).then_inc(in1[u], 16)

                def load2(g, b, gg, u):
                    for dst, src in ((q2, sq), (k2, sk)):
                        sp.dma_start(dst[0:ROWS, u], src[g]).then_inc(in2[u], 16)
                    sp.dma_start(vx[:, u], vd[b, gg]).then_inc(vin[u], 16)

                def maximum(g, u):
                    sp.wait_ge(mt_ok, g + 1)
                    for j in range(MROWS):
                        sp.dma_start(q2[ROWS + j:ROWS + j + 1, u].rearrange("o h (i t) -> o (h i) t", t=P),
                                     mt[j * HG * TB:(j + 1) * HG * TB, :]).then_inc(m_in, 16)
                load1(0, 0)
                load1(1, 1)
                load2(0, 0, 0, 0)
                maximum(0, 0)
                load2(1, 0, 1, 1)

                def step(g, b2, g2, u, more1=True, more2=True):
                    if more1:
                        sp.wait_ge(s1_ok, 2 * TB * HG * (g + 2))
                        load1(g + 3, 1 - u)
                    maximum(g + 1, 1 - u)
                    if more2:
                        sp.wait_ge(pv_ok, TB * (g + 1))
                        load2(g + 2, b2, g2, u)
                sp.wait_ge(s1_ok, 2 * TB * HG)
                load1(2, 0)
                step(0, 0, 2, 0)
                step(1, 0, 3, 1)
                with sp.Fori(0, NB - 2) as r:
                    for v in range(4):
                        step(4 * r + 2 + v, r + 1, v, v % 2)
                step(10, 3, 0, 0)
                step(11, 3, 1, 1)
                step(12, 3, 2, 0)
                step(13, 3, 3, 1, more1=False)
                step(14, 0, 0, 0, more1=False, more2=False)

            @block.gpsimd
            def _(pool):
                for u in range(2):
                    nc.gpsimd.memset(k2[ROWS:ROWS + MROWS, u], 1.0).then_inc(ones_ok, 1)

            @block.tensor
            def _(pe):
                def pass1(g, u, n):
                    h, i = n // TB, n % TB
                    for half in range(2):
                        count = 2 * n + half
                        after(pe, mx_ok, g * (2 * TB * HG) + count - 1)
                        far = far_pieces(i, half)
                        last = nc.tensor.matmul(s1[:, half, :], q1[0:ROWS, u, h, i * P:(i + 1) * P],
                                                k1[0:ROWS, u, h, half * CH:(half + 1) * CH], start=True, stop=not far)
                        for a, m, j in far:
                            last = nc.tensor.matmul(s1[:, half, a:a + m], c["ident16"][:], c["far"][:, j:j + m],
                                                    start=False, stop=True)
                        last.then_inc(s1_ok, 1)

                def pass2(g, u, n):
                    half, pair, h = n // (PAIRS * HG), n // HG % PAIRS, n % HG
                    after(pe, exp_ok, g * XS + n - 1)
                    for k in range(2):
                        i = 2 * pair + k
                        far = far_pieces(i, half)
                        last = nc.tensor.matmul(s2[:, n % 2, k, :], k2[0:ROWS + MROWS, u, h, i * P:(i + 1) * P],
                                                q2[0:ROWS + MROWS, u, h, half * CH:(half + 1) * CH],
                                                start=True, stop=not far)
                        for a, m, j in far:
                            last = nc.tensor.matmul(s2[:, n % 2, k, a:a + m], c["ident16"][:], c["far"][:, j:j + m],
                                                    start=False, stop=True)
                    last.then_inc(s2_ok, 1)

                def values(g, u, n):
                    half, pair = n // PAIRS, n % PAIRS
                    pe.wait_ge(exp_ok, g * XS + HG * (n + 1))
                    if pair == 0:
                        after(pe, ot_ok, 2 * g + half)
                    for k in range(2):
                        i = 2 * pair + k
                        for h in range(HG):
                            last = nc.tensor.matmul(po[h * VW:(h + 1) * VW, :], vx[:, u, i, h * VW:(h + 1) * VW],
                                                    pr[:, n % 2, h, k, :], start=(i == 0), stop=(i == TB - 1),
                                                    tile_position=(0, h * VW))
                    last.then_inc(pv_ok, 1)

                def output_rows(g, half, made):
                    pe.wait_ge(ot_ok, 2 * g + half + 1)
                    after(pe, mt_ok, made)
                    after(pe, oa_ok, 2 * g + half)
                    for i in range(CT):
                        last = nc.tensor.transpose(misc[:, i * P:(i + 1) * P], ot[:, i * P:(i + 1) * P], c["ident"][:])
                    last.then_inc(otT_ok, 1)

                def maximum_rows(g, outs):
                    pe.wait_ge(mparts_ok, g + 1)
                    after(pe, oa_ok, outs)
                    nc.tensor.transpose(misc[:, 0:P // 2].bitcast(BF16), mparts[:].rearrange("p j h i -> p (j h i)"),
                                        c["ident16"][:]).then_inc(mt_ps_ok, 1)

                def group(g, u, k, more=True, carried=True):
                    pe.wait_ge(in2[u], 32 * k)
                    pe.wait_ge(vin[u], 16 * k)
                    pe.wait_ge(m_in, 16 * MROWS * (g + 1))
                    if more:
                        pe.wait_ge(in1[1 - u], 32 * (k + u))
                    done = 0
                    for n in range(XS):
                        pass2(g, u, n)
                        while more and done < min(TB * HG, -(-TB * HG * (n + 1) // QUOTA)):
                            pass1(g + 1, 1 - u, done)
                            done += 1
                        if n % HG == 1:
                            if n > HG:
                                values(g, u, n // HG - 1)
                            elif carried:
                                values(g - 1, 1 - u, 2 * PAIRS - 1)
                        if n == 7 and carried:
                            output_rows(g - 1, 1, g + 1)
                        if n == 23:
                            output_rows(g, 0, g + 1)
                        if n == XS - 2 and more:
                            maximum_rows(g + 1, 2 * g + 1)

                pe.wait_ge(ones_ok, 2)
                pe.wait_ge(in1[0], 32)
                for n in range(TB * HG):
                    pass1(0, 0, n)
                maximum_rows(0, 0)
                group(0, 0, 1, carried=False)
                with pe.Fori(0, NG // 2 - 1) as r:
                    group(2 * r + 1, 1, r + 1)
                    group(2 * r + 2, 0, r + 2)
                group(NG - 1, 1, NG // 2, more=False)
                values(NG - 1, 1, 2 * PAIRS - 1)
                output_rows(NG - 1, 1, NG)

            @block.vector
            def _(dve):
                CHAIN = 4

                def maxima(g):
                    def link(ins, k):
                        ins.then_inc(chain, 1)
                        dve.wait_ge(chain, g * CHAIN + k)
                    for n in range(TB * HG):
                        for half in range(2):
                            dve.wait_ge(s1_ok, g * (2 * TB * HG) + 2 * n + half + 1)
                            nc.vector.reduce_max(mx[:, n // TB, n % TB, half:half + 1], s1[:, half, :],
                                                 AX.X).then_inc(mx_ok, 1)
                    dve.wait_ge(mx_ok, (g + 1) * (2 * TB * HG))
                    link(nc.vector.tensor_tensor(ma[:], mx[:, :, :, 0], mx[:, :, :, 1], ALU.max), 1)
                    link(nc.vector.tensor_tensor(mb[:], ma[:], bmax[:, g], ALU.max), 2)
                    link(nc.vector.tensor_scalar(mparts[:, 0], mb[:], -1.0, None, ALU.mult), 3)
                    link(nc.vector.scalar_tensor_tensor(out=mparts[:, 1], in0=mb[:], scalar=-1.0, in1=mparts[:, 0],
                                                        op0=ALU.mult, op1=ALU.subtract), 4)
                    nc.vector.tensor_tensor(neg[:, g], mparts[:, 0], mparts[:, 1], ALU.add).then_inc(mparts_ok, 1)
                    dve.wait_ge(mt_ps_ok, g + 1)
                    after(dve, m_in, 16 * MROWS * g)
                    nc.vector.tensor_copy(mt[:], misc[0:2 * HG * TB, 0:P // 2].bitcast(BF16)).then_inc(mt_ok, 1)
                nc.vector.memset(mparts[:], 0.0).then_inc(zeros_ok, 1)
                dve.wait_ge(zeros_ok, 1)
                maxima(0)
                maxima(1)
                with dve.Fori(0, NG // 2 - 1) as r:
                    maxima(2 * r + 2)
                    maxima(2 * r + 3)

            @block.scalar
            def _(act):
                def copy_sums(g, half):
                    act.wait_ge(pv_ok, TB * g + PAIRS * (half + 1))
                    after(act, otT_ok, 2 * g + half)
                    nc.scalar.copy(ot[:], po[:]).then_inc(ot_ok, 1)

                def keep_rows(g, half):
                    act.wait_ge(otT_ok, 2 * g + half + 1)
                    nc.scalar.copy(oa[:, g, half * CT:(half + 1) * CT],
                                   misc[:].rearrange("p (i h v) -> p i h v", h=HG, v=VW)[:, :, :, 0:D + 1]).then_inc(oa_ok, 1)

                def exps(g, carried=True):
                    for n in range(XS):
                        k = n // HG
                        act.wait_ge(s2_ok, g * XS + n + 1)
                        if n % HG == 0:
                            after(act, pv_ok, TB * g + k - 1)
                        nc.scalar.activation(pr[:, k % 2, n % HG], s2[:, n % 2], ACT.Exp).then_inc(exp_ok, 1)
                        if n == 1 and carried:
                            copy_sums(g - 1, 1)
                        if n == 8 and carried:
                            keep_rows(g - 1, 1)
                        if n == 17:
                            copy_sums(g, 0)
                        if n == 24:
                            keep_rows(g, 0)
                exps(0, carried=False)
                with act.Fori(0, NG // 2 - 1) as r:
                    exps(2 * r + 1)
                    exps(2 * r + 2)
                exps(NG - 1)
                copy_sums(NG - 1, 1)
                keep_rows(NG - 1, 1)


def regroup(nc, pairs):
    with ExitStack() as ctx:
        ok = ctx.enter_context(nc.semaphore("regrouped"))
        with nc.Block() as block:
            @block.vector
            def _(dve):
                for dst, src in pairs:
                    nc.vector.tensor_copy(dst, src).then_inc(ok, 1)


def finish(nc, c, dr, x, Wo, bo, rel_v, band, neg, oa, res):
    with ExitStack() as ctx:
        def sb(name, shape, dt=F32):
            return ctx.enter_context(nc.sbuf_tensor("f_" + name, shape, dt))

        def ps(name, shape, dt=F32):
            return ctx.enter_context(nc.psum_tensor("f_" + name, shape, dt))

        def sem(name):
            return ctx.enter_context(nc.semaphore("f_" + name))
        M0 = P // H
        R1 = (NM - M0) * H
        wo = sb("wo", [P, KC, E])
        bob = sb("bob", [P, E])
        rv = sb("rv", [P, 2, D])
        pick = sb("pick", [P, H, M0])
        hsel = sb("hsel", [P, H])
        rvm = sb("rvm", [P, 2, H, D])
        vs = sb("vs", [P, 2, NM, E])
        xt = sb("xt", [P, 2, E])
        bs = sb("bs", [P, 2, NM * H])
        e = sb("e", [P, 2, NM * H])
        prod = sb("prod", [P, 2, NM, E])
        eT0 = sb("eT0", [P, 2, P])
        eT1 = sb("eT1", [R1, 2, P])
        es = sb("es", [P, H])
        z = sb("z", [P, H])
        rz = sb("rz", [P, H])
        o1 = sb("o1", [P, E])
        o2 = sb("o2", [P, E])
        o3 = sb("o3", [P, E])
        on = sb("on", [P, 2, E])
        onT = sb("onT", [P, 2, KC, P])
        y = sb("y", [P, E])
        pe_t = ps("pe_t", [P, CH])
        prv = ps("prv", [P, CH])
        pon = ps("pon", [P, CH])
        py = ps("py", [P, CH])
        w_in, set_ok, v_in = sem("w_in"), sem("set_ok"), [sem(f"v_in{i}") for i in range(2)]
        bs_ok, e_ok, prod_ok, et_ps_ok, et_ok, rv_ok = (
            sem("bs_ok"), sem("e_ok"), sem("prod_ok"), sem("et_ps_ok"), sem("et_ok"), sem("rv_ok"))
        chain, on_ok, on_ps_ok, ont_ok, y_ok, res_ok = (
            sem("chain"), sem("on_ok"), sem("on_ps_ok"), sem("ont_ok"), sem("y_ok"), sem("res_ok"))
        x_v = x.rearrange("(n p) e -> n p e", p=P)

        def windows(n):
            v = dr["v"][0:T, :].rearrange("(n p) e -> n p e", p=P)[n]
            return bass.AP(v.tensor, v.offset, [[E, P], [1, NM * E]])

        with nc.Block() as block:
            @block.sync
            def _(sp):
                sp.dma_start(wo[:], Wo.rearrange("(k p) e -> p k e", p=P)).then_inc(w_in, 16)
                sp.dma_start(bob[:], bo.rearrange("(o e) -> o e", o=1).broadcast_to([P, E])).then_inc(w_in, 16)
                for m in range(NM):
                    r = m % M0 * H
                    sp.dma_start(rv[r:r + H, m // M0, :], rel_v[0, m:m + 1, :].broadcast_to([H, D])).then_inc(w_in, 16)

                def load(t, u):
                    sp.dma_start(vs[:, u].rearrange("p m e -> p (m e)"), windows(t)).then_inc(v_in[u], 16)
                    sp.dma_start(xt[:, u, :], x_v[t]).then_inc(v_in[u], 16)
                load(0, 0)
                load(1, 1)
                with sp.Fori(0, NT // 2 - 1) as r:
                    for u in range(2):
                        sp.wait_ge(res_ok, 2 * r + u + 1)
                        load(2 * r + 2 + u, u)

            @block.gpsimd
            def _(pool):
                nc.gpsimd.memset(pick[:], 0.0).then_inc(set_ok, 1)
                pool.wait_ge(set_ok, 1)
                nc.gpsimd.affine_select(out=pick[:], in_=pick[:], compare_op=ALU.not_equal, fill=1.0, base=0,
                                        pattern=[[-1, H], [-H, M0]], channel_multiplier=1).then_inc(set_ok, 1)
                with pool.Fori(0, NT // 2) as r:
                    for u in range(2):
                        t = 2 * r + u
                        pool.wait_ge(e_ok, t + 1)
                        pool.wait_ge(v_in[u], 32 * r + 32)
                        pool.wait_ge(on_ok, 2 * r)
                        nc.gpsimd.tensor_tensor(
                            prod[:, u].rearrange("p m (h d) -> p (m h) d", d=D),
                            vs[:, u].rearrange("p m (h d) -> p (m h) d", d=D),
                            e[:, u, :].rearrange("p (q o) -> p q o", o=1).broadcast_to([P, NM * H, D]),
                            ALU.mult).then_inc(prod_ok, 1)

            @block.vector
            def _(dve):
                dve.wait_ge(set_ok, 2)
                nc.vector.tensor_reduce(hsel[:], pick[:], AX.X, ALU.add).then_inc(chain, 1)
                dve.wait_ge(chain, 1)
                dve.wait_ge(w_in, 16 * (2 + NM))
                for k, rows in ((0, P), (1, R1)):
                    last = nc.vector.tensor_tensor(
                        rvm[0:rows, k], rv[0:rows, k, :].rearrange("p (o d) -> p o d", o=1).broadcast_to([rows, H, D]),
                        hsel[0:rows, :].rearrange("p (h o) -> p h o", o=1).broadcast_to([rows, H, D]), ALU.mult)
                last.then_inc(chain, 1)
                BASE, STEPS = 2, 6

                def shifted(t, u):
                    nc.vector.tensor_tensor(bs[:, u, :].rearrange("p (m h) -> p m h", h=H), band[:, t],
                                            neg[:, t].rearrange("p (o h) -> p o h", o=1).broadcast_to([P, NM, H]), ALU.add).then_inc(bs_ok, 1)

                def rows(t, u, r):
                    def link(ins, k):
                        ins.then_inc(chain, 1)
                        dve.wait_ge(chain, t * STEPS + BASE + k)
                    dve.wait_ge(prod_ok, t + 1)
                    nc.vector.tensor_reduce(es[:], e[:, u, :].rearrange("p (m h) -> p h m", h=H), AX.X, ALU.add).then_inc(chain, 1)
                    nc.vector.tensor_reduce(o1[:], prod[:, u].rearrange("p m e -> p e m"), AX.X, ALU.add).then_inc(chain, 1)
                    dve.wait_ge(chain, t * STEPS + BASE + 2)
                    nc.vector.tensor_tensor(z[:], es[:], oa[:, t, :, D], ALU.add).then_inc(chain, 1)
                    nc.vector.tensor_tensor(o2[:].rearrange("p (h d) -> p h d", d=D), o1[:].rearrange("p (h d) -> p h d", d=D),
                                            oa[:, t, :, 0:D], ALU.add).then_inc(chain, 1)
                    dve.wait_ge(chain, t * STEPS + BASE + 4)
                    nc.vector.reciprocal(rz[:], z[:]).then_inc(chain, 1)
                    dve.wait_ge(rv_ok, t + 1)
                    nc.vector.tensor_tensor(o3[:], o2[:], prv[:, 0:E], ALU.add).then_inc(chain, 1)
                    dve.wait_ge(chain, t * STEPS + BASE + 6)
                    nc.vector.tensor_tensor(on[:, u, :].rearrange("p (h d) -> p h d", d=D),
                                            o3[:].rearrange("p (h d) -> p h d", d=D),
                                            rz[:].rearrange("p (h o) -> p h o", o=1).broadcast_to([P, H, D]),
                                            ALU.mult).then_inc(on_ok, 1)

                def result(t, u):
                    dve.wait_ge(y_ok, t + 1)
                    nc.vector.tensor_tensor(y[:], py[:, 0:E], xt[:, u, :], ALU.add).then_inc(yc, 1)
                    dve.wait_ge(yc, t + 1)
                    nc.vector.tensor_tensor(res[:, t, :], y[:], bob[:], ALU.add).then_inc(res_ok, 1)
                yc = sem("yc")
                shifted(0, 0)
                shifted(1, 1)
                rows(0, 0, 0)
                with dve.Fori(0, NT // 2 - 1) as r:
                    shifted(2 * r + 2, 0)
                    rows(2 * r + 1, 1, r)
                    result(2 * r, 0)
                    shifted(2 * r + 3, 1)
                    rows(2 * r + 2, 0, r)
                    result(2 * r + 1, 1)
                rows(NT - 1, 1, 0)
                result(NT - 2, 0)
                result(NT - 1, 1)

            @block.scalar
            def _(act):
                def exps(t, u):
                    act.wait_ge(bs_ok, t + 1)
                    nc.scalar.activation(e[:, u, :], bs[:, u, :], ACT.Exp).then_inc(e_ok, 1)

                def columns(t, u):
                    act.wait_ge(et_ps_ok, t + 1)
                    nc.scalar.copy(eT0[:, u, :], pe_t[:, 0:P])
                    nc.scalar.copy(eT1[:, u, :], pe_t[0:R1, P:2 * P]).then_inc(et_ok, 1)

                def normed(t, u):
                    act.wait_ge(on_ps_ok, t + 1)
                    nc.scalar.copy(onT[:, u], pon[:, 0:E].rearrange("p (k t) -> p k t", k=KC)).then_inc(ont_ok, 1)
                exps(0, 0)
                columns(0, 0)
                exps(1, 1)
                with act.Fori(0, NT // 2 - 1) as r:
                    columns(2 * r + 1, 1)
                    normed(2 * r, 0)
                    exps(2 * r + 2, 0)
                    columns(2 * r + 2, 0)
                    normed(2 * r + 1, 1)
                    exps(2 * r + 3, 1)
                columns(NT - 1, 1)
                normed(NT - 2, 0)
                normed(NT - 1, 1)

            @block.tensor
            def _(pe):
                def columns(t, u):
                    pe.wait_ge(e_ok, t + 1)
                    after(pe, et_ok, t)
                    nc.tensor.transpose(pe_t[:, 0:P], e[:, u, 0:P], c["ident"][:])
                    nc.tensor.transpose(pe_t[0:R1, P:2 * P], e[:, u, P:P + R1], c["ident"][:]).then_inc(et_ps_ok, 1)

                def relative(t, u):
                    pe.wait_ge(et_ok, t + 1)
                    after(pe, on_ok, t)
                    nc.tensor.matmul(prv[:, 0:E], eT0[:, u, :], rvm[:, 0].rearrange("p h d -> p (h d)"), start=True, stop=False)
                    nc.tensor.matmul(prv[:, 0:E], eT1[:, u, :], rvm[0:R1, 1].rearrange("p h d -> p (h d)"),
                                     start=False, stop=True).then_inc(rv_ok, 1)

                def project(t, u):
                    pe.wait_ge(on_ok, t + 1)
                    after(pe, ont_ok, t)
                    for k in range(KC):
                        last = nc.tensor.transpose(pon[:, k * P:(k + 1) * P], on[:, u, k * P:(k + 1) * P], c["ident"][:])
                    last.then_inc(on_ps_ok, 1)

                def output(t, u):
                    pe.wait_ge(ont_ok, t + 1)
                    after(pe, res_ok, t)
                    for k in range(KC):
                        last = nc.tensor.matmul(py[:, 0:E], onT[:, u, k, :], wo[:, k, :], start=(k == 0), stop=(k == KC - 1))
                    last.then_inc(y_ok, 1)
                pe.wait_ge(w_in, 16 * (2 + NM))
                pe.wait_ge(chain, 2)
                columns(0, 0)
                relative(0, 0)
                with pe.Fori(0, NT // 2 - 1) as r:
                    columns(2 * r + 1, 1)
                    project(2 * r, 0)
                    relative(2 * r + 1, 1)
                    output(2 * r, 0)
                    columns(2 * r + 2, 0)
                    project(2 * r + 1, 1)
                    relative(2 * r + 2, 0)
                    output(2 * r + 1, 1)
                columns(NT - 1, 1)
                project(NT - 2, 0)
                relative(NT - 1, 1)
                output(NT - 2, 0)
                project(NT - 1, 1)
                output(NT - 1, 1)


def store(nc, res, out):
    with ExitStack() as ctx:
        stored = ctx.enter_context(nc.semaphore("stored"))
        with nc.Block() as block:
            @block.sync
            def _(sp):
                sp.dma_start(out.rearrange("(n p) e -> p n e", p=P), res[:]).then_inc(stored, 16)
                sp.wait_ge(stored, 16)


def route(nc, c, dr, logits, dst, gates, table):
    I32 = mybir.dt.int32
    with ExitStack() as ctx:
        def sb(name, shape, dt=F32):
            return ctx.enter_context(nc.sbuf_tensor("r_" + name, shape, dt))

        def sem(name):
            return ctx.enter_context(nc.semaphore("r_" + name))
        KMAX = T // TS
        iota_e = sb("iota_e", [P, X])
        iota_k = sb("iota_k", [P, KMAX])
        iota_s = sb("iota_s", [1, NS])
        iota_i = sb("iota_i", [P, NS], I32)
        tri = sb("tri", [P, P], BF16)
        ones = sb("ones", [P, P], BF16)
        zero = sb("zero", [P, 6 * E])
        m = sb("m", [P, 2, NT])
        eq = sb("eq", [P, NT, X])
        cand = sb("cand", [P, NT, X])
        first = sb("first", [P, 2, NT])
        hot = sb("hot", [P, 2, NT, X])
        rest = sb("rest", [P, NT, X])
        gap = sb("gap", [P, NT])
        eg = sb("eg", [P, NT])
        sg = sb("sg", [P, NT])
        chosen = sb("chosen", [P, NT, X], BF16)
        total = sb("total", [P, NT, X])
        scan = sb("scan", [P, 2, NT, X])
        over = sb("over", [P, X, KMAX])
        slots = sb("slots", [P, X])
        ends = sb("ends", [P, 2, X])
        start = sb("start", [P, X])
        place = sb("place", [P, NT, X])
        pick = sb("pick", [P, 2, NT, X])
        where = sb("where", [P, 2, NT])
        past = sb("past", [1, NS, X])
        tab = sb("tab", [1, NS])
        rows = sb("rows", [P, 2, E])
        pc = ctx.enter_context(nc.psum_tensor("r_pc", [P, NT * X], F32))
        pt = ctx.enter_context(nc.psum_tensor("r_pt", [P, NT * X], F32))
        made, chain, gap_ok, eg_ok, chosen_ok, count_ok, dst_ok = (
            sem("made"), sem("chain"), sem("gap_ok"), sem("eg_ok"), sem("chosen_ok"), sem("count_ok"), sem("dst_ok"))
        zero_out, sent = sem("zero_out"), [sem(f"sent{i}") for i in range(2)]
        row_in = [sem(f"row_in{i}") for i in range(2)]
        xn_v = dr["xn"].rearrange("(n p) e -> n p e", p=P)
        N_ZERO = NS * TS // P // 6
        CONST = 7

        def over_x(a):
            return a.rearrange("p (n o) -> p n o", o=1).broadcast_to([P, NT, X])

        def over_n(a):
            return a.rearrange("p (o e) -> p o e", o=1).broadcast_to([P, NT, X])

        with nc.Block() as block:
            @block.sync
            def _(sp):
                sp.wait_ge(made, CONST)
                v = dr["xs"].rearrange("(z p r) e -> z p (r e)", p=P, r=6)
                for i in range(N_ZERO):
                    sp.dma_start(v[i], zero[:]).then_inc(zero_out, 16)
                for u in range(2):
                    sp.dma_start(rows[:, u, :], xn_v[u]).then_inc(row_in[u], 16)
                with sp.Fori(0, NT // 2 - 1) as r:
                    for u in range(2):
                        sp.wait_ge(sent[u], 32 * r + 32)
                        sp.dma_start(rows[:, u, :], xn_v[2 * r + 2 + u]).then_inc(row_in[u], 16)

            @block.gpsimd
            def _(pool):
                count = [0]

                def then(ins):
                    count[0] += 1
                    ins.then_inc(made, 1)
                    pool.wait_ge(made, count[0])
                then(nc.gpsimd.iota(iota_i[:], [[1, NS]], base=0, channel_multiplier=0))
                nc.gpsimd.memset(tri[:], 1.0).then_inc(made, 1)
                nc.gpsimd.memset(ones[:], 1.0).then_inc(made, 1)
                count[0] += 2
                then(nc.gpsimd.memset(zero[:], 0.0))
                then(nc.gpsimd.affine_select(out=tri[:], in_=tri[:], compare_op=ALU.is_gt, fill=0.0, base=0,
                                             pattern=[[1, P]], channel_multiplier=-1))
                then(nc.gpsimd.tensor_copy(iota_s[:], iota_i[0:1, :]))
                then(nc.gpsimd.tensor_copy(iota_e[:], iota_i[:, 0:X]))
                pool.wait_ge(dst_ok, 1)
                pool.wait_ge(zero_out, 16 * N_ZERO)
                for t in range(NT):
                    u = t % 2
                    pool.wait_ge(row_in[u], 16 * (t // 2 + 1))
                    for k in range(2):
                        nc.gpsimd.indirect_dma_start(
                            out=dr["xs"], out_offset=bass.IndirectOffsetOnAxis(ap=dst[:, t, k:k + 1], axis=0),
                            in_=rows[:, u, :], in_offset=None).then_inc(sent[u], 16)
                for u in range(2):
                    pool.wait_ge(sent[u], 16 * NT)

            @block.vector
            def _(dve):
                count = [0]

                def then(ins):
                    count[0] += 1
                    ins.then_inc(chain, 1)
                    dve.wait_ge(chain, count[0])
                dve.wait_ge(made, CONST)
                then(nc.vector.tensor_scalar(iota_k[:], iota_i[:, 0:KMAX], float(TS), None, ALU.mult))
                for k, src in ((0, logits), (1, rest)):
                    then(nc.vector.tensor_reduce(m[:, k, :], src[:], AX.X, ALU.max))
                    then(nc.vector.tensor_tensor(eq[:], src[:], over_x(m[:, k, :]), ALU.is_equal))
                    then(nc.vector.scalar_tensor_tensor(out=cand[:], in0=eq[:], scalar=-float(X), in1=over_n(iota_e[:]),
                                                        op0=ALU.mult, op1=ALU.add))
                    then(nc.vector.tensor_reduce(first[:, k, :], cand[:], AX.X, ALU.min))
                    then(nc.vector.tensor_scalar_add(first[:, k, :], first[:, k, :], float(X)))
                    then(nc.vector.tensor_tensor(hot[:, k], over_n(iota_e[:]), over_x(first[:, k, :]), ALU.is_equal))
                    if k == 0:
                        then(nc.vector.scalar_tensor_tensor(out=rest[:], in0=hot[:, 0], scalar=FAR, in1=logits[:],
                                                            op0=ALU.mult, op1=ALU.add))
                nc.vector.tensor_tensor(chosen[:], hot[:, 0], hot[:, 1], ALU.add).then_inc(chosen_ok, 1)
                nc.vector.tensor_tensor(gap[:], m[:, 1, :], m[:, 0, :], ALU.subtract).then_inc(gap_ok, 1)
                dve.wait_ge(eg_ok, 1)
                then(nc.vector.tensor_scalar_add(sg[:], eg[:], 1.0))
                then(nc.vector.reciprocal(gates[:, :, 0], sg[:]))
                then(nc.vector.tensor_tensor(gates[:, :, 1], eg[:], gates[:, :, 0], ALU.mult))
                dve.wait_ge(count_ok, 1)
                nc.vector.tensor_copy(total[:], pt[:].rearrange("p (n e) -> p n e", e=X))
                then(nc.vector.tensor_copy(scan[:, 0], pt[:].rearrange("p (n e) -> p n e", e=X)))
                a, step = 0, 1
                while step < NT:
                    then(nc.vector.tensor_copy(scan[:, 1 - a, 0:step, :], scan[:, a, 0:step, :]))
                    then(nc.vector.tensor_tensor(scan[:, 1 - a, step:, :], scan[:, a, step:, :], scan[:, a, 0:NT - step, :], ALU.add))
                    a, step = 1 - a, 2 * step
                then(nc.vector.tensor_tensor(over[:], scan[:, a, NT - 1, :].rearrange("p (e o) -> p e o", o=1).broadcast_to([P, X, KMAX]),
                                             iota_k[:].rearrange("p (o k) -> p o k", o=1).broadcast_to([P, X, KMAX]), ALU.is_gt))
                then(nc.vector.tensor_reduce(slots[:], over[:], AX.X, ALU.add))
                then(nc.vector.tensor_copy(ends[:, 0, :], slots[:]))
                b, step = 0, 1
                while step < X:
                    then(nc.vector.tensor_copy(ends[:, 1 - b, 0:step], ends[:, b, 0:step]))
                    then(nc.vector.tensor_tensor(ends[:, 1 - b, step:], ends[:, b, step:], ends[:, b, 0:X - step], ALU.add))
                    b, step = 1 - b, 2 * step
                then(nc.vector.tensor_tensor(start[:], ends[:, b, :], slots[:], ALU.subtract))
                then(nc.vector.tensor_scalar(start[:], start[:], float(TS), None, ALU.mult))
                then(nc.vector.tensor_tensor(place[:], scan[:, a], total[:], ALU.subtract))
                then(nc.vector.tensor_tensor(place[:], place[:], pc[:].rearrange("p (n e) -> p n e", e=X), ALU.add))
                then(nc.vector.tensor_tensor(place[:], place[:], over_n(start[:]), ALU.add))
                for k in range(2):
                    then(nc.vector.tensor_tensor(pick[:, k], hot[:, k], place[:], ALU.mult))
                    then(nc.vector.tensor_reduce(where[:, k, :], pick[:, k], AX.X, ALU.add))
                then(nc.vector.tensor_tensor(past[:], iota_s[:].rearrange("p (s o) -> p s o", o=1).broadcast_to([1, NS, X]),
                                             ends[0:1, b, :].rearrange("p (o e) -> p o e", o=1).broadcast_to([1, NS, X]), ALU.is_ge))
                then(nc.vector.tensor_reduce(tab[:], past[:], AX.X, ALU.add))
                then(nc.vector.tensor_scalar_min(tab[:], tab[:], float(X - 1)))
                then(nc.vector.tensor_copy(table[:], tab[:]))
                nc.vector.tensor_copy(dst[:], where[:].rearrange("p k n -> p n k")).then_inc(dst_ok, 1)

            @block.scalar
            def _(act):
                act.wait_ge(gap_ok, 1)
                nc.scalar.activation(eg[:], gap[:], ACT.Exp).then_inc(eg_ok, 1)

            @block.tensor
            def _(pe):
                pe.wait_ge(made, CONST)
                pe.wait_ge(chosen_ok, 1)
                nc.tensor.matmul(pc[:], tri[:], chosen[:].rearrange("p n e -> p (n e)"), start=True, stop=True)
                nc.tensor.matmul(pt[:], ones[:], chosen[:].rearrange("p n e -> p (n e)"), start=True, stop=True).then_inc(count_ok, 1)


def experts(nc, c, dr, w1, w3, w2, table):
    with ExitStack() as ctx:
        def sb(name, shape, dt=F32):
            return ctx.enter_context(nc.sbuf_tensor("e_" + name, shape, dt))

        def ps(name, shape, dt=F32):
            return ctx.enter_context(nc.psum_tensor("e_" + name, shape, dt))

        def sem(name):
            return ctx.enter_context(nc.semaphore("e_" + name))

        def sems(name):
            return [sem(f"{name}{i}") for i in range(2)]
        ST = TS // P
        LAG = 2
        PA = 4
        w1s = sb("w1s", [P, 2, KC, F])
        w3s = sb("w3s", [P, 2, KC, F])
        w2s = sb("w2s", [P, 2, FC, E])
        xr = sb("xr", [P, 2, ST, E])
        xT = sb("xT", [P, 2, KC, TS])
        sg = sb("sg", [P, 2, TS])
        hT = sb("hT", [P, 2, FC, TS])
        y = sb("y", [P, 2, ST, E])
        px = ps("px", [P, 2, KC, TS])
        pa = ps("pa", [P, PA, 2, TS])
        py = ps("py", [P, ST, CH])
        w_in, x_in, y_out = sems("w_in"), sems("x_in"), sems("y_out")
        xt_ps, xt_ok, a_ok, g_ok, h_ok, y_ps, y_ok = (
            sem("xt_ps"), sem("xt_ok"), sem("a_ok"), sem("g_ok"), sem("h_ok"), sem("y_ps"), sem("y_ok"))
        xs = dr["xs"].rearrange("(s i p) e -> s p i e", p=P, i=ST)
        ys = dr["ys"].rearrange("(s i p) e -> s p i e", p=P, i=ST)

        def slots(eng, body):
            body(0, 0, 0, first=True)
            with eng.Fori(0, (NS - 3) // 2) as r:
                body(2 * r + 1, 1, r)
                body(2 * r + 2, 0, r + 1)
            body(NS - 2, 1, (NS - 2) // 2)
            body(NS - 1, 0, (NS - 1) // 2, final=True)

        with nc.Block() as block:
            @block.sync
            def _(sp):
                def load(s, u):
                    e = sp.value_load(table[0:1, bass.ds(s, 1)], min_val=0, max_val=X - 1)
                    sp.dma_start(xr[:, u], xs[s]).then_inc(x_in[u], 16)
                    sp.dma_start(w1s[:, u], w1[e].rearrange("(k p) f -> p k f", p=P)).then_inc(w_in[u], 16)
                    sp.dma_start(w3s[:, u], w3[e].rearrange("(k p) f -> p k f", p=P)).then_inc(w_in[u], 16)
                    sp.dma_start(w2s[:, u], w2[e].rearrange("(k p) f -> p k f", p=P)).then_inc(w_in[u], 16)

                def step(s, u):
                    sp.wait_ge(y_ps, s + 1)
                    load(s + 2, u)
                load(0, 0)
                load(1, 1)
                with sp.Fori(0, (NS - 2) // 2) as r:
                    step(2 * r, 0)
                    step(2 * r + 1, 1)
                for s in range((NS - 2) // 2 * 2, NS - 2):
                    step(s, s % 2)

            @block.gpsimd
            def _(pool):
                def put(s, u, k, first=False, final=False):
                    pool.wait_ge(y_ok, s + 1)
                    pool.dma_start(ys[s], y[:, u]).then_inc(y_out[u], 16)
                slots(pool, put)
                pool.wait_ge(y_out[0], 16 * ((NS + 1) // 2))
                pool.wait_ge(y_out[1], 16 * (NS // 2))

            @block.tensor
            def _(pe):
                def columns(s, u, k):
                    pe.wait_ge(x_in[u], 16 * (k + 1))
                    after(pe, xt_ok, s - 1)
                    for j in range(KC):
                        for i in range(ST):
                            last = nc.tensor.transpose(px[:, u, j, i * P:(i + 1) * P], xr[:, u, i, j * P:(j + 1) * P], c["ident"][:])
                    last.then_inc(xt_ps, 1)

                def hidden(s, u, f):
                    after(pe, h_ok, s * FC + f - PA + 1)
                    for j, w in enumerate((w1s, w3s)):
                        for k in range(KC):
                            last = nc.tensor.matmul(pa[:, f % PA, j, :], w[:, u, k, f * P:(f + 1) * P], xT[:, u, k, :],
                                                    start=(k == 0), stop=(k == KC - 1))
                    last.then_inc(a_ok, 1)

                def outputs(s, u, f):
                    pe.wait_ge(h_ok, s * FC + f + 1)
                    if f == 0:
                        after(pe, y_ok, s)
                    for i in range(ST):
                        last = nc.tensor.matmul(py[:, i, 0:E], hT[:, u, f, i * P:(i + 1) * P], w2s[:, u, f, :],
                                                start=(f == 0), stop=(f == FC - 1))
                    if f == FC - 1:
                        last.then_inc(y_ps, 1)

                def slot(s, u, k, first=False, final=False):
                    if first:
                        columns(s, u, k)
                    pe.wait_ge(xt_ok, s + 1)
                    pe.wait_ge(w_in[u], 48 * (k + 1))
                    for f in range(FC):
                        hidden(s, u, f)
                        if f >= LAG:
                            outputs(s, u, f - LAG)
                        elif not first:
                            outputs(s - 1, 1 - u, FC - LAG + f)
                        if f == FC - 3 and not final:
                            columns(s + 1, 1 - u, k + u)
                    if final:
                        for f in range(FC - LAG, FC):
                            outputs(s, u, f)
                slots(pe, slot)

            @block.scalar
            def _(act):
                def keep_columns(s, u):
                    act.wait_ge(xt_ps, s + 1)
                    nc.scalar.copy(xT[:, u], px[:, u]).then_inc(xt_ok, 1)

                def keep_outputs(s, u, k):
                    act.wait_ge(y_ps, s + 1)
                    act.wait_ge(y_out[u], 16 * k)
                    nc.scalar.copy(y[:, u], py[:, :, 0:E]).then_inc(y_ok, 1)

                def slot(s, u, k, first=False, final=False):
                    if first:
                        keep_columns(s, u)
                    for f in range(FC):
                        act.wait_ge(a_ok, s * FC + f + 1)
                        after(act, h_ok, s * FC + f - 1)
                        nc.scalar.activation(sg[:, f % 2, :], pa[:, f % PA, 0, :], ACT.Silu).then_inc(g_ok, 1)
                        if f == LAG - 1 and not first:
                            keep_outputs(s - 1, 1 - u, k if u else k - 1)
                        if f == FC - 2 and not final:
                            keep_columns(s + 1, 1 - u)
                    if final:
                        keep_outputs(s, u, k)
                slots(act, slot)

            @block.vector
            def _(dve):
                def slot(s, u, k, first=False, final=False):
                    after(dve, y_ps, s - 1)
                    for f in range(FC):
                        dve.wait_ge(g_ok, s * FC + f + 1)
                        nc.vector.tensor_tensor(hT[:, u, f, :], sg[:, f % 2, :], pa[:, f % PA, 1, :], ALU.mult).then_inc(h_ok, 1)
                slots(dve, slot)


def combine(nc, c, dr, dst, gates, res, out):
    I32 = mybir.dt.int32
    with ExitStack() as ctx:
        def sb(name, shape, dt=F32):
            return ctx.enter_context(nc.sbuf_tensor("c_" + name, shape, dt))

        def sem(name):
            return ctx.enter_context(nc.semaphore("c_" + name))
        BUF = 4
        y = sb("y", [P, BUF, 2, E])
        half = sb("half", [P, BUF, E])
        o = sb("o", [P, BUF, E])
        y_in, part_ok, o_ok, o_out = (
            [sem(f"y_in{i}") for i in range(BUF)], sem("part_ok"), sem("o_ok"), [sem(f"o_out{i}") for i in range(BUF)])
        out_v = out.rearrange("(n p) e -> n p e", p=P)
        with nc.Block() as block:
            @block.gpsimd
            def _(pool):
                for t in range(NT):
                    u = t % BUF
                    after(pool, o_ok, t - BUF + 1)
                    for k in range(2):
                        nc.gpsimd.indirect_dma_start(
                            out=y[:, u, k, :], out_offset=None, in_=dr["ys"],
                            in_offset=bass.IndirectOffsetOnAxis(ap=dst[:, t, k:k + 1], axis=0)).then_inc(y_in[u], 16)

            @block.vector
            def _(dve):
                with dve.Fori(0, NT // BUF) as r:
                    for u in range(BUF):
                        t = BUF * r + u
                        dve.wait_ge(y_in[u], 32 * r + 32)
                        dve.wait_ge(o_out[u], 16 * r)
                        nc.vector.scalar_tensor_tensor(out=half[:, u, :], in0=y[:, u, 0, :], scalar=gates[:, t, 0:1],
                                                       in1=res[:, t, :], op0=ALU.mult, op1=ALU.add).then_inc(part_ok, 1)
                        dve.wait_ge(part_ok, t + 1)
                        nc.vector.scalar_tensor_tensor(out=o[:, u, :], in0=y[:, u, 1, :], scalar=gates[:, t, 1:2],
                                                       in1=half[:, u, :], op0=ALU.mult, op1=ALU.add).then_inc(o_ok, 1)

            @block.sync
            def _(sp):
                with sp.Fori(0, NT // BUF) as r:
                    for u in range(BUF):
                        t = BUF * r + u
                        sp.wait_ge(o_ok, t + 1)
                        sp.dma_start(out_v[t], o[:, u, :]).then_inc(o_out[u], 16)
                for u in range(BUF):
                    sp.wait_ge(o_out[u], 16 * NT // BUF)


def constants(nc, c):
    with ExitStack() as ctx:
        made = ctx.enter_context(nc.semaphore("const_made"))
        with nc.Block() as block:
            @block.gpsimd
            def _(pool):
                count = [0]

                def then(ins):
                    count[0] += 1
                    ins.then_inc(made, 1)
                    pool.wait_ge(made, count[0])
                for m in (c["ident"], c["ident16"]):
                    then(nc.gpsimd.memset(m[:], 0.0))
                    then(nc.gpsimd.affine_select(out=m[:], in_=m[:], compare_op=ALU.not_equal, fill=1.0, base=0,
                                                 pattern=[[-1, P]], channel_multiplier=1))
                then(nc.gpsimd.memset(c["far"][:], FAR))
                then(nc.gpsimd.affine_select(out=c["far"][:], in_=c["far"][:], compare_op=ALU.is_ge, fill=0.0, base=0,
                                             pattern=[[1, BW]], channel_multiplier=-1))
                then(nc.gpsimd.affine_select(out=c["far"][:], in_=c["far"][:], compare_op=ALU.is_ge, fill=0.0, base=2 * W,
                                             pattern=[[-1, BW]], channel_multiplier=1))
                then(nc.gpsimd.memset(c["edge"][:], 0.0))
                first = c["edge"][:].rearrange("p (b i) m -> p b i m", i=TB)[:, :, 0, :]
                final = c["edge"][:].rearrange("p (b i) m -> p b i m", i=TB)[:, :, TB - 1, :]
                then(nc.gpsimd.affine_select(out=first, in_=first, compare_op=ALU.is_ge, fill=FAR, base=-W,
                                             pattern=[[0, NB], [1, NM]], channel_multiplier=1))
                then(nc.gpsimd.affine_select(out=final, in_=final, compare_op=ALU.is_ge, fill=FAR, base=P - 1 + W,
                                             pattern=[[0, NB], [-1, NM]], channel_multiplier=-1))


def build(nc, x, Wq, bq, Wk, bk, Wv, bv, Wo, bo, rel_k, rel_v, gate_w, gate_b, w1, w3, w2, out, stages=9):
    with ExitStack() as ctx:
        def sb(name, shape, dt=F32):
            return ctx.enter_context(nc.sbuf_tensor(name, shape, dt))
        c = dict(ident=sb("ident", [P, P]), ident16=sb("ident16", [P, P], BF16), far=sb("far", [P, BW], BF16),
                 edge=sb("edge", [P, NT, NM]))
        x = x.rearrange("b l e -> (b l) e")
        out = out.rearrange("b l e -> (b l) e")
        dr = scratch(nc)
        band = sb("band", [P, NT, NM, H])
        bmax = sb("bmax", [P, NT, H])
        logits = sb("logits", [P, NT, X])
        constants(nc, c)
        norm_and_project(nc, c, dr, x, Wq, bq, Wk, bk, Wv, bv, rel_k, gate_w, gate_b, band, logits)
        if stages < 2: return
        dst = sb("dst", [P, NT, 2], mybir.dt.int32)
        gates = sb("gates", [P, NT, 2])
        table = sb("table", [1, NS], mybir.dt.int32)
        route(nc, c, dr, logits, dst, gates, table)
        if stages == 2:
            return
        band_scores(nc, c, dr, band, bmax)
        if stages < 3: return
        bmax_g = sb("bmax_g", [P, NG, HG, TB])
        neg_g = sb("neg_g", [P, NG, HG, TB])
        neg = sb("neg", [P, NT, H])
        oa = sb("oa", [P, NG, TB, HG, D + 1])
        regroup(nc, [(bmax_g[:, b * 4:(b + 1) * 4].rearrange("p g h i -> p (g h) i"),
                      bmax[:, b * TB:(b + 1) * TB, :].rearrange("p i h -> p h i")) for b in range(NB)])
        attention(nc, c, dr, band, bmax_g, neg_g, oa)
        if stages < 4: return
        oa_t = sb("oa_t", [P, NT, H, D + 1])
        res = sb("res", [P, NT, E])
        regroup(nc, [(neg[:, b * TB:(b + 1) * TB, :].rearrange("p i h -> p h i"),
                      neg_g[:, b * 4:(b + 1) * 4].rearrange("p g h i -> p (g h) i")) for b in range(NB)]
                + [(oa_t[:, b * TB:(b + 1) * TB, g * HG:(g + 1) * HG], oa[:, b * 4 + g]) for b in range(NB) for g in range(4)])
        finish(nc, c, dr, x, Wo, bo, rel_v, band, neg, oa_t, res)
        if stages < 5:
            store(nc, res, out)
            return
        experts(nc, c, dr, w1, w3, w2, table)
        combine(nc, c, dr, dst, gates, res, out)


_INS = ['L0_attn_hidden_states', 'L0_attn_Wq', 'L0_attn_bq', 'L0_attn_Wk', 'L0_attn_bk', 'L0_attn_Wv', 'L0_attn_bv',
        'L0_attn_Wo', 'L0_attn_bo', 'L0_attn_emb_rel_k', 'L0_attn_emb_rel_v', 'L0_ffn_gate_w', 'L0_ffn_gate_b',
        'L0_ffn_w1', 'L0_ffn_w3', 'L0_ffn_w2']


def kernel(**inputs):
    import numpy as _np
    import concourse.bacc as _bacc
    from concourse.bass_utils import run_bass_kernel_spmd as _run

    nc = _bacc.Bacc("TRN2", target_bir_lowering=False, num_devices=1)
    arrays, args = {}, []
    for name in _INS:
        a = _np.ascontiguousarray(inputs[name])
        arrays[f"in_{name}_dram"] = a
        args.append(nc.dram_tensor(f"in_{name}_dram", a.shape, mybir.dt.from_np(a.dtype), kind="ExternalInput").ap())
    args.append(nc.dram_tensor("out_0_dram", (NB, L, E), F32, kind="ExternalOutput").ap())
    build(nc, *args)
    r = _run(nc, [arrays], core_ids=[0])
    return r.results[0]["out_0_dram"]
```

```python
import concourse.bass as bass
from concourse import mybir
from contextlib import ExitStack

F32 = mybir.dt.float32
BF16 = mybir.dt.bfloat16
ALU = mybir.AluOpType
ACT = mybir.ActivationFunctionType
AX = mybir.AxisListType

P = 128
NB, L, E = 4, 1024, 256
H, D = 16, 16
T = NB * L
NT = T // P
TB = L // P
KC = E // P
CH = 512
NC = T // CH
CT = CH // P
W = 4
NM = 2 * W + 1
HG = 4
NG = NB * H // HG
VW = 32
ROWS = 6 * D
MROWS = 2
BW = P + 2 * W
X = 8
F = 1024
FC = F // P
TS = 2 * P
NS = 2 * T // TS + X - 1
N_ZERO = NS * TS // P // 6
FAR = -1e30
EPS = 1e-5
Q_PARTS = (0, 0, 0, 1, 1, 2)
K_PARTS = (0, 1, 2, 0, 1, 0)


def after(eng, sem, value):
    if not (isinstance(value, int) and value <= 0):
        eng.wait_ge(sem, value)


def scratch(nc):
    def dram(name, shape, dt):
        return nc.dram_tensor(name, shape, dt, kind="Internal").ap()
    return dict(
        xn=dram("xn_rows", [T, E], F32),
        q=dram("q_rows", [T, E], F32),
        k=dram("k_rows", [W + T + W, E], F32),
        v=dram("v_rows", [W + T + W, E], F32),
        vx=dram("vx_rows", [T, H * VW], F32),
        sq=dram("q_stack", [NB, H // HG, HG, ROWS, L], BF16),
        sk=dram("k_stack", [NB, H // HG, HG, ROWS, L], BF16),
        xs=dram("slot_rows", [NS * TS, E], F32),
        ys=dram("slot_outputs", [NS * TS, E], F32),
    )


def norm_and_project(nc, c, dr, x, Wq, bq, Wk, bk, Wv, bv, rel_k, gate_w, gate_b, band, logits):
    with ExitStack() as ctx:
        def sb(name, shape, dt=F32):
            return ctx.enter_context(nc.sbuf_tensor("a_" + name, shape, dt))

        def ps(name, shape, dt=F32):
            return ctx.enter_context(nc.psum_tensor("a_" + name, shape, dt))

        def sem(name):
            return ctx.enter_context(nc.semaphore("a_" + name))

        w = {n: sb("w" + n, [P, KC, E]) for n in "qkv"}
        bcol = sb("bcol", [P, 2, KC])
        gw = sb("gw", [P, KC, X])
        gb = sb("gb", [P, X])
        bvb = sb("bvb", [P, E])
        relk = sb("relk", [P, NM])
        hmask = sb("hmask", [P, 8])
        rk = sb("rk", [P, NM, 8])
        zpad = sb("zpad", [W, E])
        xt = sb("xt", [P, CT, E])
        st = sb("st", [P, CT, 6])
        mv = sb("mv", [P, 3, CT])
        std = sb("std", [P, CT])
        rstd = sb("rstd", [P, CT])
        xn = sb("xn", [P, CT, E])
        xnT = sb("xnT", [P, KC, CH])
        qkT = sb("qkT", [P, 2 * KC, CH])
        rest = sb("rest", [P, 2 * KC, CH])
        part = [sb(f"part{i}", [P, 2 * KC, CH], BF16) for i in range(3)]
        vrow = sb("vrow", [P, CT, E])
        vx = sb("vx", [P, CT, H, VW])
        qrow = sb("qrow", [P, CT, E])
        krow = sb("krow", [P, CT, E])
        pT = ps("pT", [P, 2, CH])
        pqk = ps("pqk", [P, 2 * KC, CH])
        pv = ps("pv", [P, 2, CH])

        w_in, const_ok, x_in = sem("w_in"), sem("const_ok"), sem("x_in")
        dchain, var_ok, std_ok, xn_ok = sem("dchain"), sem("var_ok"), sem("std_ok"), sem("xn_ok")
        tp_ok, xnT_ok, qk_ok, v_ok, qkT_ok = sem("tp_ok"), sem("xnT_ok"), sem("qk_ok"), sem("v_ok"), sem("qkT_ok")
        rows_ok, rel_ok, qrow_ok, krow_ok = sem("rows_ok"), sem("rel_ok"), sem("qrow_ok"), sem("krow_ok")
        v_out, parts_ok, rel_out = sem("v_out"), sem("parts_ok"), sem("rel_out")
        st_xn, st_parts, st_rows, st_v, st_pad = (
            sem("st_xn"), sem("st_parts"), sem("st_rows"), sem("st_v"), sem("st_pad"))
        achain, bias_ok = sem("achain"), sem("bias_ok")

        x_v = x.rearrange("(n i p) e -> n p i e", p=P, i=CT)

        def rows_view(a, off=0):
            return a[off:off + T, :].rearrange("(n i p) e -> n p i e", p=P, i=CT)
        N_LOAD = 3 + 2 + 1 + 8 + 2
        RELW = NM * H
        RG = RELW + X

        with nc.Block() as block:
            @block.sync
            def _(sp):
                for n, src in (("q", Wq), ("k", Wk), ("v", Wv)):
                    sp.dma_start(w[n][:], src.rearrange("(k p) e -> p k e", p=P)).then_inc(w_in, 16)
                for i, src in enumerate((bq, bk)):
                    sp.dma_start(bcol[:, i, :], src.rearrange("(k p) -> p k", p=P),
                                 allow_slow_non_contiguous=True).then_inc(w_in, 16)
                sp.dma_start(bvb[:], bv.rearrange("(o e) -> o e", o=1).broadcast_to([P, E])).then_inc(w_in, 16)
                for h in range(8):
                    sp.dma_start(relk[h * D:(h + 1) * D, :], rel_k[0].rearrange("m d -> d m"),
                                 allow_slow_non_contiguous=True).then_inc(w_in, 16)
                sp.dma_start(gw[:], gate_w.rearrange("(k p) e -> p k e", p=P)).then_inc(w_in, 16)
                sp.dma_start(gb[:], gate_b.rearrange("(o e) -> o e", o=1).broadcast_to([P, X])).then_inc(w_in, 16)
                sp.wait_ge(const_ok, 1)
                for a in (dr["k"], dr["v"]):
                    for r in (0, W + T):
                        sp.dma_start(a[r:r + W, :], zpad[:]).then_inc(st_pad, 16)
                sp.dma_start(xt[:], x_v[0]).then_inc(x_in, 16)

                def chunk(b, u, more=True):
                    n = 2 * b + u
                    sp.wait_ge(xn_ok, n + 1)
                    if more:
                        sp.dma_start(xt[:], x_v[n + 1]).then_inc(x_in, 16)
                    sp.dma_start(rows_view(dr["xn"])[n], xn[:]).then_inc(st_xn, 16)
                    sp.wait_ge(v_out, n + 1)
                    sp.dma_start(rows_view(dr["v"], W)[n], vrow[:]).then_inc(st_v, 16)
                    sp.dma_start(rows_view(dr["vx"])[n], vx[:].rearrange("p i h v -> p i (h v)")).then_inc(st_v, 16)
                    sp.wait_ge(parts_ok, n + 1)
                    for j in range(6):
                        for a, (stack, parts) in enumerate(((dr["sq"], Q_PARTS), (dr["sk"], K_PARTS))):
                            for k in range(KC):
                                dst = stack[b, 2 * k:2 * k + 2, :, j * D:(j + 1) * D, u * CH:(u + 1) * CH].rearrange(
                                    "g h d c -> (g h) d c")
                                sp.dma_start(dst, part[parts[j]][:, a * KC + k, :]).then_inc(st_parts, 16)
                    sp.wait_ge(krow_ok, n + 1)
                    sp.dma_start(rows_view(dr["k"], W)[n], krow[:]).then_inc(st_rows, 16)
                    sp.wait_ge(qrow_ok, n + 1)
                    sp.dma_start(rows_view(dr["q"])[n], qrow[:]).then_inc(st_rows, 16)
                with sp.Fori(0, NB - 1) as b:
                    chunk(b, 0)
                    chunk(b, 1)
                chunk(NB - 1, 0)
                chunk(NB - 1, 1, more=False)
                sp.wait_ge(st_pad, 64)
                sp.wait_ge(st_xn, 16 * NC)
                sp.wait_ge(st_v, 32 * NC)
                sp.wait_ge(st_parts, 16 * 24 * NC)
                sp.wait_ge(st_rows, 32 * NC)

            @block.gpsimd
            def _(pool):
                nc.gpsimd.memset(zpad[:], 0.0).then_inc(const_ok, 1)
                nc.gpsimd.memset(vx[:], 0.0).then_inc(const_ok, 1)
                pool.wait_ge(const_ok, 2)
                nc.gpsimd.memset(vx[:, :, :, D:D + 1], 1.0).then_inc(const_ok, 1)
                nc.gpsimd.memset(hmask[:], 1.0).then_inc(const_ok, 1)
                pool.wait_ge(const_ok, 4)
                nc.gpsimd.affine_select(out=hmask[:], in_=hmask[:], compare_op=ALU.is_ge, fill=0.0, base=0,
                                        pattern=[[-D, 8]], channel_multiplier=1).then_inc(const_ok, 1)
                pool.wait_ge(const_ok, 5)
                nc.gpsimd.affine_select(out=hmask[:], in_=hmask[:], compare_op=ALU.is_ge, fill=0.0, base=D - 1,
                                        pattern=[[D, 8]], channel_multiplier=-1).then_inc(const_ok, 1)
                pool.wait_ge(const_ok, 6)
                pool.wait_ge(w_in, 16 * N_LOAD)
                nc.gpsimd.tensor_tensor(rk[:], relk[:].rearrange("p (m o) -> p m o", o=1).broadcast_to([P, NM, 8]),
                                        hmask[:].rearrange("p (o h) -> p o h", o=1).broadcast_to([P, NM, 8]),
                                        ALU.mult).then_inc(const_ok, 1)

            @block.vector
            def _(dve):
                dve.wait_ge(w_in, 16 * N_LOAD)
                dve.wait_ge(const_ok, 3)
                with dve.Fori(0, NC) as n:
                    STEPS = 4

                    def link(ins, k):
                        ins.then_inc(dchain, 1)
                        dve.wait_ge(dchain, n * STEPS + k)
                    dve.wait_ge(x_in, 16 * n + 16)
                    for i in range(CT - 1):
                        nc.vector.bn_stats(st[:, i, :], xt[:, i, :])
                    link(nc.vector.bn_stats(st[:, CT - 1, :], xt[:, CT - 1, :]), 1)
                    nc.vector.tensor_tensor(mv[:, 0, :], st[:, :, 1], st[:, :, 4], ALU.add)
                    nc.vector.tensor_tensor(mv[:, 1, :], st[:, :, 1], st[:, :, 4], ALU.subtract)
                    link(nc.vector.tensor_tensor(mv[:, 2, :], st[:, :, 2], st[:, :, 5], ALU.add), 2)
                    nc.vector.tensor_scalar(mv[:, 0, :], mv[:, 0, :], 0.5, None, ALU.mult)
                    nc.vector.tensor_scalar(mv[:, 2, :], mv[:, 2, :], 1.0 / E, EPS, ALU.mult, ALU.add)
                    link(nc.vector.scalar_tensor_tensor(out=mv[:, 1, :], in0=mv[:, 1, :], scalar=0.25, in1=mv[:, 1, :],
                                                        op0=ALU.mult, op1=ALU.mult), 3)
                    nc.vector.tensor_tensor(std[:], mv[:, 1, :], mv[:, 2, :], ALU.add).then_inc(var_ok, 1)
                    dve.wait_ge(std_ok, n + 1)
                    link(nc.vector.reciprocal(rstd[:], std[:]), 4)
                    dve.wait_ge(tp_ok, n)
                    dve.wait_ge(st_xn, 16 * n)
                    for i in range(CT):
                        last = nc.vector.tensor_scalar(xn[:, i, :], xt[:, i, :], mv[:, 0, i:i + 1], rstd[:, i:i + 1],
                                                       ALU.subtract, ALU.mult)
                    last.then_inc(xn_ok, 1)
                    dve.wait_ge(v_ok, n + 1)
                    dve.wait_ge(st_v, 32 * n)
                    for u in range(2):
                        src = pv[:, u, :].rearrange("p (i e) -> p i e", i=2)
                        b = bvb[:].rearrange("p (o e) -> p o e", o=1).broadcast_to([P, 2, E])
                        nc.vector.tensor_tensor(vrow[:, 2 * u:2 * u + 2, :], src, b, ALU.add)
                        for i in range(2):
                            last = nc.vector.tensor_tensor(
                                vx[:, 2 * u + i, :, 0:D], src[:, i, :].rearrange("p (h d) -> p h d", d=D),
                                bvb[:].rearrange("p (h d) -> p h d", d=D), ALU.add)
                    last.then_inc(v_out, 1)
                    dve.wait_ge(qkT_ok, n + 1)
                    dve.wait_ge(st_parts, 16 * 24 * n)
                    nc.vector.tensor_copy(part[0][:], qkT[:]).then_inc(achain, 1)
                    dve.wait_ge(achain, 3 * n + 1)
                    nc.vector.tensor_tensor(rest[:], qkT[:], part[0][:], ALU.subtract).then_inc(achain, 1)
                    dve.wait_ge(achain, 3 * n + 2)
                    nc.vector.tensor_copy(part[1][:], rest[:]).then_inc(achain, 1)
                    dve.wait_ge(achain, 3 * n + 3)
                    nc.vector.tensor_tensor(part[2][:], rest[:], part[1][:], ALU.subtract).then_inc(parts_ok, 1)
                    dve.wait_ge(rel_ok, n + 1)
                    for i in range(CT):
                        o = (i % 2) * RG
                        nc.vector.tensor_tensor(logits[:, n * CT + i, :], pT[:, i // 2, o + RELW:o + RG], gb[:], ALU.add)
                        src = pT[:, i // 2, o:o + RELW].rearrange("p (c m h) -> p c m h", c=2, m=NM)
                        for k in range(KC):
                            last = nc.vector.tensor_tensor(
                                band[:, n * CT + i, :, k * 8:(k + 1) * 8], src[:, k, :, :],
                                c["edge"][:, n * CT + i, :].rearrange("p (m o) -> p m o", o=1).broadcast_to([P, NM, 8]),
                                ALU.add)
                    last.then_inc(rel_out, 1)
                    dve.wait_ge(rows_ok, n + 1)
                    dve.wait_ge(st_rows, 32 * n)
                    for u in range(2):
                        last = nc.vector.tensor_copy(krow[:, 2 * u:2 * u + 2, :],
                                                     pqk[:, 2 + u, :].rearrange("p (i e) -> p i e", i=2))
                    last.then_inc(krow_ok, 1)

            @block.scalar
            def _(act):
                act.wait_ge(w_in, 16 * N_LOAD)
                nc.scalar.mul(bcol[:, 0, :], bcol[:, 0, :], float(D) ** -0.5).then_inc(bias_ok, 1)
                act.wait_ge(bias_ok, 1)
                with act.Fori(0, NC) as n:
                    act.wait_ge(var_ok, n + 1)
                    nc.scalar.activation(std[:], std[:], ACT.Sqrt).then_inc(std_ok, 1)
                    act.wait_ge(tp_ok, n + 1)
                    act.wait_ge(rel_ok, n)
                    for k in range(KC):
                        last = nc.scalar.copy(xnT[:, k, :], pT[:, k, :])
                    last.then_inc(xnT_ok, 1)
                    act.wait_ge(qk_ok, n + 1)
                    act.wait_ge(parts_ok, n)
                    act.wait_ge(rel_ok, n)
                    for a in range(2 * KC):
                        last = nc.scalar.activation(qkT[:, a, :], pqk[:, a, :], ACT.Identity,
                                                    bias=bcol[:, a // KC, a % KC:a % KC + 1],
                                                    scale=float(D) ** -0.5 if a < KC else 1.0)
                    last.then_inc(qkT_ok, 1)
                    act.wait_ge(rows_ok, n + 1)
                    act.wait_ge(st_rows, 32 * n)
                    for u in range(2):
                        last = nc.scalar.copy(qrow[:, 2 * u:2 * u + 2, :],
                                              pqk[:, u, :].rearrange("p (i e) -> p i e", i=2))
                    last.then_inc(qrow_ok, 1)

            @block.tensor
            def _(pe):
                pe.wait_ge(w_in, 16 * N_LOAD)
                pe.wait_ge(const_ok, 7)
                with pe.Fori(0, NC) as n:
                    pe.wait_ge(xn_ok, n + 1)
                    pe.wait_ge(rel_out, n)
                    for k in range(KC):
                        for i in range(CT):
                            last = nc.tensor.transpose(pT[:, k, i * P:(i + 1) * P], xn[:, i, k * P:(k + 1) * P], c["ident"][:])
                    last.then_inc(tp_ok, 1)
                    pe.wait_ge(xnT_ok, n + 1)
                    pe.wait_ge(krow_ok, n)
                    pe.wait_ge(qrow_ok, n)
                    for a in range(2 * KC):
                        m = a % KC
                        for k in range(KC):
                            last = nc.tensor.matmul(pqk[:, a, :], w["qk"[a // KC]][:, k, m * P:(m + 1) * P], xnT[:, k, :],
                                                    start=(k == 0), stop=(k == KC - 1))
                    last.then_inc(qk_ok, 1)
                    pe.wait_ge(v_out, n)
                    for i in range(CT):
                        for k in range(KC):
                            last = nc.tensor.matmul(pv[:, i // 2, (i % 2) * E:(i % 2 + 1) * E], xnT[:, k, i * P:(i + 1) * P],
                                                    w["v"][:, k, :], start=(k == 0), stop=(k == KC - 1))
                    last.then_inc(v_ok, 1)
                    pe.wait_ge(qkT_ok, n + 1)
                    for a in range(2):
                        for i in range(CT):
                            for k in range(KC):
                                o = (i % 2) * E + k * P
                                last = nc.tensor.transpose(pqk[:, 2 * a + i // 2, o:o + P],
                                                           qkT[:, a * KC + k, i * P:(i + 1) * P], c["ident"][:])
                    last.then_inc(rows_ok, 1)
                    for i in range(CT):
                        for k in range(KC):
                            o = (i % 2) * RG + k * NM * 8
                            last = nc.tensor.matmul(pT[:, i // 2, o:o + NM * 8], qkT[:, k, i * P:(i + 1) * P],
                                                    rk[:].rearrange("p m h -> p (m h)"), start=True, stop=True)
                        o = (i % 2) * RG + RELW
                        for k in range(KC):
                            last = nc.tensor.matmul(pT[:, i // 2, o:o + X], xnT[:, k, i * P:(i + 1) * P], gw[:, k, :],
                                                    start=(k == 0), stop=(k == KC - 1))
                    last.then_inc(rel_ok, 1)


def band_scores(nc, c, dr, band, bmax):
    with ExitStack() as ctx:
        def sb(name, shape, dt=F32):
            return ctx.enter_context(nc.sbuf_tensor("b_" + name, shape, dt))

        def sem(name):
            return ctx.enter_context(nc.semaphore("b_" + name))
        BUF = 2
        q = sb("q", [P, BUF, E])
        ks = sb("ks", [P, BUF, NM * E])
        prod = sb("prod", [P, BUF, NM, H, D])
        dot = sb("dot", [P, BUF, NM * H])
        q_in = [sem(f"q_in{i}") for i in range(BUF)]
        mul_ok, sum_ok, chain = sem("mul_ok"), sem("sum_ok"), sem("chain")
        q_v = dr["q"].rearrange("(n p) e -> n p e", p=P)

        def windows(n):
            v = dr["k"][0:T, :].rearrange("(n p) e -> n p e", p=P)[n]
            return bass.AP(v.tensor, v.offset, [[E, P], [1, NM * E]])

        with nc.Block() as block:
            @block.sync
            def _(sp):
                def load(t, u):
                    sp.dma_start(q[:, u, :], q_v[t]).then_inc(q_in[u], 16)
                    sp.dma_start(ks[:, u, :], windows(t)).then_inc(q_in[u], 16)
                for u in range(BUF):
                    load(u, u)
                with sp.Fori(0, NT // BUF - 1) as r:
                    for u in range(BUF):
                        sp.wait_ge(mul_ok, BUF * r + u + 1)
                        load(BUF * r + BUF + u, u)

            @block.gpsimd
            def _(pool):
                with pool.Fori(0, NT // BUF) as r:
                    for u in range(BUF):
                        pool.wait_ge(q_in[u], 32 * r + 32)
                        pool.wait_ge(sum_ok, BUF * r)
                        nc.gpsimd.tensor_tensor(
                            prod[:, u].rearrange("p m h d -> p m (h d)"), ks[:, u, :].rearrange("p (m e) -> p m e", m=NM),
                            q[:, u:u + 1, :].broadcast_to([P, NM, E]), ALU.mult).then_inc(mul_ok, 1)

            @block.vector
            def _(dve):
                with dve.Fori(0, NT // BUF) as r:
                    for u in range(BUF):
                        t = r * BUF + u
                        dve.wait_ge(mul_ok, t + 1)
                        nc.vector.tensor_reduce(dot[:, u, :], prod[:, u].rearrange("p m h d -> p (m h) d"),
                                                AX.X, ALU.add).then_inc(sum_ok, 1)
                        dve.wait_ge(sum_ok, t + 1)
                        b = band[:, t, :, :].rearrange("p m h -> p (m h)")
                        nc.vector.tensor_tensor(b, b, dot[:, u, :], ALU.add).then_inc(chain, 1)
                        dve.wait_ge(chain, t + 1)
                        nc.vector.tensor_reduce(bmax[:, t, :], band[:, t, :, :].rearrange("p m h -> p h m"), AX.X, ALU.max)


def attention(nc, c, dr, bmax, neg, oa, dst, zero_out):
    XS = 2 * TB * HG
    QUOTA = 52
    B1, B2, BP = 3, 3, 3
    with ExitStack() as ctx:
        def sb(name, shape, dt=F32):
            return ctx.enter_context(nc.sbuf_tensor("t_" + name, shape, dt))

        def ps(name, shape, dt=F32):
            return ctx.enter_context(nc.psum_tensor("t_" + name, shape, dt))

        def sem(name):
            return ctx.enter_context(nc.semaphore("t_" + name))

        def sems(name):
            return [sem(f"{name}{i}") for i in range(2)]
        q1 = sb("q1", [P, 2, HG, L], BF16)
        k1 = sb("k1", [P, 2, HG, L], BF16)
        q2 = sb("q2", [P, 2, HG, L], BF16)
        k2 = sb("k2", [P, 2, HG, L], BF16)
        vx = sb("vx", [P, 2, TB, HG * VW])
        pr = sb("pr", [P, BP, HG, CH])
        mx = sb("mx", [P, HG, TB, 2])
        ma = sb("ma", [P, HG, TB])
        mb = sb("mb", [P, HG, TB])
        mparts = sb("mparts", [P, 4, HG, TB], BF16)
        mt = sb("mt", [2 * HG * TB, P], BF16)
        ot = sb("ot", [P, CH])
        xn = sb("xn", [P, NT, E])
        xn_in, sent = sem("xn_in"), sem("sent")
        s1 = ps("s1", [P, B1, CH])
        s2 = ps("s2", [P, B2, CH])
        po = ps("po", [P, CH])
        misc = ps("misc", [P, CH])
        in1, in2, vin, ones_ok = sems("in1_"), sems("in2_"), sems("vin"), sem("ones_ok")
        zeros_ok = sem("zeros_ok")
        s1_ok, mx_ok, chain, mparts_ok, mt_ps_ok, mt_ok, m_in = (
            sem("s1_ok"), sem("mx_ok"), sem("chain"), sem("mparts_ok"), sem("mt_ps_ok"), sem("mt_ok"), sem("m_in"))
        s2_ok, exp_ok, pv_ok, ot_ok, otT_ok, oa_ok = (
            sem("s2_ok"), sem("exp_ok"), sem("pv_ok"), sem("ot_ok"), sem("otT_ok"), sem("oa_ok"))
        sq = dr["sq"].rearrange("b g h r c -> (b g) r h c")
        sk = dr["sk"].rearrange("b g h r c -> (b g) r h c")
        vd = dr["vx"].rearrange("(b i p) (g v) -> b g p i v", p=P, i=TB, v=HG * VW)

        def turn(u, n, per_group):
            return (u * per_group + n) % 3

        def freed(g, u, n, per_group):
            return g * per_group + n - 2 + (1 if u == 0 and n < 2 else 0)

        def far_pieces(tile, half):
            a, b = max(tile * P - W, half * CH), min(tile * P + P + W, half * CH + CH)
            return [(a - half * CH, b - a, a - (tile * P - W))] if a < b else []

        with nc.Block() as block:
            @block.sync
            def _(sp):
                def load1(g, u):
                    for dst, src in ((q1, sq), (k1, sk)):
                        sp.dma_start(dst[0:ROWS, u], src[g]).then_inc(in1[u], 16)

                def load2(g, b, gg, u):
                    for dst, src in ((q2, sq), (k2, sk)):
                        sp.dma_start(dst[0:ROWS, u], src[g]).then_inc(in2[u], 16)
                    sp.dma_start(vx[:, u], vd[b, gg]).then_inc(vin[u], 16)

                def maximum(g, u):
                    sp.wait_ge(mt_ok, g + 1)
                    for j in range(MROWS):
                        sp.dma_start(q2[ROWS + j:ROWS + j + 1, u].rearrange("o h (i t) -> o (h i) t", t=P),
                                     mt[j * HG * TB:(j + 1) * HG * TB, :]).then_inc(m_in, 16)
                load1(0, 0)
                load1(1, 1)
                load2(0, 0, 0, 0)
                sp.dma_start(xn[:], dr["xn"].rearrange("(n p) e -> p n e", p=P)).then_inc(xn_in, 16)
                maximum(0, 0)
                load2(1, 0, 1, 1)

                def step(g, b2, g2, u, more1=True, more2=True):
                    if more1:
                        sp.wait_ge(s1_ok, XS * (g + 2))
                        load1(g + 3, 1 - u)
                    maximum(g + 1, 1 - u)
                    if more2:
                        sp.wait_ge(pv_ok, 2 * TB * (g + 1))
                        load2(g + 2, b2, g2, u)
                sp.wait_ge(s1_ok, XS)
                load1(2, 0)
                step(0, 0, 2, 0)
                step(1, 0, 3, 1)
                with sp.Fori(0, NB - 2) as r:
                    for v in range(4):
                        step(4 * r + 2 + v, r + 1, v, v % 2)
                step(10, 3, 0, 0)
                step(11, 3, 1, 1)
                step(12, 3, 2, 0)
                step(13, 3, 3, 1, more1=False)
                step(14, 0, 0, 0, more1=False, more2=False)

            @block.gpsimd
            def _(pool):
                for u in range(2):
                    nc.gpsimd.memset(k2[ROWS:ROWS + MROWS, u], 1.0).then_inc(ones_ok, 1)
                pool.wait_ge(zero_out, 16 * N_ZERO)
                pool.wait_ge(xn_in, 16)
                for t in range(NT):
                    for k in range(2):
                        nc.gpsimd.indirect_dma_start(
                            out=dr["xs"], out_offset=bass.IndirectOffsetOnAxis(ap=dst[:, t, k:k + 1], axis=0),
                            in_=xn[:, t, :], in_offset=None).then_inc(sent, 16)
                pool.wait_ge(sent, 32 * NT)

            @block.tensor
            def _(pe):
                def pass1(g, u, n):
                    h, i, half, bank = n // (2 * TB), n // 2 % TB, n % 2, turn(u, n, XS)
                    after(pe, mx_ok, freed(g, u, n, XS))
                    far = far_pieces(i, half)
                    last = nc.tensor.matmul(s1[:, bank, :], q1[0:ROWS, u, h, i * P:(i + 1) * P],
                                            k1[0:ROWS, u, h, half * CH:(half + 1) * CH], start=True, stop=not far)
                    for a, m, j in far:
                        last = nc.tensor.matmul(s1[:, bank, a:a + m], c["ident16"][:], c["far"][:, j:j + m],
                                                start=False, stop=True)
                    last.then_inc(s1_ok, 1)

                def pass2(g, u, n):
                    half, i, h, bank = n // (TB * HG), n // HG % TB, n % HG, turn(u, n, XS)
                    after(pe, exp_ok, freed(g, u, n, XS))
                    far = far_pieces(i, half)
                    last = nc.tensor.matmul(s2[:, bank, :], k2[0:ROWS + MROWS, u, h, i * P:(i + 1) * P],
                                            q2[0:ROWS + MROWS, u, h, half * CH:(half + 1) * CH],
                                            start=True, stop=not far)
                    for a, m, j in far:
                        last = nc.tensor.matmul(s2[:, bank, a:a + m], c["ident16"][:], c["far"][:, j:j + m],
                                                start=False, stop=True)
                    last.then_inc(s2_ok, 1)

                def values(g, u, k):
                    half, i = k // TB, k % TB
                    pe.wait_ge(exp_ok, g * XS + HG * (k + 1))
                    if i == 0:
                        after(pe, ot_ok, 2 * g + half)
                    for h in range(HG):
                        last = nc.tensor.matmul(po[h * VW:(h + 1) * VW, :], vx[:, u, i, h * VW:(h + 1) * VW],
                                                pr[:, turn(u, k, 2 * TB), h, :], start=(i == 0), stop=(i == TB - 1),
                                                tile_position=(0, h * VW))
                    last.then_inc(pv_ok, 1)

                def output_rows(g, half, made):
                    pe.wait_ge(ot_ok, 2 * g + half + 1)
                    after(pe, mt_ok, made)
                    after(pe, oa_ok, 2 * g + half)
                    for i in range(CT):
                        last = nc.tensor.transpose(misc[:, i * P:(i + 1) * P], ot[:, i * P:(i + 1) * P], c["ident"][:])
                    last.then_inc(otT_ok, 1)

                def maximum_rows(g, outs):
                    pe.wait_ge(mparts_ok, g + 1)
                    after(pe, oa_ok, outs)
                    nc.tensor.transpose(misc[:, 0:P // 2].bitcast(BF16), mparts[:].rearrange("p j h i -> p (j h i)"),
                                        c["ident16"][:]).then_inc(mt_ps_ok, 1)

                def group(g, u, k, more=True, carried=True):
                    pe.wait_ge(in2[u], 32 * k)
                    pe.wait_ge(vin[u], 16 * k)
                    pe.wait_ge(m_in, 16 * MROWS * (g + 1))
                    if more:
                        pe.wait_ge(in1[1 - u], 32 * (k + u))
                    done = 0
                    for n in range(XS):
                        pass2(g, u, n)
                        while more and done < min(XS, -(-XS * (n + 1) // QUOTA)):
                            pass1(g + 1, 1 - u, done)
                            done += 1
                        if n % HG == 2:
                            if n > HG:
                                values(g, u, n // HG - 1)
                            elif carried:
                                values(g - 1, 1 - u, 2 * TB - 1)
                        if n == 14 and carried:
                            output_rows(g - 1, 1, g + 1)
                        if n == 46:
                            output_rows(g, 0, g + 1)
                        if n == XS - 3 and more:
                            maximum_rows(g + 1, 2 * g + 1)

                pe.wait_ge(ones_ok, 2)
                pe.wait_ge(in1[0], 32)
                for n in range(XS):
                    pass1(0, 0, n)
                maximum_rows(0, 0)
                group(0, 0, 1, carried=False)
                with pe.Fori(0, NG // 2 - 1) as r:
                    group(2 * r + 1, 1, r + 1)
                    group(2 * r + 2, 0, r + 2)
                group(NG - 1, 1, NG // 2, more=False)
                values(NG - 1, 1, 2 * TB - 1)
                output_rows(NG - 1, 1, NG)

            @block.vector
            def _(dve):
                CHAIN = 4

                bmax_v = bmax[:].rearrange("p (b i) (g h) -> p b g h i", i=TB, h=HG)
                neg_v = neg[:].rearrange("p (b i) (g h) -> p b g h i", i=TB, h=HG)

                def maxima(b, v):
                    def link(ins, k):
                        ins.then_inc(chain, 1)
                        dve.wait_ge(chain, g * CHAIN + k)
                    g, u = NG // NB * b + v, v % 2
                    for n in range(XS):
                        dve.wait_ge(s1_ok, g * XS + n + 1)
                        nc.vector.reduce_max(mx[:, n // (2 * TB), n // 2 % TB, n % 2:n % 2 + 1],
                                             s1[:, turn(u, n, XS), :], AX.X).then_inc(mx_ok, 1)
                    dve.wait_ge(mx_ok, (g + 1) * XS)
                    link(nc.vector.tensor_tensor(ma[:], mx[:, :, :, 0], mx[:, :, :, 1], ALU.max), 1)
                    link(nc.vector.tensor_tensor(mb[:], ma[:], bmax_v[:, b, v], ALU.max), 2)
                    link(nc.vector.tensor_scalar(mparts[:, 0], mb[:], -1.0, None, ALU.mult), 3)
                    link(nc.vector.scalar_tensor_tensor(out=mparts[:, 1], in0=mb[:], scalar=-1.0, in1=mparts[:, 0],
                                                        op0=ALU.mult, op1=ALU.subtract), 4)
                    nc.vector.tensor_tensor(neg_v[:, b, v], mparts[:, 0], mparts[:, 1], ALU.add).then_inc(mparts_ok, 1)
                    dve.wait_ge(mt_ps_ok, g + 1)
                    after(dve, m_in, 16 * MROWS * g)
                    nc.vector.tensor_copy(mt[:], misc[0:2 * HG * TB, 0:P // 2].bitcast(BF16)).then_inc(mt_ok, 1)
                nc.vector.memset(mparts[:], 0.0).then_inc(zeros_ok, 1)
                dve.wait_ge(zeros_ok, 1)
                for v in range(NG // NB):
                    maxima(0, v)
                with dve.Fori(1, NB) as b:
                    for v in range(NG // NB):
                        maxima(b, v)

            @block.scalar
            def _(act):
                def copy_sums(g, half):
                    act.wait_ge(pv_ok, 2 * TB * g + TB * (half + 1))
                    after(act, otT_ok, 2 * g + half)
                    nc.scalar.copy(ot[:], po[:]).then_inc(ot_ok, 1)

                oa_v = oa[:].rearrange("p (b s i) (g h) v -> p b s g i h v", i=CT, s=2, h=HG)

                def keep_rows(b, v, half):
                    act.wait_ge(otT_ok, 2 * (NG // NB * b + v) + half + 1)
                    nc.scalar.copy(oa_v[:, b, half, v],
                                   misc[:].rearrange("p (i h v) -> p i h v", h=HG, v=VW)[:, :, :, 0:D + 1]).then_inc(oa_ok, 1)

                def exps(b, v, before=None):
                    g, u = NG // NB * b + v, v % 2
                    for n in range(XS):
                        k = n // HG
                        act.wait_ge(s2_ok, g * XS + n + 1)
                        if n % HG == 0:
                            after(act, pv_ok, freed(g, u, k, 2 * TB))
                        nc.scalar.activation(pr[:, turn(u, k, 2 * TB), n % HG], s2[:, turn(u, n, XS)], ACT.Exp).then_inc(exp_ok, 1)
                        if n == 3 and before:
                            copy_sums(g - 1, 1)
                        if n == 16 and before:
                            keep_rows(*before, 1)
                        if n == 36:
                            copy_sums(g, 0)
                        if n == 48:
                            keep_rows(b, v, 0)
                final = NG // NB - 1
                exps(0, 0)
                for v in range(1, final + 1):
                    exps(0, v, (0, v - 1))
                with act.Fori(1, NB) as b:
                    exps(b, 0, (b - 1, final))
                    for v in range(1, final + 1):
                        exps(b, v, (b, v - 1))
                copy_sums(NG - 1, 1)
                keep_rows(NB - 1, final, 1)


def route(nc, c, dr, logits, dst, gates, table, zero, zero_out):
    I32 = mybir.dt.int32
    with ExitStack() as ctx:
        def sb(name, shape, dt=F32):
            return ctx.enter_context(nc.sbuf_tensor("r_" + name, shape, dt))

        def sem(name):
            return ctx.enter_context(nc.semaphore("r_" + name))
        KMAX = T // TS
        iota_e = sb("iota_e", [P, X])
        iota_k = sb("iota_k", [P, KMAX])
        iota_s = sb("iota_s", [1, NS])
        iota_i = sb("iota_i", [P, NS], I32)
        tri = sb("tri", [P, P], BF16)
        ones = sb("ones", [P, P], BF16)
        m = sb("m", [P, 2, NT])
        eq = sb("eq", [P, NT, X])
        cand = sb("cand", [P, NT, X])
        first = sb("first", [P, 2, NT])
        hot = sb("hot", [P, 2, NT, X])
        rest = sb("rest", [P, NT, X])
        gap = sb("gap", [P, NT])
        eg = sb("eg", [P, NT])
        sg = sb("sg", [P, NT])
        chosen = sb("chosen", [P, NT, X], BF16)
        total = sb("total", [P, NT, X])
        scan = sb("scan", [P, 2, NT, X])
        over = sb("over", [P, X, KMAX])
        slots = sb("slots", [P, X])
        ends = sb("ends", [P, 2, X])
        start = sb("start", [P, X])
        place = sb("place", [P, NT, X])
        pick = sb("pick", [P, 2, NT, X])
        where = sb("where", [P, 2, NT])
        past = sb("past", [1, NS, X])
        tab = sb("tab", [1, NS])
        pc = ctx.enter_context(nc.psum_tensor("r_pc", [P, NT * X], F32))
        pt = ctx.enter_context(nc.psum_tensor("r_pt", [P, NT * X], F32))
        made, chain, gap_ok, eg_ok, chosen_ok, count_ok, dst_ok = (
            sem("made"), sem("chain"), sem("gap_ok"), sem("eg_ok"), sem("chosen_ok"), sem("count_ok"), sem("dst_ok"))
        CONST = 7

        def over_x(a):
            return a.rearrange("p (n o) -> p n o", o=1).broadcast_to([P, NT, X])

        def over_n(a):
            return a.rearrange("p (o e) -> p o e", o=1).broadcast_to([P, NT, X])

        with nc.Block() as block:
            @block.sync
            def _(sp):
                sp.wait_ge(made, CONST)
                v = dr["xs"].rearrange("(z p r) e -> z p (r e)", p=P, r=6)
                for i in range(N_ZERO):
                    sp.dma_start(v[i], zero[:]).then_inc(zero_out, 16)

            @block.gpsimd
            def _(pool):
                count = [0]

                def then(ins):
                    count[0] += 1
                    ins.then_inc(made, 1)
                    pool.wait_ge(made, count[0])
                then(nc.gpsimd.iota(iota_i[:], [[1, NS]], base=0, channel_multiplier=0))
                nc.gpsimd.memset(tri[:], 1.0).then_inc(made, 1)
                nc.gpsimd.memset(ones[:], 1.0).then_inc(made, 1)
                count[0] += 2
                then(nc.gpsimd.memset(zero[:], 0.0))
                then(nc.gpsimd.affine_select(out=tri[:], in_=tri[:], compare_op=ALU.is_gt, fill=0.0, base=0,
                                             pattern=[[1, P]], channel_multiplier=-1))
                then(nc.gpsimd.tensor_copy(iota_s[:], iota_i[0:1, :]))
                then(nc.gpsimd.tensor_copy(iota_e[:], iota_i[:, 0:X]))

            @block.vector
            def _(dve):
                count = [0]

                def then(ins):
                    count[0] += 1
                    ins.then_inc(chain, 1)
                    dve.wait_ge(chain, count[0])
                dve.wait_ge(made, CONST)
                then(nc.vector.tensor_scalar(iota_k[:], iota_i[:, 0:KMAX], float(TS), None, ALU.mult))
                for k, src in ((0, logits), (1, rest)):
                    then(nc.vector.tensor_reduce(m[:, k, :], src[:], AX.X, ALU.max))
                    then(nc.vector.tensor_tensor(eq[:], src[:], over_x(m[:, k, :]), ALU.is_equal))
                    then(nc.vector.scalar_tensor_tensor(out=cand[:], in0=eq[:], scalar=-float(X), in1=over_n(iota_e[:]),
                                                        op0=ALU.mult, op1=ALU.add))
                    then(nc.vector.tensor_reduce(first[:, k, :], cand[:], AX.X, ALU.min))
                    then(nc.vector.tensor_scalar_add(first[:, k, :], first[:, k, :], float(X)))
                    then(nc.vector.tensor_tensor(hot[:, k], over_n(iota_e[:]), over_x(first[:, k, :]), ALU.is_equal))
                    if k == 0:
                        then(nc.vector.scalar_tensor_tensor(out=rest[:], in0=hot[:, 0], scalar=FAR, in1=logits[:],
                                                            op0=ALU.mult, op1=ALU.add))
                nc.vector.tensor_tensor(chosen[:], hot[:, 0], hot[:, 1], ALU.add).then_inc(chosen_ok, 1)
                nc.vector.tensor_tensor(gap[:], m[:, 1, :], m[:, 0, :], ALU.subtract).then_inc(gap_ok, 1)
                dve.wait_ge(eg_ok, 1)
                then(nc.vector.tensor_scalar_add(sg[:], eg[:], 1.0))
                then(nc.vector.reciprocal(gates[:, :, 0], sg[:]))
                then(nc.vector.tensor_tensor(gates[:, :, 1], eg[:], gates[:, :, 0], ALU.mult))
                dve.wait_ge(count_ok, 1)
                nc.vector.tensor_copy(total[:], pt[:].rearrange("p (n e) -> p n e", e=X))
                then(nc.vector.tensor_copy(scan[:, 0], pt[:].rearrange("p (n e) -> p n e", e=X)))
                a, step = 0, 1
                while step < NT:
                    then(nc.vector.tensor_copy(scan[:, 1 - a, 0:step, :], scan[:, a, 0:step, :]))
                    then(nc.vector.tensor_tensor(scan[:, 1 - a, step:, :], scan[:, a, step:, :], scan[:, a, 0:NT - step, :], ALU.add))
                    a, step = 1 - a, 2 * step
                then(nc.vector.tensor_tensor(over[:], scan[:, a, NT - 1, :].rearrange("p (e o) -> p e o", o=1).broadcast_to([P, X, KMAX]),
                                             iota_k[:].rearrange("p (o k) -> p o k", o=1).broadcast_to([P, X, KMAX]), ALU.is_gt))
                then(nc.vector.tensor_reduce(slots[:], over[:], AX.X, ALU.add))
                then(nc.vector.tensor_copy(ends[:, 0, :], slots[:]))
                b, step = 0, 1
                while step < X:
                    then(nc.vector.tensor_copy(ends[:, 1 - b, 0:step], ends[:, b, 0:step]))
                    then(nc.vector.tensor_tensor(ends[:, 1 - b, step:], ends[:, b, step:], ends[:, b, 0:X - step], ALU.add))
                    b, step = 1 - b, 2 * step
                then(nc.vector.tensor_tensor(start[:], ends[:, b, :], slots[:], ALU.subtract))
                then(nc.vector.tensor_scalar(start[:], start[:], float(TS), None, ALU.mult))
                then(nc.vector.tensor_tensor(place[:], scan[:, a], total[:], ALU.subtract))
                then(nc.vector.tensor_tensor(place[:], place[:], pc[:].rearrange("p (n e) -> p n e", e=X), ALU.add))
                then(nc.vector.tensor_tensor(place[:], place[:], over_n(start[:]), ALU.add))
                for k in range(2):
                    then(nc.vector.tensor_tensor(pick[:, k], hot[:, k], place[:], ALU.mult))
                    then(nc.vector.tensor_reduce(where[:, k, :], pick[:, k], AX.X, ALU.add))
                then(nc.vector.tensor_tensor(past[:], iota_s[:].rearrange("p (s o) -> p s o", o=1).broadcast_to([1, NS, X]),
                                             ends[0:1, b, :].rearrange("p (o e) -> p o e", o=1).broadcast_to([1, NS, X]), ALU.is_ge))
                then(nc.vector.tensor_reduce(tab[:], past[:], AX.X, ALU.add))
                then(nc.vector.tensor_scalar_min(tab[:], tab[:], float(X - 1)))
                then(nc.vector.tensor_copy(table[:], tab[:]))
                nc.vector.tensor_copy(dst[:], where[:].rearrange("p k n -> p n k")).then_inc(dst_ok, 1)

            @block.scalar
            def _(act):
                act.wait_ge(gap_ok, 1)
                nc.scalar.activation(eg[:], gap[:], ACT.Exp).then_inc(eg_ok, 1)

            @block.tensor
            def _(pe):
                pe.wait_ge(made, CONST)
                pe.wait_ge(chosen_ok, 1)
                nc.tensor.matmul(pc[:], tri[:], chosen[:].rearrange("p n e -> p (n e)"), start=True, stop=True)
                nc.tensor.matmul(pt[:], ones[:], chosen[:].rearrange("p n e -> p (n e)"), start=True, stop=True).then_inc(count_ok, 1)


def finish_and_experts(nc, c, dr, x, Wo, bo, rel_v, band, neg, oa, w1, w3, w2, table):
    with ExitStack() as ctx:
        def sb(name, shape, dt=F32):
            return ctx.enter_context(nc.sbuf_tensor("e_" + name, shape, dt))

        def ps(name, shape, dt=F32):
            return ctx.enter_context(nc.psum_tensor("e_" + name, shape, dt))

        def sem(name):
            return ctx.enter_context(nc.semaphore("e_" + name))

        def sems(name):
            return [sem(f"{name}{i}") for i in range(2)]
        ST = TS // P
        LAG = 2
        PA = 3
        w1s = sb("w1s", [P, 2, KC, F])
        w3s = sb("w3s", [P, 2, KC, F])
        w2s = sb("w2s", [P, 2, FC, E])
        xr = sb("xr", [P, 2, ST, E])
        xT = sb("xT", [P, 2, KC, TS])
        sg = sb("sg", [P, 2, TS])
        hT = sb("hT", [P, 2, FC, TS])
        y = sb("y", [P, 2, ST, E])
        px = ps("px", [P, KC, TS])
        pa = ps("pa", [P, PA, 2, TS])
        py = ps("py", [P, ST, CH])
        w_in, x_in, y_out = sems("w_in"), sems("x_in"), sems("y_out")
        xt_ps, xt_ok, a_ok, g_ok, h_ok, y_ps, y_ok = (
            sem("xt_ps"), sem("xt_ok"), sem("a_ok"), sem("g_ok"), sem("h_ok"), sem("y_ps"), sem("y_ok"))
        xs = dr["xs"].rearrange("(s i p) e -> s p i e", p=P, i=ST)
        ys = dr["ys"].rearrange("(s i p) e -> s p i e", p=P, i=ST)

        M0 = P // H
        R1 = (NM - M0) * H
        TSLOTS = NT // 2
        HF = FC // 2
        wo = sb("wo", [P, KC, E])
        bob = sb("bob", [P, E])
        rv = sb("rv", [P, 2, D])
        pick = sb("pick", [P, H, M0])
        hsel = sb("hsel", [P, H])
        rvm = sb("rvm", [P, 2, H, D])
        vs = sb("vs", [P, 2, NM, E])
        xt = sb("xt", [P, 2, E])
        xb = sb("xb", [P, 2, E])
        bs = sb("bs", [P, 2, NM * H])
        e = sb("e", [P, 2, 2, NM * H])
        prod = sb("prod", [P, 2, NM, E])
        eT0 = sb("eT0", [P, 2, P])
        eT1 = sb("eT1", [R1, 2, P])
        es = sb("es", [P, H])
        z = sb("z", [P, H])
        rz = sb("rz", [P, H])
        o1 = sb("o1", [P, E])
        o2 = sb("o2", [P, E])
        o3 = sb("o3", [P, E])
        on = sb("on", [P, 2, E])
        onT = sb("onT", [P, 2, KC, P])
        pcol = ps("pcol", [P, 2, E])
        prow = ps("prow", [P, 2, E])
        c_in, set_ok, v_in = sem("c_in"), sem("set_ok"), sems("v_in")
        bs_ok, e_ok, prod_ok, et_ps_ok, et_ok, rv_ok = (
            sem("bs_ok"), sem("e_ok"), sem("prod_ok"), sem("et_ps_ok"), sem("et_ok"), sem("rv_ok"))
        chain, on_ok, on_ps_ok, ont_ok, att_ok, res_ok = (
            sem("chain"), sem("on_ok"), sem("on_ps_ok"), sem("ont_ok"), sem("att_ok"), sem("res_ok"))
        x_v = x.rearrange("(n p) e -> n p e", p=P)
        res = oa[:].rearrange("p n h v -> p n (h v)")[:, :, 0:E]

        def windows(n):
            v = dr["v"][0:T, :].rearrange("(n p) e -> n p e", p=P)[n]
            return bass.AP(v.tensor, v.offset, [[E, P], [1, NM * E]])

        def slots(eng, body):
            for s in (0, 1, 2):
                body(s, s % 2, s // 2)
            with eng.Fori(1, TSLOTS // 2 - 1) as r:
                body(2 * r + 1, 1, r)
                body(2 * r + 2, 0, r + 1)
            for s in (TSLOTS - 1, TSLOTS):
                body(s, s % 2, s // 2)
            with eng.Fori(TSLOTS // 2, (NS - 3) // 2) as r:
                body(2 * r + 1, 1, r, tiles=False)
                body(2 * r + 2, 0, r + 1, tiles=False)
            for s in (NS - 2, NS - 1):
                body(s, s % 2, s // 2, tiles=False)

        def stages(f, s, tiles, table):
            if tiles:
                j = f // HF
                for stage, behind in table.get(f % HF, ()):
                    t = 2 * s + j - behind
                    if not isinstance(t, int) or 0 <= t < NT:
                        stage(t, (j - behind) % 2)

        with nc.Block() as block:
            @block.sync
            def _(sp):
                def load(s, u):
                    ex = sp.value_load(table[0:1, bass.ds(s, 1)], min_val=0, max_val=X - 1)
                    sp.dma_start(xr[:, u], xs[s]).then_inc(x_in[u], 16)
                    sp.dma_start(w1s[:, u], w1[ex].rearrange("(k p) f -> p k f", p=P)).then_inc(w_in[u], 16)
                    sp.dma_start(w3s[:, u], w3[ex].rearrange("(k p) f -> p k f", p=P)).then_inc(w_in[u], 16)
                    sp.dma_start(w2s[:, u], w2[ex].rearrange("(k p) f -> p k f", p=P)).then_inc(w_in[u], 16)

                def load_tile(t, u):
                    sp.dma_start(vs[:, u].rearrange("p m e -> p (m e)"), windows(t)).then_inc(v_in[u], 16)
                    sp.dma_start(xt[:, u, :], x_v[t]).then_inc(v_in[u], 16)

                def slot(s, u, k, tiles=True):
                    if not isinstance(s, int) or 0 < s < NS - 1:
                        sp.wait_ge(y_ps, s)
                        load(s + 1, 1 - u)
                    if tiles and not (isinstance(s, int) and s >= TSLOTS - 1):
                        for i in range(2):
                            sp.wait_ge(prod_ok, 2 * s + i + 1)
                            load_tile(2 * s + 2 + i, i)
                load(0, 0)
                load_tile(0, 0)
                load_tile(1, 1)
                sp.dma_start(wo[:], Wo.rearrange("(k p) e -> p k e", p=P)).then_inc(c_in, 16)
                sp.dma_start(bob[:], bo.rearrange("(o e) -> o e", o=1).broadcast_to([P, E])).then_inc(c_in, 16)
                for m in range(NM):
                    r = m % M0 * H
                    sp.dma_start(rv[r:r + H, m // M0, :], rel_v[0, m:m + 1, :].broadcast_to([H, D])).then_inc(c_in, 16)
                load(1, 1)
                slots(sp, slot)

            @block.gpsimd
            def _(pool):
                def put(s, u, k):
                    pool.wait_ge(y_ok, s + 1)
                    pool.dma_start(ys[s], y[:, u]).then_inc(y_out[u], 16)

                def products(t, u, su, k):
                    pool.wait_ge(v_in[u], 32 * (k + 1))
                    if u == 0:
                        after(pool, res_ok, t - 1)
                    else:
                        after(pool, res_ok, t - 2 + 1)
                    nc.gpsimd.tensor_tensor(xb[:, u, :], xt[:, u, :], bob[:], ALU.add)
                    after(pool, on_ok, t - 1)
                    nc.gpsimd.tensor_tensor(
                        prod[:, u].rearrange("p m (h d) -> p (m h) d", d=D),
                        vs[:, u].rearrange("p m (h d) -> p (m h) d", d=D),
                        e[:, su, u, :].rearrange("p (q o) -> p q o", o=1).broadcast_to([P, NM * H, D]),
                        ALU.mult).then_inc(prod_ok, 1)

                def slot(s, u, k, tiles=True):
                    tiles = tiles and not (isinstance(s, int) and s >= TSLOTS)
                    if tiles:
                        pool.wait_ge(e_ok, s + 1)
                        products(2 * s, 0, u, s)
                    if not isinstance(s, int) or s > 0:
                        put(s - 1, 1 - u, k)
                    if tiles:
                        products(2 * s + 1, 1, u, s)
                nc.gpsimd.memset(pick[:], 0.0).then_inc(set_ok, 1)
                pool.wait_ge(set_ok, 1)
                nc.gpsimd.affine_select(out=pick[:], in_=pick[:], compare_op=ALU.not_equal, fill=1.0, base=0,
                                        pattern=[[-1, H], [-H, M0]], channel_multiplier=1).then_inc(set_ok, 1)
                pool.wait_ge(c_in, 16 * (2 + NM))
                slots(pool, slot)
                put(NS - 1, (NS - 1) % 2, 0)
                pool.wait_ge(y_out[0], 16 * ((NS + 1) // 2))
                pool.wait_ge(y_out[1], 16 * (NS // 2))

            @block.tensor
            def _(pe):
                def columns(s, u, k):
                    pe.wait_ge(x_in[u], 16 * (k + 1))
                    after(pe, xt_ok, s)
                    for j in range(KC):
                        for i in range(ST):
                            last = nc.tensor.transpose(px[:, j, i * P:(i + 1) * P], xr[:, u, i, j * P:(j + 1) * P], c["ident"][:])
                    last.then_inc(xt_ps, 1)

                def hidden(s, u, f):
                    before = f - PA if f >= PA else max(g for g in range(FC) if g % PA == f % PA) - FC
                    after(pe, h_ok, s * FC + before + 1)
                    for j, w in enumerate((w1s, w3s)):
                        for k in range(KC):
                            last = nc.tensor.matmul(pa[:, f % PA, j, :], w[:, u, k, f * P:(f + 1) * P], xT[:, u, k, :],
                                                    start=(k == 0), stop=(k == KC - 1))
                    last.then_inc(a_ok, 1)

                def outputs(s, u, f):
                    pe.wait_ge(h_ok, s * FC + f + 1)
                    if f == 0:
                        after(pe, y_ok, s)
                    for i in range(ST):
                        last = nc.tensor.matmul(py[:, i, 0:E], hT[:, u, f, i * P:(i + 1) * P], w2s[:, u, f, :],
                                                start=(f == 0), stop=(f == FC - 1))
                    if f == FC - 1:
                        last.then_inc(y_ps, 1)

                def exp_columns(t, j, s, u):
                    pe.wait_ge(e_ok, s + 1)
                    after(pe, ont_ok, t - 1)
                    nc.tensor.transpose(pcol[:, 0, 0:P], e[:, u, j, 0:P], c["ident"][:])
                    nc.tensor.transpose(pcol[0:R1, 0, P:2 * P], e[:, u, j, P:P + R1], c["ident"][:]).then_inc(et_ps_ok, 1)

                def relative(t, j):
                    pe.wait_ge(et_ok, t + 1)
                    after(pe, on_ok, t)
                    after(pe, res_ok, t - 1)
                    nc.tensor.matmul(prow[:, 0, :], eT0[:, j, :], rvm[:, 0].rearrange("p h d -> p (h d)"), start=True, stop=False)
                    nc.tensor.matmul(prow[:, 0, :], eT1[:, j, :], rvm[0:R1, 1].rearrange("p h d -> p (h d)"),
                                     start=False, stop=True).then_inc(rv_ok, 1)

                def row_columns(t, j):
                    pe.wait_ge(on_ok, t + 1)
                    after(pe, et_ok, min(t + 2, NT) if isinstance(t, int) else t + 2)
                    for k in range(KC):
                        last = nc.tensor.transpose(pcol[:, 1, k * P:(k + 1) * P], on[:, j, k * P:(k + 1) * P], c["ident"][:])
                    last.then_inc(on_ps_ok, 1)

                def project(t, j):
                    pe.wait_ge(ont_ok, t + 1)
                    for k in range(KC):
                        last = nc.tensor.matmul(prow[:, 1, :], onT[:, j, k, :], wo[:, k, :], start=(k == 0), stop=(k == KC - 1))
                    last.then_inc(att_ok, 1)

                def slot(s, u, k, tiles=True):
                    first, final = isinstance(s, int) and s == 0, isinstance(s, int) and s == NS - 1
                    if first:
                        columns(0, 0, 0)
                    pe.wait_ge(xt_ok, s + 1)
                    pe.wait_ge(w_in[u], 48 * (k + 1))
                    for f in range(FC):
                        hidden(s, u, f)
                        if f >= LAG:
                            outputs(s, u, f - LAG)
                        elif not first:
                            outputs(s - 1, 1 - u, FC - LAG + f)
                        if f == FC - 3 and not final:
                            columns(s + 1, 1 - u, k + u)
                        stages(f, s, tiles, {0: [(row_columns, 2)], 1: [(relative, 1)],
                                             2: [(project, 2), (lambda t, j: exp_columns(t, j, s, u), 0)]})
                    if final:
                        for f in range(FC - LAG, FC):
                            outputs(s, u, f)
                pe.wait_ge(c_in, 16 * (2 + NM))
                pe.wait_ge(chain, 2)
                slots(pe, slot)

            @block.scalar
            def _(act):
                def keep_columns(s, u):
                    act.wait_ge(xt_ps, s + 1)
                    nc.scalar.copy(xT[:, u], px[:]).then_inc(xt_ok, 1)

                def keep_outputs(s, u, k):
                    act.wait_ge(y_ps, s + 1)
                    after(act, y_out[u], 16 * k)
                    nc.scalar.copy(y[:, u], py[:, :, 0:E]).then_inc(y_ok, 1)

                def exps(s, u):
                    act.wait_ge(bs_ok, s + 1)
                    nc.scalar.activation(e[:, u], bs[:], ACT.Exp).then_inc(e_ok, 1)

                def keep_exp_columns(t, j):
                    act.wait_ge(et_ps_ok, t + 1)
                    nc.scalar.copy(eT0[:, j, :], pcol[:, 0, 0:P])
                    nc.scalar.copy(eT1[:, j, :], pcol[0:R1, 0, P:2 * P]).then_inc(et_ok, 1)

                def keep_row_columns(t, j):
                    act.wait_ge(on_ps_ok, t + 1)
                    nc.scalar.copy(onT[:, j], pcol[:, 1, :].rearrange("p (k t) -> p k t", k=KC)).then_inc(ont_ok, 1)

                def slot(s, u, k, tiles=True):
                    first, final = isinstance(s, int) and s == 0, isinstance(s, int) and s == NS - 1
                    if first:
                        keep_columns(0, 0)
                    for f in range(FC):
                        act.wait_ge(a_ok, s * FC + f + 1)
                        after(act, h_ok, s * FC + f - 1)
                        nc.scalar.activation(sg[:, f % 2, :], pa[:, f % PA, 0, :], ACT.Silu).then_inc(g_ok, 1)
                        if f == 0 and tiles and not (isinstance(s, int) and s >= TSLOTS):
                            exps(s, u)
                        if f == LAG - 1 and not first:
                            keep_outputs(s - 1, 1 - u, k if u else k - 1)
                        if f == FC - 2 and not final:
                            keep_columns(s + 1, 1 - u)
                        stages(f, s, tiles, {1: [(keep_row_columns, 2)], 3: [(keep_exp_columns, 0)]})
                    if final:
                        keep_outputs(s, u, k)
                slots(act, slot)

            @block.vector
            def _(dve):
                BASE, STEPS = 2, 7

                def shifted(s):
                    after(dve, e_ok, s)
                    for i in range(2):
                        last = nc.vector.tensor_tensor(
                            bs[:, i, :].rearrange("p (m h) -> p m h", h=H), band[:, 2 * s + i],
                            neg[:, 2 * s + i].rearrange("p (o h) -> p o h", o=1).broadcast_to([P, NM, H]), ALU.add)
                    last.then_inc(bs_ok, 1)

                def link(ins):
                    ins.then_inc(chain, 1)

                def linked(t, k):
                    dve.wait_ge(chain, t * STEPS + BASE + k)

                def totals(t, j, u):
                    dve.wait_ge(prod_ok, t + 1)
                    link(nc.vector.tensor_reduce(es[:], e[:, u, j, :].rearrange("p (m h) -> p h m", h=H), AX.X, ALU.add))
                    linked(t, 1)
                    link(nc.vector.tensor_tensor(z[:], es[:], oa[:, t, :, D], ALU.add))
                    linked(t, 2)
                    link(nc.vector.reciprocal(rz[:], z[:]))

                def window_sum(t, j, part):
                    cols = slice(part * P, (part + 1) * P)
                    link(nc.vector.tensor_reduce(o1[:, cols], prod[:, j, :, cols].rearrange("p m e -> p e m"), AX.X, ALU.add))

                def rows(t, j):
                    linked(t, 5)
                    link(nc.vector.tensor_tensor(o2[:].rearrange("p (h d) -> p h d", d=D), o1[:].rearrange("p (h d) -> p h d", d=D),
                                                 oa[:, t, :, 0:D], ALU.add))
                    dve.wait_ge(rv_ok, t + 1)
                    after(dve, att_ok, t)
                    linked(t, 6)
                    link(nc.vector.tensor_tensor(o3[:], o2[:], prow[:, 0, :], ALU.add))
                    linked(t, 7)
                    after(dve, on_ps_ok, t - 1)
                    nc.vector.tensor_tensor(on[:, j, :].rearrange("p (h d) -> p h d", d=D),
                                            o3[:].rearrange("p (h d) -> p h d", d=D),
                                            rz[:].rearrange("p (h o) -> p h o", o=1).broadcast_to([P, H, D]),
                                            ALU.mult).then_inc(on_ok, 1)

                def result(t, j):
                    dve.wait_ge(att_ok, t + 1)
                    nc.vector.tensor_tensor(res[:, t, :], prow[:, 1, :], xb[:, j, :], ALU.add).then_inc(res_ok, 1)

                def slot(s, u, k, tiles=True):
                    after(dve, y_ps, s - 1)
                    for f in range(FC):
                        dve.wait_ge(g_ok, s * FC + f + 1)
                        nc.vector.tensor_tensor(hT[:, u, f, :], sg[:, f % 2, :], pa[:, f % PA, 1, :], ALU.mult).then_inc(h_ok, 1)
                        stages(f, s, tiles, {
                            0: [(lambda t, j: totals(t, j, u if j == 0 else 1 - u), 1)],
                            1: [(lambda t, j: window_sum(t, j, 0), 1)],
                            2: [(lambda t, j: window_sum(t, j, 1), 1)],
                            3: [(result, 2), (rows, 1)]})
                        if f == FC - 1 and tiles and not (isinstance(s, int) and s >= TSLOTS - 1):
                            shifted(s + 1)
                dve.wait_ge(set_ok, 2)
                nc.vector.tensor_reduce(hsel[:], pick[:], AX.X, ALU.add).then_inc(chain, 1)
                dve.wait_ge(chain, 1)
                dve.wait_ge(c_in, 16 * (2 + NM))
                for k, rows_in in ((0, P), (1, R1)):
                    last = nc.vector.tensor_tensor(
                        rvm[0:rows_in, k], rv[0:rows_in, k, :].rearrange("p (o d) -> p o d", o=1).broadcast_to([rows_in, H, D]),
                        hsel[0:rows_in, :].rearrange("p (h o) -> p h o", o=1).broadcast_to([rows_in, H, D]), ALU.mult)
                last.then_inc(chain, 1)
                shifted(0)
                slots(dve, slot)


def combine(nc, c, dr, dst, gates, res, out):
    I32 = mybir.dt.int32
    with ExitStack() as ctx:
        def sb(name, shape, dt=F32):
            return ctx.enter_context(nc.sbuf_tensor("c_" + name, shape, dt))

        def sem(name):
            return ctx.enter_context(nc.semaphore("c_" + name))
        BUF = 4
        y = sb("y", [P, BUF, 2, E])
        half = sb("half", [P, BUF, E])
        o = sb("o", [P, BUF, E])
        y_in, part_ok, o_ok, o_out = (
            [sem(f"y_in{i}") for i in range(BUF)], sem("part_ok"), sem("o_ok"), [sem(f"o_out{i}") for i in range(BUF)])
        out_v = out.rearrange("(n p) e -> n p e", p=P)
        with nc.Block() as block:
            @block.gpsimd
            def _(pool):
                for t in range(NT):
                    u = t % BUF
                    after(pool, o_ok, t - BUF + 1)
                    for k in range(2):
                        nc.gpsimd.indirect_dma_start(
                            out=y[:, u, k, :], out_offset=None, in_=dr["ys"],
                            in_offset=bass.IndirectOffsetOnAxis(ap=dst[:, t, k:k + 1], axis=0)).then_inc(y_in[u], 16)

            @block.vector
            def _(dve):
                with dve.Fori(0, NT // BUF) as r:
                    for u in range(BUF):
                        t = BUF * r + u
                        dve.wait_ge(y_in[u], 32 * r + 32)
                        dve.wait_ge(o_out[u], 16 * r)
                        nc.vector.scalar_tensor_tensor(out=half[:, u, :], in0=y[:, u, 0, :], scalar=gates[:, t, 0:1],
                                                       in1=res[:, t, :], op0=ALU.mult, op1=ALU.add).then_inc(part_ok, 1)
                        dve.wait_ge(part_ok, t + 1)
                        nc.vector.scalar_tensor_tensor(out=o[:, u, :], in0=y[:, u, 1, :], scalar=gates[:, t, 1:2],
                                                       in1=half[:, u, :], op0=ALU.mult, op1=ALU.add).then_inc(o_ok, 1)

            @block.sync
            def _(sp):
                with sp.Fori(0, NT // BUF) as r:
                    for u in range(BUF):
                        t = BUF * r + u
                        sp.wait_ge(o_ok, t + 1)
                        sp.dma_start(out_v[t], o[:, u, :]).then_inc(o_out[u], 16)
                for u in range(BUF):
                    sp.wait_ge(o_out[u], 16 * NT // BUF)


def constants(nc, c):
    with ExitStack() as ctx:
        made = ctx.enter_context(nc.semaphore("const_made"))
        with nc.Block() as block:
            @block.gpsimd
            def _(pool):
                count = [0]

                def then(ins):
                    count[0] += 1
                    ins.then_inc(made, 1)
                    pool.wait_ge(made, count[0])
                for m in (c["ident"], c["ident16"]):
                    then(nc.gpsimd.memset(m[:], 0.0))
                    then(nc.gpsimd.affine_select(out=m[:], in_=m[:], compare_op=ALU.not_equal, fill=1.0, base=0,
                                                 pattern=[[-1, P]], channel_multiplier=1))
                then(nc.gpsimd.memset(c["far"][:], FAR))
                then(nc.gpsimd.affine_select(out=c["far"][:], in_=c["far"][:], compare_op=ALU.is_ge, fill=0.0, base=0,
                                             pattern=[[1, BW]], channel_multiplier=-1))
                then(nc.gpsimd.affine_select(out=c["far"][:], in_=c["far"][:], compare_op=ALU.is_ge, fill=0.0, base=2 * W,
                                             pattern=[[-1, BW]], channel_multiplier=1))
                then(nc.gpsimd.memset(c["edge"][:], 0.0))
                first = c["edge"][:].rearrange("p (b i) m -> p b i m", i=TB)[:, :, 0, :]
                final = c["edge"][:].rearrange("p (b i) m -> p b i m", i=TB)[:, :, TB - 1, :]
                then(nc.gpsimd.affine_select(out=first, in_=first, compare_op=ALU.is_ge, fill=FAR, base=-W,
                                             pattern=[[0, NB], [1, NM]], channel_multiplier=1))
                then(nc.gpsimd.affine_select(out=final, in_=final, compare_op=ALU.is_ge, fill=FAR, base=P - 1 + W,
                                             pattern=[[0, NB], [-1, NM]], channel_multiplier=-1))


def build(nc, x, Wq, bq, Wk, bk, Wv, bv, Wo, bo, rel_k, rel_v, gate_w, gate_b, w1, w3, w2, out, stages=9):
    with ExitStack() as ctx:
        def sb(name, shape, dt=F32):
            return ctx.enter_context(nc.sbuf_tensor(name, shape, dt))
        c = dict(ident=sb("ident", [P, P]), ident16=sb("ident16", [P, P], BF16), far=sb("far", [P, BW], BF16),
                 edge=sb("edge", [P, NT, NM]))
        nc.disable_value_cache = True
        x = x.rearrange("b l e -> (b l) e")
        out = out.rearrange("b l e -> (b l) e")
        dr = scratch(nc)
        band = sb("band", [P, NT, NM, H])
        neg = sb("neg", [P, NT, H])
        oa = sb("oa", [P, NT, H, D + 1])
        dst = sb("dst", [P, NT, 2], mybir.dt.int32)
        gates = sb("gates", [P, NT, 2])
        table = sb("table", [1, NS], mybir.dt.int32)
        constants(nc, c)
        with ExitStack() as early:
            def sb_early(name, shape, dt=F32):
                return early.enter_context(nc.sbuf_tensor(name, shape, dt))
            bmax = sb_early("bmax", [P, NT, H])
            logits = sb_early("logits", [P, NT, X])
            norm_and_project(nc, c, dr, x, Wq, bq, Wk, bk, Wv, bv, rel_k, gate_w, gate_b, band, logits)
            if stages < 2: return
            zero = sb_early("zero", [P, 6 * E])
            zero_out = early.enter_context(nc.semaphore("zero_out"))
            route(nc, c, dr, logits, dst, gates, table, zero, zero_out)
            if stages == 2: return
            band_scores(nc, c, dr, band, bmax)
            attention(nc, c, dr, bmax, neg, oa, dst, zero_out)
            if stages < 4: return
        finish_and_experts(nc, c, dr, x, Wo, bo, rel_v, band, neg, oa, w1, w3, w2, table)
        combine(nc, c, dr, dst, gates, oa[:].rearrange("p n h v -> p n (h v)")[:, :, 0:E], out)


_INS = ['L0_attn_hidden_states', 'L0_attn_Wq', 'L0_attn_bq', 'L0_attn_Wk', 'L0_attn_bk', 'L0_attn_Wv', 'L0_attn_bv',
        'L0_attn_Wo', 'L0_attn_bo', 'L0_attn_emb_rel_k', 'L0_attn_emb_rel_v', 'L0_ffn_gate_w', 'L0_ffn_gate_b',
        'L0_ffn_w1', 'L0_ffn_w3', 'L0_ffn_w2']


def kernel(**inputs):
    import numpy as _np
    import concourse.bacc as _bacc
    from concourse.bass_utils import run_bass_kernel_spmd as _run

    nc = _bacc.Bacc("TRN2", target_bir_lowering=False, num_devices=1)
    arrays, args = {}, []
    for name in _INS:
        a = _np.ascontiguousarray(inputs[name])
        arrays[f"in_{name}_dram"] = a
        args.append(nc.dram_tensor(f"in_{name}_dram", a.shape, mybir.dt.from_np(a.dtype), kind="ExternalInput").ap())
    args.append(nc.dram_tensor("out_0_dram", (NB, L, E), F32, kind="ExternalOutput").ap())
    build(nc, *args)
    r = _run(nc, [arrays], core_ids=[0])
    return r.results[0]["out_0_dram"]
```

```python
import concourse.bass as bass
from concourse import mybir
from contextlib import ExitStack

F32 = mybir.dt.float32
BF16 = mybir.dt.bfloat16
F16 = mybir.dt.float16
ALU = mybir.AluOpType
ACT = mybir.ActivationFunctionType
AX = mybir.AxisListType

P = 128
NB, L, E = 4, 1024, 256
H, D = 16, 16
T = NB * L
NT = T // P
TB = L // P
KC = E // P
CH = 512
NC = T // CH
CT = CH // P
W = 4
NM = 2 * W + 1
HG = 4
NG = NB * H // HG
VW = 32
ROWS = 6 * D
MROWS = 2
BW = P + 2 * W
X = 8
F = 1024
FC = F // P
TS = 2 * P
NS = 2 * T // TS + X - 1
N_ZERO = NS * TS // P // 6
FAR = -1e30
EPS = 1e-5
Q_PLACES = ((0, 3, 1), (3, 6, 2), (4, 5, 1))
K_PLACES = ((2, 5, 1), (1, 6, 4), (0, 1, 1))


def after(eng, sem, value):
    if not (isinstance(value, int) and value <= 0):
        eng.wait_ge(sem, value)


def scratch(nc):
    def dram(name, shape, dt):
        return nc.dram_tensor(name, shape, dt, kind="Internal").ap()
    return dict(
        xn=dram("xn_rows", [T, E], F32),
        q=dram("q_rows", [T, E], F32),
        k=dram("k_rows", [W + T + W, E], F32),
        v=dram("v_rows", [W + T + W, E], F32),
        vx=dram("vx_rows", [T, H * VW], F32),
        sq=dram("q_stack", [NB, H // HG, HG, ROWS, L], BF16),
        sk=dram("k_stack", [NB, H // HG, HG, ROWS, L], BF16),
        xs=dram("slot_rows", [NS * TS, E], F32),
        ys=dram("slot_outputs", [NS * TS, E], F32),
    )


def norm_and_project(nc, c, dr, x, Wq, bq, Wk, bk, Wv, bv, rel_k, gate_w, gate_b, band, dst, gates, table, iota_e, slot_expert):
    with ExitStack() as ctx:
        def sb(name, shape, dt=F32):
            return ctx.enter_context(nc.sbuf_tensor("a_" + name, shape, dt))

        def ps(name, shape, dt=F32):
            return ctx.enter_context(nc.psum_tensor("a_" + name, shape, dt))

        def sem(name):
            return ctx.enter_context(nc.semaphore("a_" + name))

        w = {n: sb("w" + n, [P, KC, E]) for n in "qkv"}
        bcol = sb("bcol", [P, 2, KC])
        gw = sb("gw", [P, KC, X])
        gb = sb("gb", [P, X])
        bvb = sb("bvb", [P, E])
        relk = sb("relk", [P, NM])
        hmask = sb("hmask", [P, 8])
        rk = sb("rk", [P, NM, 8])
        zpad = sb("zpad", [W, E])
        xt = sb("xt", [P, CT, E])
        st = sb("st", [P, CT, 6])
        mv = sb("mv", [P, 3, CT])
        std = sb("std", [P, CT])
        rstd = sb("rstd", [P, CT])
        xn = sb("xn", [P, CT, E])
        xnT = sb("xnT", [P, 2, KC, CH])
        qkT = sb("qkT", [P, 2 * KC, CH])
        rest = sb("rest", [P, 2 * KC, CH])
        logits = sb("logits", [P, NT, X])
        part = [sb(f"part{i}", [P, 2 * KC, CH], BF16) for i in range(3)]
        vrow = sb("vrow", [P, CT, E])
        vx = sb("vx", [P, CT, H, VW])
        qrow = sb("qrow", [P, CT, E])
        krow = sb("krow", [P, CT, E])
        pT = ps("pT", [P, 2, CH])
        pqk = ps("pqk", [P, 2 * KC, CH])
        pv = ps("pv", [P, 2, CH])

        w_in, const_ok, x_in = sem("w_in"), sem("const_ok"), sem("x_in")
        dchain, var_ok, std_ok, xn_ok = sem("dchain"), sem("var_ok"), sem("std_ok"), sem("xn_ok")
        tp_ok, xnT_ok, qk_ok, v_ok, qkT_ok = sem("tp_ok"), sem("xnT_ok"), sem("qk_ok"), sem("v_ok"), sem("qkT_ok")
        rows_ok, rel_ok, qrow_ok, krow_ok = sem("rows_ok"), sem("rel_ok"), sem("qrow_ok"), sem("krow_ok")
        v_out, rel_out, rest_ok, bias_ok = sem("v_out"), sem("rel_out"), sem("rest_ok"), sem("bias_ok")
        part_ok = [sem(f"part_ok{i}") for i in range(3)]
        st_xn, st_rows, st_v, st_pad = sem("st_xn"), sem("st_rows"), sem("st_v"), sem("st_pad")
        st_part = [sem(f"st_part{i}") for i in range(3)]

        x_v = x.rearrange("(n i p) e -> n p i e", p=P, i=CT)

        def rows_view(a, off=0):
            return a[off:off + T, :].rearrange("(n i p) e -> n p i e", p=P, i=CT)
        N_LOAD = 3 + 2 + 1 + 8 + 2
        RELW = NM * H
        RG = RELW + X

        def chunks(eng, body):
            body(0, 0, 0)
            body(1, 1, 0)
            with eng.Fori(1, NC // 2 - 1) as b:
                body(2 * b, 0, b)
                body(2 * b + 1, 1, b)
            body(NC - 2, 0, NC // 2 - 1)
            body(NC - 1, 1, NC // 2 - 1)

        with nc.Block() as block:
            @block.sync
            def _(sp):
                sp.dma_start(xt[:], x_v[0]).then_inc(x_in, 16)
                for n, src in (("q", Wq), ("k", Wk), ("v", Wv)):
                    sp.dma_start(w[n][:], src.rearrange("(k p) e -> p k e", p=P)).then_inc(w_in, 16)
                for i, src in enumerate((bq, bk)):
                    sp.dma_start(bcol[:, i, :], src.rearrange("(k p) -> p k", p=P),
                                 allow_slow_non_contiguous=True).then_inc(w_in, 16)
                sp.dma_start(bvb[:], bv.rearrange("(o e) -> o e", o=1).broadcast_to([P, E])).then_inc(w_in, 16)
                for h in range(8):
                    sp.dma_start(relk[h * D:(h + 1) * D, :], rel_k[0].rearrange("m d -> d m"),
                                 allow_slow_non_contiguous=True).then_inc(w_in, 16)
                sp.dma_start(gw[:], gate_w.rearrange("(k p) e -> p k e", p=P)).then_inc(w_in, 16)
                sp.dma_start(gb[:], gate_b.rearrange("(o e) -> o e", o=1).broadcast_to([P, X])).then_inc(w_in, 16)
                sp.wait_ge(const_ok, 1)
                for a in (dr["k"], dr["v"]):
                    for r in (0, W + T):
                        sp.dma_start(a[r:r + W, :], zpad[:]).then_inc(st_pad, 16)

                def put_xn(n):
                    sp.wait_ge(xn_ok, n + 1)
                    sp.dma_start(rows_view(dr["xn"])[n], xn[:]).then_inc(st_xn, 16)
                    if not isinstance(n, int) or n + 1 < NC:
                        sp.dma_start(xt[:], x_v[n + 1]).then_inc(x_in, 16)

                def put_part(n, b, u, p):
                    sp.wait_ge(part_ok[p], n + 1)
                    for a, (stack, (j0, j1, step)) in enumerate(((dr["sq"], Q_PLACES[p]), (dr["sk"], K_PLACES[p]))):
                        count = len(range(j0, j1, step))
                        for k in range(KC):
                            rows = stack[b, 2 * k:2 * k + 2, :, :, u * CH:(u + 1) * CH].rearrange(
                                "g h (d j) c -> (g h d) j c", j=6)
                            src = part[p][:, a * KC + k, :].rearrange("p (o c) -> p o c", o=1)
                            sp.dma_start(rows[:, j0:j1:step, :], src.broadcast_to([P, count, CH])).then_inc(st_part[p], 16)

                def chunk(n, u, b):
                    put_xn_next(n)
                    put_part(n, b, u, 0)
                    sp.wait_ge(v_out, n + 1)
                    sp.dma_start(rows_view(dr["v"], W)[n], vrow[:]).then_inc(st_v, 16)
                    sp.dma_start(rows_view(dr["vx"])[n], vx[:].rearrange("p i h v -> p i (h v)")).then_inc(st_v, 16)
                    sp.wait_ge(krow_ok, n + 1)
                    sp.dma_start(rows_view(dr["q"])[n], qrow[:]).then_inc(st_rows, 16)
                    sp.dma_start(rows_view(dr["k"], W)[n], krow[:]).then_inc(st_rows, 16)
                    put_part(n, b, u, 1)
                    put_part(n, b, u, 2)

                def put_xn_next(n):
                    if not isinstance(n, int) or n + 1 < NC:
                        put_xn(n + 1)
                put_xn(0)
                chunks(sp, chunk)
                sp.wait_ge(st_pad, 64)
                sp.wait_ge(st_xn, 16 * NC)
                sp.wait_ge(st_v, 32 * NC)
                sp.wait_ge(st_rows, 32 * NC)
                for p in range(3):
                    sp.wait_ge(st_part[p], 16 * 2 * KC * NC)

            @block.gpsimd
            def _(pool):
                nc.gpsimd.memset(zpad[:], 0.0).then_inc(const_ok, 1)
                nc.gpsimd.memset(vx[:], 0.0).then_inc(const_ok, 1)
                pool.wait_ge(const_ok, 2)
                nc.gpsimd.memset(vx[:, :, :, D:D + 1], 1.0).then_inc(const_ok, 1)
                nc.gpsimd.memset(hmask[:], 1.0).then_inc(const_ok, 1)
                pool.wait_ge(const_ok, 4)
                nc.gpsimd.affine_select(out=hmask[:], in_=hmask[:], compare_op=ALU.is_ge, fill=0.0, base=0,
                                        pattern=[[-D, 8]], channel_multiplier=1).then_inc(const_ok, 1)
                pool.wait_ge(const_ok, 5)
                nc.gpsimd.affine_select(out=hmask[:], in_=hmask[:], compare_op=ALU.is_ge, fill=0.0, base=D - 1,
                                        pattern=[[D, 8]], channel_multiplier=-1).then_inc(const_ok, 1)
                pool.wait_ge(const_ok, 6)
                pool.wait_ge(w_in, 16 * N_LOAD)
                nc.gpsimd.tensor_tensor(rk[:], relk[:].rearrange("p (m o) -> p m o", o=1).broadcast_to([P, NM, 8]),
                                        hmask[:].rearrange("p (o h) -> p o h", o=1).broadcast_to([P, NM, 8]),
                                        ALU.mult).then_inc(const_ok, 1)

            @block.vector
            def _(dve):
                def normed(n):
                    STEPS = 4

                    def link(ins, k):
                        ins.then_inc(dchain, 1)
                        dve.wait_ge(dchain, n * STEPS + k)
                    dve.wait_ge(x_in, 16 * (n + 1))
                    for i in range(CT - 1):
                        nc.vector.bn_stats(st[:, i, :], xt[:, i, :])
                    link(nc.vector.bn_stats(st[:, CT - 1, :], xt[:, CT - 1, :]), 1)
                    nc.vector.tensor_tensor(mv[:, 0, :], st[:, :, 1], st[:, :, 4], ALU.add)
                    nc.vector.tensor_tensor(mv[:, 1, :], st[:, :, 1], st[:, :, 4], ALU.subtract)
                    link(nc.vector.tensor_tensor(mv[:, 2, :], st[:, :, 2], st[:, :, 5], ALU.add), 2)
                    nc.vector.tensor_scalar(mv[:, 0, :], mv[:, 0, :], 0.5, None, ALU.mult)
                    nc.vector.tensor_scalar(mv[:, 2, :], mv[:, 2, :], 1.0 / E, EPS, ALU.mult, ALU.add)
                    link(nc.vector.scalar_tensor_tensor(out=mv[:, 1, :], in0=mv[:, 1, :], scalar=0.25, in1=mv[:, 1, :],
                                                        op0=ALU.mult, op1=ALU.mult), 3)
                    nc.vector.tensor_tensor(std[:], mv[:, 1, :], mv[:, 2, :], ALU.add).then_inc(var_ok, 1)
                    dve.wait_ge(std_ok, n + 1)
                    link(nc.vector.reciprocal(rstd[:], std[:]), 4)
                    after(dve, tp_ok, n)
                    after(dve, st_xn, 16 * n)
                    for i in range(CT):
                        last = nc.vector.tensor_scalar(xn[:, i, :], xt[:, i, :], mv[:, 0, i:i + 1], rstd[:, i:i + 1],
                                                       ALU.subtract, ALU.mult)
                    last.then_inc(xn_ok, 1)

                def values(n):
                    dve.wait_ge(v_ok, n + 1)
                    after(dve, st_v, 32 * n)
                    for u in range(2):
                        src = pv[:, u, :].rearrange("p (i e) -> p i e", i=2)
                        b = bvb[:].rearrange("p (o e) -> p o e", o=1).broadcast_to([P, 2, E])
                        nc.vector.tensor_tensor(vrow[:, 2 * u:2 * u + 2, :], src, b, ALU.add)
                        for i in range(2):
                            last = nc.vector.tensor_tensor(
                                vx[:, 2 * u + i, :, 0:D], src[:, i, :].rearrange("p (h d) -> p h d", d=D),
                                bvb[:].rearrange("p (h d) -> p h d", d=D), ALU.add)
                    last.then_inc(v_out, 1)

                def relative(n):
                    dve.wait_ge(rel_ok, n + 1)
                    for i in range(CT):
                        o = (i % 2) * RG
                        nc.vector.tensor_tensor(logits[:, n * CT + i, :], pv[:, i // 2, o + RELW:o + RG], gb[:], ALU.add)
                        src = pv[:, i // 2, o:o + RELW].rearrange("p (c m h) -> p c m h", c=2, m=NM)
                        for k in range(KC):
                            last = nc.vector.tensor_tensor(
                                band[:, n * CT + i, :, k * 8:(k + 1) * 8], src[:, k, :, :],
                                c["edge"][:, n * CT + i, :].rearrange("p (m o) -> p m o", o=1).broadcast_to([P, NM, 8]),
                                ALU.add)
                    last.then_inc(rel_out, 1)

                def chunk(n, u, b):
                    if not isinstance(n, int) or n + 1 < NC:
                        normed(n + 1)
                    values(n)
                    dve.wait_ge(part_ok[0], n + 1)
                    after(dve, part_ok[2], n)
                    nc.vector.tensor_tensor(rest[:], qkT[:], part[0][:], ALU.subtract).then_inc(rest_ok, 1)
                    relative(n)
                    dve.wait_ge(part_ok[1], n + 1)
                    after(dve, st_part[2], 16 * 2 * KC * n)
                    nc.vector.tensor_tensor(part[2][:], rest[:], part[1][:], ALU.subtract).then_inc(part_ok[2], 1)
                normed(0)
                dve.wait_ge(w_in, 16 * N_LOAD)
                dve.wait_ge(const_ok, 3)
                chunks(dve, chunk)

            @block.scalar
            def _(act):
                def root(n):
                    act.wait_ge(var_ok, n + 1)
                    nc.scalar.activation(std[:], std[:], ACT.Sqrt).then_inc(std_ok, 1)

                def keep_normed(n, u):
                    act.wait_ge(tp_ok, n + 1)
                    for k in range(KC):
                        last = nc.scalar.copy(xnT[:, u, k, :], pT[:, k, :])
                    last.then_inc(xnT_ok, 1)

                def chunk(n, u, b):
                    more = not isinstance(n, int) or n + 1 < NC
                    if more:
                        root(n + 1)
                    act.wait_ge(qk_ok, n + 1)
                    after(act, rest_ok, n)
                    for a in range(2 * KC):
                        last = nc.scalar.activation(qkT[:, a, :], pqk[:, a, :], ACT.Identity,
                                                    bias=bcol[:, a // KC, a % KC:a % KC + 1],
                                                    scale=float(D) ** -0.5 if a < KC else 1.0)
                    last.then_inc(qkT_ok, 1)
                    act.wait_ge(qkT_ok, n + 1)
                    after(act, st_part[0], 16 * 2 * KC * n)
                    nc.scalar.copy(part[0][:], qkT[:]).then_inc(part_ok[0], 1)
                    if more:
                        keep_normed(n + 1, 1 - u)
                    act.wait_ge(rows_ok, n + 1)
                    after(act, st_rows, 32 * n)
                    for i in range(2):
                        last = nc.scalar.copy(qrow[:, 2 * i:2 * i + 2, :],
                                              pqk[:, i, :].rearrange("p (i e) -> p i e", i=2))
                    last.then_inc(qrow_ok, 1)
                    for i in range(2):
                        last = nc.scalar.copy(krow[:, 2 * i:2 * i + 2, :],
                                              pqk[:, 2 + i, :].rearrange("p (i e) -> p i e", i=2))
                    last.then_inc(krow_ok, 1)
                    act.wait_ge(rest_ok, n + 1)
                    after(act, part_ok[2], n)
                    after(act, st_part[1], 16 * 2 * KC * n)
                    nc.scalar.copy(part[1][:], rest[:]).then_inc(part_ok[1], 1)
                root(0)
                act.wait_ge(w_in, 16 * N_LOAD)
                nc.scalar.mul(bcol[:, 0, :], bcol[:, 0, :], float(D) ** -0.5).then_inc(bias_ok, 1)
                act.wait_ge(bias_ok, 1)
                keep_normed(0, 0)
                chunks(act, chunk)

            @block.tensor
            def _(pe):
                def columns(n):
                    pe.wait_ge(xn_ok, n + 1)
                    after(pe, xnT_ok, n)
                    for k in range(KC):
                        for i in range(CT):
                            last = nc.tensor.transpose(pT[:, k, i * P:(i + 1) * P], xn[:, i, k * P:(k + 1) * P], c["ident"][:])
                    last.then_inc(tp_ok, 1)

                def chunk(n, u, b):
                    pe.wait_ge(xnT_ok, n + 1)
                    for a in range(2 * KC):
                        m = a % KC
                        if m == 0:
                            after(pe, (qrow_ok, krow_ok)[a // KC], n)
                        for k in range(KC):
                            last = nc.tensor.matmul(pqk[:, a, :], w["qk"[a // KC]][:, k, m * P:(m + 1) * P], xnT[:, u, k, :],
                                                    start=(k == 0), stop=(k == KC - 1))
                    last.then_inc(qk_ok, 1)
                    after(pe, rel_out, n)
                    for i in range(CT):
                        for k in range(KC):
                            last = nc.tensor.matmul(pv[:, i // 2, (i % 2) * E:(i % 2 + 1) * E], xnT[:, u, k, i * P:(i + 1) * P],
                                                    w["v"][:, k, :], start=(k == 0), stop=(k == KC - 1))
                    last.then_inc(v_ok, 1)
                    if not isinstance(n, int) or n + 1 < NC:
                        columns(n + 1)
                    pe.wait_ge(qkT_ok, n + 1)
                    for a in range(2):
                        for i in range(CT):
                            for k in range(KC):
                                o = (i % 2) * E + k * P
                                last = nc.tensor.transpose(pqk[:, 2 * a + i // 2, o:o + P],
                                                           qkT[:, a * KC + k, i * P:(i + 1) * P], c["ident"][:])
                    last.then_inc(rows_ok, 1)
                    pe.wait_ge(v_out, n + 1)
                    for i in range(CT):
                        for k in range(KC):
                            o = (i % 2) * RG + k * NM * 8
                            last = nc.tensor.matmul(pv[:, i // 2, o:o + NM * 8], qkT[:, k, i * P:(i + 1) * P],
                                                    rk[:].rearrange("p m h -> p (m h)"), start=True, stop=True)
                        o = (i % 2) * RG + RELW
                        for k in range(KC):
                            last = nc.tensor.matmul(pv[:, i // 2, o:o + X], xnT[:, u, k, i * P:(i + 1) * P], gw[:, k, :],
                                                    start=(k == 0), stop=(k == KC - 1))
                    last.then_inc(rel_ok, 1)
                columns(0)
                pe.wait_ge(w_in, 16 * N_LOAD)
                pe.wait_ge(const_ok, 7)
                chunks(pe, chunk)

            route(nc, block, ctx, logits, rel_out, pT, dst, gates, table, iota_e, slot_expert)


def attention(nc, c, dr, band, bmax, neg, oa, dst, w1, w3, wsum):
    XS = 2 * TB * HG
    PIECES = 3
    HF = XS // X
    MLEAD = 9
    QUOTA = 52
    B1, B2, BP = 3, 3, 3
    with ExitStack() as ctx:
        def sb(name, shape, dt=F32):
            return ctx.enter_context(nc.sbuf_tensor("t_" + name, shape, dt))

        def ps(name, shape, dt=F32):
            return ctx.enter_context(nc.psum_tensor("t_" + name, shape, dt))

        def sem(name):
            return ctx.enter_context(nc.semaphore("t_" + name))

        def sems(name):
            return [sem(f"{name}{i}") for i in range(2)]
        q1 = sb("q1", [P, 2, HG, L], BF16)
        k1 = sb("k1", [P, 2, HG, L], BF16)
        q2 = sb("q2", [P, 2, HG, L], BF16)
        k2 = sb("k2", [P, 2, HG, L], BF16)
        vx = sb("vx", [P, 2, TB, HG * VW])
        pr = sb("pr", [P, BP, HG, CH])
        mx = sb("mx", [P, HG, TB, 2])
        ma = sb("ma", [P, HG, TB])
        mb = sb("mb", [P, HG, TB])
        mparts = sb("mparts", [P, 4, HG, TB], BF16)
        mt = sb("mt", [2 * HG * TB, P], BF16)
        ot = sb("ot", [P, CH])
        zero = sb("zero", [P, 1, E])
        xn = sb("xn", [P, 2, CT, E])
        qw = sb("qw", [P, 2, E])
        kw = sb("kw", [P, 2, NM * E])
        prod = sb("prod", [P, 2, NM, H * D])
        dot = sb("dot", [P, NM * H])
        xn_in, sent, zero_ok, zero_out = sems("xn_in"), sems("sent"), sem("zero_ok"), sem("zero_out")
        win_early, win_in = sems("win_early"), sems("win_in")
        mul_ok, sum_ok, band_ok, bmax_ok = sem("mul_ok"), sem("sum_ok"), sem("band_ok"), sem("bmax_ok")
        s1 = ps("s1", [P, B1, CH])
        s2 = ps("s2", [P, B2, CH])
        po = ps("po", [P, CH])
        misc = ps("misc", [P, CH])
        in1, in2, vin, ones_ok = sems("in1_"), sems("in2_"), sems("vin"), sem("ones_ok")
        zeros_ok, wsum_ok, wsum_in = sem("zeros_ok"), sem("wsum_ok"), sems("wsum_in")
        s1_ok, mx_ok, chain, mparts_ok, mt_ps_ok, mt_ok, m_in = (
            sem("s1_ok"), sem("mx_ok"), sem("chain"), sem("mparts_ok"), sem("mt_ps_ok"), sem("mt_ok"), sem("m_in"))
        s2_ok, exp_ok, pv_ok, ot_ok, otT_ok, oa_ok = (
            sem("s2_ok"), sem("exp_ok"), sem("pv_ok"), sem("ot_ok"), sem("otT_ok"), sem("oa_ok"))
        sq = dr["sq"].rearrange("b g h r c -> (b g) r h c")
        sk = dr["sk"].rearrange("b g h r c -> (b g) r h c")
        vd = dr["vx"].rearrange("(b i p) (g v) -> b g p i v", p=P, i=TB, v=HG * VW)

        def turn(u, n, per_group):
            return (u * per_group + n) % 3

        def freed(g, u, n, per_group):
            return g * per_group + n - 2 + (1 if u == 0 and n < 2 else 0)

        def far_pieces(tile, half):
            a, b = max(tile * P - W, half * CH), min(tile * P + P + W, half * CH + CH)
            return [(a - half * CH, b - a, a - (tile * P - W))] if a < b else []

        def load_window(eng, t, u, came):
            eng.dma_start(qw[:, u, :], q_v[t]).then_inc(came[u], 16)
            eng.dma_start(kw[:, u, :], bass.AP(k_v[t].tensor, k_v[t].offset, [[E, P], [1, NM * E]])).then_inc(came[u], 16)

        q_v = dr["q"].rearrange("(n p) e -> n p e", p=P)
        k_v = dr["k"][0:T, :].rearrange("(n p) e -> n p e", p=P)

        with nc.Block() as block:
            @block.sync
            def _(sp):
                def load1(g, u):
                    for dst, src in ((q1, sq), (k1, sk)):
                        sp.dma_start(dst[0:ROWS, u], src[g]).then_inc(in1[u], 16)

                def load2(g, b, gg, u):
                    for dst, src in ((q2, sq), (k2, sk)):
                        sp.dma_start(dst[0:ROWS, u], src[g]).then_inc(in2[u], 16)
                    sp.dma_start(vx[:, u], vd[b, gg]).then_inc(vin[u], 16)

                def maximum(g, u):
                    sp.wait_ge(mt_ok, g + 1)
                    for j in range(MROWS):
                        sp.dma_start(q2[ROWS + j:ROWS + j + 1, u].rearrange("o h (i t) -> o (h i) t", t=P),
                                     mt[j * HG * TB:(j + 1) * HG * TB, :]).then_inc(m_in, 16)
                zeros = dr["xs"].rearrange("(z p r) e -> z p r e", p=P, r=6)
                load1(0, 0)
                load_window(sp, 0, 0, win_early)
                load_window(sp, 1, 1, win_early)
                load2(0, 0, 0, 0)
                load1(1, 1)
                sp.wait_ge(zero_ok, 1)
                for t in range(2, TB + 2):
                    sp.wait_ge(mul_ok, t - 1)
                    load_window(sp, t, t % 2, win_early)
                    for z in range((t - 2) * N_ZERO // TB, (t - 1) * N_ZERO // TB):
                        sp.dma_start(zeros[z], zero[:].broadcast_to([P, 6, E])).then_inc(zero_out, 16)
                maximum(0, 0)
                load2(1, 0, 1, 1)

                def step(g, b2, g2, u, more1=True, more2=True):
                    if more1:
                        sp.wait_ge(s1_ok, XS * (g + 2))
                        load1(g + 3, 1 - u)
                    maximum(g + 1, 1 - u)
                    if more2:
                        sp.wait_ge(pv_ok, 2 * TB * (g + 1))
                        load2(g + 2, b2, g2, u)
                sp.wait_ge(s1_ok, XS)
                load1(2, 0)
                step(0, 0, 2, 0)
                step(1, 0, 3, 1)
                with sp.Fori(0, NB - 2) as r:
                    for v in range(4):
                        step(4 * r + 2 + v, r + 1, v, v % 2)
                step(10, 3, 0, 0)
                step(11, 3, 1, 1)
                step(12, 3, 2, 0)
                step(13, 3, 3, 1, more1=False)
                step(14, 0, 0, 0, more1=False, more2=False)

            @block.gpsimd
            def _(pool):
                for u in range(2):
                    nc.gpsimd.memset(k2[ROWS:ROWS + MROWS, u], 1.0).then_inc(ones_ok, 1)
                pool.wait_ge(ones_ok, 2)
                nc.gpsimd.memset(zero[:], 0.0).then_inc(zero_ok, 1)
                xn_v = dr["xn"].rearrange("(c i p) e -> c p i e", p=P, i=CT)

                def window_products(t, u, k, more=True):
                    if t < TB + 2:
                        pool.wait_ge(win_early[u], 32 * (k + 1))
                    else:
                        pool.wait_ge(win_in[u], 32 * (k + 1 - (TB + 2) // 2))
                    after(pool, sum_ok, PIECES * (t - 1))
                    nc.gpsimd.tensor_tensor(prod[:, u], kw[:, u, :].rearrange("p (m e) -> p m e", m=NM),
                                            qw[:, u:u + 1, :].broadcast_to([P, NM, E]), ALU.mult).then_inc(mul_ok, 1)
                    if more:
                        pool.wait_ge(mul_ok, t + 1)
                        load_window(pool, t + 2, u, win_in)
                def load_rows(m):
                    after(pool, sent[m % 2], 2 * CT * 16 * (m // 2))
                    pool.dma_start(xn[:, m % 2], xn_v[m]).then_inc(xn_in[m % 2], 16)

                def send(t):
                    m = t // CT
                    if t == 0:
                        pool.wait_ge(zero_out, 16 * N_ZERO)
                    if t % CT == 0:
                        if 1 < m + 1 < NC:
                            load_rows(m + 1)
                        pool.wait_ge(xn_in[m % 2], 16 * (m // 2 + 1))
                    for k in range(2):
                        nc.gpsimd.indirect_dma_start(
                            out=dr["xs"], out_offset=bass.IndirectOffsetOnAxis(ap=dst[:, t, k:k + 1], axis=0),
                            in_=xn[:, m % 2, t % CT, :], in_offset=None).then_inc(sent[m % 2], 16)
                load_rows(0)
                load_rows(1)
                for t in range(NT):
                    window_products(t, t % 2, t // 2, more=TB <= t < NT - 2)
                    if t >= TB:
                        for r in range((t - TB) * NT // (NT - TB), (t - TB + 1) * NT // (NT - TB)):
                            send(r)
                for u in range(2):
                    pool.wait_ge(sent[u], 16 * NT)

            @block.tensor
            def _(pe):
                def pass1(g, u, n):
                    h, i, half, bank = n // (2 * TB), n // 2 % TB, n % 2, turn(u, n, XS)
                    after(pe, mx_ok, freed(g, u, n, XS))
                    far = far_pieces(i, half)
                    last = nc.tensor.matmul(s1[:, bank, :], q1[0:ROWS, u, h, i * P:(i + 1) * P],
                                            k1[0:ROWS, u, h, half * CH:(half + 1) * CH], start=True, stop=not far)
                    for a, m, j in far:
                        last = nc.tensor.matmul(s1[:, bank, a:a + m], c["ident16"][:], c["far"][:, j:j + m],
                                                start=False, stop=True)
                    last.then_inc(s1_ok, 1)

                def pass2(g, u, n):
                    half, i, h, bank = n // (TB * HG), n // HG % TB, n % HG, turn(u, n, XS)
                    after(pe, exp_ok, freed(g, u, n, XS))
                    far = far_pieces(i, half)
                    last = nc.tensor.matmul(s2[:, bank, :], k2[0:ROWS + MROWS, u, h, i * P:(i + 1) * P],
                                            q2[0:ROWS + MROWS, u, h, half * CH:(half + 1) * CH],
                                            start=True, stop=not far)
                    for a, m, j in far:
                        last = nc.tensor.matmul(s2[:, bank, a:a + m], c["ident16"][:], c["far"][:, j:j + m],
                                                start=False, stop=True)
                    last.then_inc(s2_ok, 1)

                def values(g, u, k):
                    half, i = k // TB, k % TB
                    pe.wait_ge(exp_ok, g * XS + HG * (k + 1))
                    if i == 0:
                        after(pe, ot_ok, 2 * g + half)
                    for h in range(HG):
                        last = nc.tensor.matmul(po[h * VW:(h + 1) * VW, :], vx[:, u, i, h * VW:(h + 1) * VW],
                                                pr[:, turn(u, k, 2 * TB), h, :], start=(i == 0), stop=(i == TB - 1),
                                                tile_position=(0, h * VW))
                    last.then_inc(pv_ok, 1)

                def output_rows(g, half, made):
                    pe.wait_ge(ot_ok, 2 * g + half + 1)
                    after(pe, mt_ok, made)
                    after(pe, oa_ok, 2 * g + half)
                    for i in range(CT):
                        last = nc.tensor.transpose(misc[:, i * P:(i + 1) * P], ot[:, i * P:(i + 1) * P], c["ident"][:])
                    last.then_inc(otT_ok, 1)

                def maximum_rows(g, outs):
                    pe.wait_ge(mparts_ok, g + 1)
                    after(pe, oa_ok, outs)
                    nc.tensor.transpose(misc[:, 0:P // 2].bitcast(BF16), mparts[:].rearrange("p j h i -> p (j h i)"),
                                        c["ident16"][:]).then_inc(mt_ps_ok, 1)

                def group(g, u, k, more=True, carried=True):
                    pe.wait_ge(in2[u], 32 * k)
                    pe.wait_ge(vin[u], 16 * k)
                    pe.wait_ge(m_in, 16 * MROWS * (g + 1))
                    if more:
                        pe.wait_ge(in1[1 - u], 32 * (k + u))
                    done = 0
                    for n in range(XS):
                        pass2(g, u, n)
                        while more and done < min(XS, -(-XS * (n + 1) // QUOTA)):
                            pass1(g + 1, 1 - u, done)
                            done += 1
                        if n % HG == 2:
                            if n > HG:
                                values(g, u, n // HG - 1)
                            elif carried:
                                values(g - 1, 1 - u, 2 * TB - 1)
                        if n == 14 and carried:
                            output_rows(g - 1, 1, g + 1)
                        if n == 46:
                            output_rows(g, 0, g + 1)
                        if n == XS - MLEAD and more:
                            maximum_rows(g + 1, 2 * g + 1)

                pe.wait_ge(ones_ok, 2)
                pe.wait_ge(in1[0], 32)
                for n in range(XS):
                    pass1(0, 0, n)
                maximum_rows(0, 0)
                group(0, 0, 1, carried=False)
                with pe.Fori(0, NG // 2 - 1) as r:
                    group(2 * r + 1, 1, r + 1)
                    group(2 * r + 2, 0, r + 2)
                group(NG - 1, 1, NG // 2, more=False)
                values(NG - 1, 1, 2 * TB - 1)
                output_rows(NG - 1, 1, NG)

            @block.vector
            def _(dve):
                CHAIN = 4

                bmax_v = bmax[:].rearrange("p (b i) (g h) -> p b g h i", i=TB, h=HG)
                neg_v = neg[:].rearrange("p (b i) (g h) -> p b g h i", i=TB, h=HG)

                first = [2, 3, 4, 6, 7]

                def window(t, u, piece):
                    M = NM // PIECES
                    if piece < PIECES:
                        dve.wait_ge(mul_ok, t + 1)
                        nc.vector.tensor_reduce(
                            dot[:, piece * M * H:(piece + 1) * M * H],
                            prod[:, u, piece * M:(piece + 1) * M, :].rearrange("p m (h d) -> p (m h) d", d=D),
                            AX.X, ALU.add).then_inc(sum_ok, 1)
                    elif piece == PIECES:
                        dve.wait_ge(sum_ok, PIECES * (t + 1))
                        scores = band[:, t, :, :].rearrange("p m h -> p (m h)")
                        nc.vector.tensor_tensor(scores, scores, dot[:], ALU.add).then_inc(band_ok, 1)
                    else:
                        dve.wait_ge(band_ok, t + 1)
                        nc.vector.tensor_reduce(bmax[:, t, :], band[:, t, :, :].rearrange("p m h -> p h m"),
                                                AX.X, ALU.max).then_inc(bmax_ok, 1)

                def maxima(b, v):
                    def link(ins, k):
                        ins.then_inc(chain, 1)
                        dve.wait_ge(chain, g * CHAIN + k)
                    g, u = NG // NB * b + v, v % 2
                    g0, more = isinstance(b, int) and g == 0, not isinstance(b, int) or b < NB - 1
                    for n in range(XS):
                        if g0 and n % 8 in first:
                            window(n // 8, n // 8 % 2, first.index(n % 8))
                        elif more and n // 4 in range(4, 4 + PIECES + 2) and n % 4 == 0 and not g0:
                            window(TB * (b + 1) + 2 * v, 0, n // 4 - 4)
                        dve.wait_ge(s1_ok, g * XS + n + 1)
                        nc.vector.reduce_max(mx[:, n // (2 * TB), n // 2 % TB, n % 2:n % 2 + 1],
                                             s1[:, turn(u, n, XS), :], AX.X).then_inc(mx_ok, 1)
                    dve.wait_ge(mx_ok, (g + 1) * XS)
                    link(nc.vector.tensor_tensor(ma[:], mx[:, :, :, 0], mx[:, :, :, 1], ALU.max), 1)
                    dve.wait_ge(bmax_ok, TB * (b + 1))
                    link(nc.vector.tensor_tensor(mb[:], ma[:], bmax_v[:, b, v], ALU.max), 2)
                    link(nc.vector.tensor_scalar(mparts[:, 0], mb[:], -1.0, None, ALU.mult), 3)
                    link(nc.vector.scalar_tensor_tensor(out=mparts[:, 1], in0=mb[:], scalar=-1.0, in1=mparts[:, 0],
                                                        op0=ALU.mult, op1=ALU.subtract), 4)
                    nc.vector.tensor_tensor(neg_v[:, b, v], mparts[:, 0], mparts[:, 1], ALU.add).then_inc(mparts_ok, 1)
                    if g0:
                        for piece in range(PIECES + 2):
                            window(TB, 0, piece)
                    if more:
                        for piece in range(PIECES + 2):
                            window(TB * (b + 1) + 2 * v + 1, 1, piece)
                nc.vector.memset(mparts[:], 0.0).then_inc(zeros_ok, 1)
                dve.wait_ge(zeros_ok, 1)
                for v in range(NG // NB):
                    maxima(0, v)
                with dve.Fori(1, NB - 1) as b:
                    for v in range(NG // NB):
                        maxima(b, v)
                for v in range(NG // NB):
                    maxima(NB - 1, v)
                dve.wait_ge(mparts_ok, NG)
                nc.vector.tensor_tensor(band[:], band[:], neg[:].rearrange("p n (o h) -> p n o h", o=1).broadcast_to(
                    [P, NT, NM, H]), ALU.add)

            @block.scalar
            def _(act):
                def copy_sums(g, half):
                    act.wait_ge(pv_ok, 2 * TB * g + TB * (half + 1))
                    after(act, otT_ok, 2 * g + half)
                    nc.scalar.copy(ot[:], po[:]).then_inc(ot_ok, 1)

                oa_v = oa[:].rearrange("p (b s i) (g h) v -> p b s g i h v", i=CT, s=2, h=HG)

                def keep_rows(b, v, half):
                    act.wait_ge(otT_ok, 2 * (NG // NB * b + v) + half + 1)
                    nc.scalar.copy(oa_v[:, b, half, v],
                                   misc[:].rearrange("p (i h v) -> p i h v", h=HG, v=VW)[:, :, :, 0:D + 1]).then_inc(oa_ok, 1)

                def keep_maximum(g):
                    act.wait_ge(mt_ps_ok, g + 1)
                    after(act, m_in, 16 * MROWS * g)
                    nc.scalar.copy(mt[:], misc[0:2 * HG * TB, 0:P // 2].bitcast(BF16)).then_inc(mt_ok, 1)

                wsrc = [a[e].rearrange("(k p) f -> p k f", p=P) for a in (w1, w3) for e in range(X)]

                def load_weights(i):
                    act.dma_start(kw[:, i % 2, 0:KC * F].rearrange("p (k f) -> p k f", k=KC), wsrc[i]).then_inc(wsum_in[i % 2], 16)

                def sum_weights(i):
                    act.wait_ge(wsum_in[i % 2], 16 * (i // 2 + 1))
                    w = kw[:, i % 2, 0:KC * F]
                    nc.scalar.activation(w, w, ACT.Abs, accum_out=wsum[:, i:i + 1]).then_inc(wsum_ok, 1)
                    if i + 2 < 2 * X:
                        act.wait_ge(wsum_ok, i + 1)
                        load_weights(i + 2)

                def exps(b, v, before=None):
                    g, u = NG // NB * b + v, v % 2
                    for n in range(XS):
                        k = n // HG
                        act.wait_ge(s2_ok, g * XS + n + 1)
                        if n % HG == 0:
                            after(act, pv_ok, freed(g, u, k, 2 * TB))
                        nc.scalar.activation(pr[:, turn(u, k, 2 * TB), n % HG], s2[:, turn(u, n, XS)], ACT.Exp).then_inc(exp_ok, 1)
                        if n == 3 and before:
                            copy_sums(g - 1, 1)
                        if n == 16 and before:
                            keep_rows(*before, 1)
                        if n == 36:
                            copy_sums(g, 0)
                        if n == 48:
                            keep_rows(b, v, 0)
                        if n == XS - MLEAD + 1 and not (isinstance(b, int) and g == NG - 1):
                            keep_maximum(g + 1)
                        if isinstance(b, int) and b == NB - 1:
                            if v == 0 and n == XS // 2:
                                act.wait_ge(mul_ok, NT)
                                load_weights(0)
                                load_weights(1)
                            if v in (1, 2) and n % HF == HF // 2:
                                sum_weights(((v - 1) * XS + n) // HF)
                final = NG // NB - 1
                keep_maximum(0)
                exps(0, 0)
                for v in range(1, final + 1):
                    exps(0, v, (0, v - 1))
                with act.Fori(1, NB - 1) as b:
                    exps(b, 0, (b - 1, final))
                    for v in range(1, final + 1):
                        exps(b, v, (b, v - 1))
                for v in range(final + 1):
                    exps(NB - 1, v, (NB - 1, v - 1) if v else (NB - 2, final))
                copy_sums(NG - 1, 1)
                keep_rows(NB - 1, final, 1)


def route(nc, block, ctx, logits, logits_ok, psum, dst, gates, table, iota_e, slot_expert):
    I32 = mybir.dt.int32
    def sb(name, shape, dt=F32):
        return ctx.enter_context(nc.sbuf_tensor("r_" + name, shape, dt))

    def sem(name):
        return ctx.enter_context(nc.semaphore("r_" + name))
    KMAX = T // TS
    iota_k = sb("iota_k", [P, KMAX])
    iota_s = sb("iota_s", [P, NS])
    iota_i = sb("iota_i", [P, NS], I32)
    tri = sb("tri", [P, P], BF16)
    ones = sb("ones", [P, P], BF16)
    m = sb("m", [P, 2, NT])
    eq = sb("eq", [P, NT, X])
    cand = sb("cand", [P, NT, X])
    first = sb("first", [P, 2, NT])
    hot = sb("hot", [P, 2, NT, X])
    rest = sb("rest", [P, NT, X])
    gap = sb("gap", [P, NT])
    eg = sb("eg", [P, NT])
    sg = sb("sg", [P, NT])
    chosen = sb("chosen", [P, NT, X], BF16)
    total = sb("total", [P, NT, X])
    scan = sb("scan", [P, 2, NT, X])
    over = sb("over", [P, X, KMAX])
    slots = sb("slots", [P, X])
    ends = sb("ends", [P, 2, X])
    start = sb("start", [P, X])
    place = sb("place", [P, NT, X])
    pick = sb("pick", [P, 2, NT, X])
    where = sb("where", [P, 2, NT])
    past = sb("past", [P, NS, X])
    pc, pt = psum[:, 0, 0:NT * X], psum[:, 1, 0:NT * X]
    made, chain, gap_ok, eg_ok, chosen_ok, count_ok, dst_ok = (
        sem("made"), sem("chain"), sem("gap_ok"), sem("eg_ok"), sem("chosen_ok"), sem("count_ok"), sem("dst_ok"))
    CONST = 6

    def over_x(a):
        return a.rearrange("p (n o) -> p n o", o=1).broadcast_to([P, NT, X])

    def over_n(a):
        return a.rearrange("p (o e) -> p o e", o=1).broadcast_to([P, NT, X])

    @block.gpsimd
    def _(pool):
        count = [0]

        def then(ins):
            count[0] += 1
            ins.then_inc(made, 1)
            pool.wait_ge(made, count[0])
        then(nc.gpsimd.iota(iota_i[:], [[1, NS]], base=0, channel_multiplier=0))
        then(nc.gpsimd.memset(tri[:], 1.0))
        then(nc.gpsimd.memset(ones[:], 1.0))
        then(nc.gpsimd.affine_select(out=tri[:], in_=tri[:], compare_op=ALU.is_gt, fill=0.0, base=0,
                                     pattern=[[1, P]], channel_multiplier=-1))
        then(nc.gpsimd.tensor_copy(iota_s[:], iota_i[:]))
        then(nc.gpsimd.tensor_copy(iota_e[:], iota_i[:, 0:X]))

    @block.vector
    def _(dve):
        count = [0]

        def then(ins):
            count[0] += 1
            ins.then_inc(chain, 1)
            dve.wait_ge(chain, count[0])
        dve.wait_ge(made, CONST)
        dve.wait_ge(logits_ok, NC)
        then(nc.vector.tensor_scalar(iota_k[:], iota_i[:, 0:KMAX], float(TS), None, ALU.mult))
        for k, src in ((0, logits), (1, rest)):
            then(nc.vector.tensor_reduce(m[:, k, :], src[:], AX.X, ALU.max))
            then(nc.vector.tensor_tensor(eq[:], src[:], over_x(m[:, k, :]), ALU.is_equal))
            then(nc.vector.scalar_tensor_tensor(out=cand[:], in0=eq[:], scalar=-float(X), in1=over_n(iota_e[:]),
                                                op0=ALU.mult, op1=ALU.add))
            then(nc.vector.tensor_reduce(first[:, k, :], cand[:], AX.X, ALU.min))
            then(nc.vector.tensor_scalar_add(first[:, k, :], first[:, k, :], float(X)))
            then(nc.vector.tensor_tensor(hot[:, k], over_n(iota_e[:]), over_x(first[:, k, :]), ALU.is_equal))
            if k == 0:
                then(nc.vector.scalar_tensor_tensor(out=rest[:], in0=hot[:, 0], scalar=FAR, in1=logits[:],
                                                    op0=ALU.mult, op1=ALU.add))
        nc.vector.tensor_tensor(chosen[:], hot[:, 0], hot[:, 1], ALU.add).then_inc(chosen_ok, 1)
        nc.vector.tensor_tensor(gap[:], m[:, 1, :], m[:, 0, :], ALU.subtract).then_inc(gap_ok, 1)
        dve.wait_ge(eg_ok, 1)
        then(nc.vector.tensor_scalar_add(sg[:], eg[:], 1.0))
        then(nc.vector.reciprocal(gates[:, :, 0], sg[:]))
        then(nc.vector.tensor_tensor(gates[:, :, 1], eg[:], gates[:, :, 0], ALU.mult))
        dve.wait_ge(count_ok, 1)
        nc.vector.tensor_copy(total[:], pt.rearrange("p (n e) -> p n e", e=X))
        then(nc.vector.tensor_copy(scan[:, 0], pt.rearrange("p (n e) -> p n e", e=X)))
        a, step = 0, 1
        while step < NT:
            then(nc.vector.tensor_copy(scan[:, 1 - a, 0:step, :], scan[:, a, 0:step, :]))
            then(nc.vector.tensor_tensor(scan[:, 1 - a, step:, :], scan[:, a, step:, :], scan[:, a, 0:NT - step, :], ALU.add))
            a, step = 1 - a, 2 * step
        then(nc.vector.tensor_tensor(over[:], scan[:, a, NT - 1, :].rearrange("p (e o) -> p e o", o=1).broadcast_to([P, X, KMAX]),
                                     iota_k[:].rearrange("p (o k) -> p o k", o=1).broadcast_to([P, X, KMAX]), ALU.is_gt))
        then(nc.vector.tensor_reduce(slots[:], over[:], AX.X, ALU.add))
        then(nc.vector.tensor_copy(ends[:, 0, :], slots[:]))
        b, step = 0, 1
        while step < X:
            then(nc.vector.tensor_copy(ends[:, 1 - b, 0:step], ends[:, b, 0:step]))
            then(nc.vector.tensor_tensor(ends[:, 1 - b, step:], ends[:, b, step:], ends[:, b, 0:X - step], ALU.add))
            b, step = 1 - b, 2 * step
        then(nc.vector.tensor_tensor(start[:], ends[:, b, :], slots[:], ALU.subtract))
        then(nc.vector.tensor_scalar(start[:], start[:], float(TS), None, ALU.mult))
        then(nc.vector.tensor_tensor(place[:], scan[:, a], total[:], ALU.subtract))
        then(nc.vector.tensor_tensor(place[:], place[:], pc.rearrange("p (n e) -> p n e", e=X), ALU.add))
        then(nc.vector.tensor_tensor(place[:], place[:], over_n(start[:]), ALU.add))
        for k in range(2):
            then(nc.vector.tensor_tensor(pick[:, k], hot[:, k], place[:], ALU.mult))
            then(nc.vector.tensor_reduce(where[:, k, :], pick[:, k], AX.X, ALU.add))
        then(nc.vector.tensor_tensor(past[:], iota_s[:].rearrange("p (s o) -> p s o", o=1).broadcast_to([P, NS, X]),
                                     ends[:, b, :].rearrange("p (o e) -> p o e", o=1).broadcast_to([P, NS, X]), ALU.is_ge))
        then(nc.vector.tensor_reduce(slot_expert[:], past[:], AX.X, ALU.add))
        then(nc.vector.tensor_scalar_min(slot_expert[:], slot_expert[:], float(X - 1)))
        then(nc.vector.tensor_copy(table[:], slot_expert[0:1, :]))
        nc.vector.tensor_copy(dst[:], where[:].rearrange("p k n -> p n k")).then_inc(dst_ok, 1)

    @block.scalar
    def _(act):
        act.wait_ge(gap_ok, 1)
        nc.scalar.activation(eg[:], gap[:], ACT.Exp).then_inc(eg_ok, 1)

    @block.tensor
    def _(pe):
        pe.wait_ge(made, CONST)
        pe.wait_ge(chosen_ok, 1)
        nc.tensor.matmul(pc, tri[:], chosen[:].rearrange("p n e -> p (n e)"), start=True, stop=True)
        nc.tensor.matmul(pt, ones[:], chosen[:].rearrange("p n e -> p (n e)"), start=True, stop=True).then_inc(count_ok, 1)


def finish_and_experts(nc, c, dr, x, Wo, bo, rel_v, band, oa, w1, w3, w2, table, iota_e, slot_expert, wsum):
    with ExitStack() as ctx:
        def sb(name, shape, dt=F32):
            return ctx.enter_context(nc.sbuf_tensor("e_" + name, shape, dt))

        def ps(name, shape, dt=F32):
            return ctx.enter_context(nc.psum_tensor("e_" + name, shape, dt))

        def sem(name):
            return ctx.enter_context(nc.semaphore("e_" + name))

        def sems(name):
            return [sem(f"{name}{i}") for i in range(2)]
        ST = TS // P
        LAG = 2
        PA = 3
        XUP, WUP, TINY = 2.0 ** 11, 2.0 ** 14, 1e-30
        NPC = 4
        SPLITS = ((0,), (1,), (2,), (3,), (4, 5), (6,), (7,), ())
        ws = sb("ws", [P, 2, KC, F])
        wh = sb("wh", [P, 2, 2, KC, F], F16)
        wl = sb("wl", [P, 2, 2, KC, F], F16)
        w2s = sb("w2s", [P, 2, FC, E])
        bound = sb("bound", [P, 2, X])
        ones = sb("ones", [2 * X, P])
        diag = sb("diag", [2 * X, 2 * X])
        wmax = sb("wmax", [2 * X, 1])
        slot_is = sb("slot_is", [P, NS, X])
        picked = sb("picked", [P, NS, X])
        slot_bound = sb("slot_bound", [P, 2, NS])
        up = sb("up", [P, 2, NS])
        down = sb("down", [P, 2, NS])
        xr = sb("xr", [P, 2, ST, E])
        xh = sb("xh", [P, 2, KC, TS], F16)
        xl = sb("xl", [P, 2, KC, TS], F16)
        sg = sb("sg", [P, 2, TS])
        hT = sb("hT", [P, FC, TS])
        y = sb("y", [P, 2, ST, E])
        px = ps("px", [P, KC, TS])
        pa = ps("pa", [P, PA, 2, TS])
        py = ps("py", [P, ST, CH])
        w_in, x_in, y_out = sems("w_in"), sems("x_in"), sems("y_out")
        xt_ps, xt_ok, a_ok, g_ok, h_ok, y_ps, y_ok = (
            sem("xt_ps"), sem("xt_ok"), sem("a_ok"), sem("g_ok"), sem("h_ok"), sem("y_ps"), sem("y_ok"))
        ws_in, wh_ok, wl_ok, xl_ok, setup, ones_ok, wt_ok, wb_ok = (
            sems("ws_in"), sem("wh_ok"), sem("wl_ok"), sem("xl_ok"), sem("setup"), sem("ones_ok"), sem("wt_ok"), sem("wb_ok"))
        xs = dr["xs"].rearrange("(s i p) e -> s p i e", p=P, i=ST)
        ys = dr["ys"].rearrange("(s i p) e -> s p i e", p=P, i=ST)

        M0 = P // H
        R1 = (NM - M0) * H
        SETUP = 11
        TSLOTS = NT
        wo = sb("wo", [P, KC, E])
        bob = sb("bob", [P, E])
        rv = sb("rv", [P, 2, D])
        pick = sb("pick", [P, H, M0])
        hsel = sb("hsel", [P, H])
        rvm = sb("rvm", [P, 2, H, D])
        vs = sb("vs", [P, 2, NM, E])
        xt = sb("xt", [P, 2, E])
        xb = sb("xb", [P, 2, E])
        e = sb("e", [P, 2, NM * H])
        prod = sb("prod", [P, 2, NM, E])
        eT0 = sb("eT0", [P, 2, P])
        eT1 = sb("eT1", [R1, 2, P])
        es = sb("es", [P, H])
        z = sb("z", [P, H])
        rz = sb("rz", [P, H])
        o1 = sb("o1", [P, E])
        o2 = sb("o2", [P, E])
        o3 = sb("o3", [P, E])
        on = sb("on", [P, 2, E])
        onT = sb("onT", [P, 2, KC, P])
        pcol = ps("pcol", [P, 2, E])
        prow = ps("prow", [P, 2, E])
        c_in, set_ok, v_in = sem("c_in"), sem("set_ok"), sems("v_in")
        band_ok, e_ok, prod_ok, et_ps_ok, et_ok, rv_ok = (
            sem("band_ok"), sem("e_ok"), sem("prod_ok"), sem("et_ps_ok"), sem("et_ok"), sem("rv_ok"))
        chain, on_ok, on_ps_ok, ont_ok, att_ok, res_ok = (
            sem("chain"), sem("on_ok"), sem("on_ps_ok"), sem("ont_ok"), sem("att_ok"), sem("res_ok"))
        x_v = x.rearrange("(n p) e -> n p e", p=P)
        res = oa[:].rearrange("p n h v -> p n (h v)")[:, :, 0:E]

        def windows(n):
            v = dr["v"][0:T, :].rearrange("(n p) e -> n p e", p=P)[n]
            return bass.AP(v.tensor, v.offset, [[E, P], [1, NM * E]])

        def slots(eng, body):
            for s in (0, 1, 2):
                body(s, s % 2, s // 2)
            with eng.Fori(1, TSLOTS // 2 - 2) as r:
                body(2 * r + 1, 1, r)
                body(2 * r + 2, 0, r + 1)
            for s in range(TSLOTS - 3, TSLOTS + 1):
                body(s, s % 2, s // 2)
            with eng.Fori(TSLOTS // 2, (NS - 3) // 2) as r:
                body(2 * r + 1, 1, r, tiles=False)
                body(2 * r + 2, 0, r + 1, tiles=False)
            for s in (NS - 2, NS - 1):
                body(s, s % 2, s // 2, tiles=False)

        def stages(s, u, f, tiles, table):
            if tiles:
                for stage, behind in table.get(f, ()):
                    t = s - behind
                    if not isinstance(t, int) or 0 <= t < NT:
                        stage(t, (u + behind) % 2)

        with nc.Block() as block:
            @block.sync
            def _(sp):
                def expert(s):
                    return sp.value_load(table[0:1, bass.ds(s, 1)], min_val=0, max_val=X - 1)

                def load(s, u):
                    sp.dma_start(xr[:, u], xs[s]).then_inc(x_in[u], 16)
                    sp.dma_start(w2s[:, u], w2[expert(s)].rearrange("(k p) f -> p k f", p=P)).then_inc(w_in[u], 16)

                def load_split(s, m):
                    after(sp, wl_ok, 2 * NPC * s - (NPC if m == 0 else 0))
                    sp.dma_start(ws[:, m], (w1, w3)[m][expert(s)].rearrange("(k p) f -> p k f", p=P)).then_inc(ws_in[m], 16)

                def slot(s, u, k, tiles=True):
                    if not isinstance(s, int) or 0 < s < NS - 1:
                        sp.wait_ge(y_ps, s)
                        load(s + 1, 1 - u)
                    if not isinstance(s, int) or s < NS - 2:
                        load_split(s + 2, 0)
                        load_split(s + 2, 1)
                load_split(0, 0)
                load_split(0, 1)
                load(0, 0)
                sp.dma_start(wo[:], Wo.rearrange("(k p) e -> p k e", p=P)).then_inc(c_in, 16)
                sp.dma_start(bob[:], bo.rearrange("(o e) -> o e", o=1).broadcast_to([P, E])).then_inc(c_in, 16)
                for m in range(NM):
                    r = m % M0 * H
                    sp.dma_start(rv[r:r + H, m // M0, :], rel_v[0, m:m + 1, :].broadcast_to([H, D])).then_inc(c_in, 16)
                load_split(1, 0)
                load_split(1, 1)
                load(1, 1)
                slots(sp, slot)

            @block.gpsimd
            def _(pool):
                def put(s, u, k):
                    pool.wait_ge(y_ok, s + 1)
                    pool.dma_start(ys[s], y[:, u]).then_inc(y_out[u], 16)

                def load_tile(t, u):
                    pool.dma_start(vs[:, u].rearrange("p m e -> p (m e)"), windows(t)).then_inc(v_in[u], 16)
                    pool.dma_start(xt[:, u, :], x_v[t]).then_inc(v_in[u], 16)

                def products(t, u, k):
                    pool.wait_ge(v_in[u], 32 * (k + 1))
                    after(pool, res_ok, t - 1)
                    nc.gpsimd.tensor_tensor(xb[:, u, :], xt[:, u, :], bob[:], ALU.add)
                    after(pool, on_ok, t - 1)
                    nc.gpsimd.tensor_tensor(
                        prod[:, u].rearrange("p m (h d) -> p (m h) d", d=D),
                        vs[:, u].rearrange("p m (h d) -> p (m h) d", d=D),
                        e[:, u, :].rearrange("p (q o) -> p q o", o=1).broadcast_to([P, NM * H, D]),
                        ALU.mult).then_inc(prod_ok, 1)
                    if not isinstance(t, int) or t + 2 < NT:
                        pool.wait_ge(prod_ok, t + 1)
                        load_tile(t + 2, u)

                def slot(s, u, k, tiles=True):
                    tiles = tiles and not (isinstance(s, int) and s >= TSLOTS)
                    if tiles:
                        pool.wait_ge(e_ok, s + 1)
                        products(s, u, k)
                    if not isinstance(s, int) or s > 0:
                        put(s - 1, 1 - u, k)
                nc.gpsimd.memset(ones[:], 1.0).then_inc(ones_ok, 1)
                load_tile(0, 0)
                load_tile(1, 1)
                nc.gpsimd.memset(pick[:], 0.0).then_inc(set_ok, 1)
                pool.wait_ge(set_ok, 1)
                nc.gpsimd.affine_select(out=pick[:], in_=pick[:], compare_op=ALU.not_equal, fill=1.0, base=0,
                                        pattern=[[-1, H], [-H, M0]], channel_multiplier=1).then_inc(set_ok, 1)
                pool.wait_ge(c_in, 16 * (2 + NM))
                slots(pool, slot)
                put(NS - 1, (NS - 1) % 2, 0)
                pool.wait_ge(y_out[0], 16 * ((NS + 1) // 2))
                pool.wait_ge(y_out[1], 16 * (NS // 2))

            @block.tensor
            def _(pe):
                def columns(s, u, k):
                    pe.wait_ge(x_in[u], 16 * (k + 1))
                    after(pe, xl_ok, s)
                    for j in range(KC):
                        for i in range(ST):
                            last = nc.tensor.transpose(px[:, j, i * P:(i + 1) * P], xr[:, u, i, j * P:(j + 1) * P], c["ident"][:])
                    last.then_inc(xt_ps, 1)

                def hidden(s, u, f):
                    before = f - PA if f >= PA else max(g for g in range(FC) if g % PA == f % PA) - FC
                    after(pe, h_ok, s * FC + before + 1)
                    for j in range(2):
                        parts = [(w, x, k) for w, x in ((wh, xh), (wh, xl), (wl, xh)) for k in range(KC)]
                        for i, (w, x, k) in enumerate(parts):
                            last = nc.tensor.matmul(pa[:, f % PA, j, :], w[:, u, j, k, f * P:(f + 1) * P], x[:, u, k, :],
                                                    start=(i == 0), stop=(i == len(parts) - 1))
                    last.then_inc(a_ok, 1)

                def outputs(s, u, f):
                    pe.wait_ge(h_ok, s * FC + f + 1)
                    if f == 0:
                        after(pe, y_ok, s)
                    for i in range(ST):
                        last = nc.tensor.matmul(py[:, i, 0:E], hT[:, f, i * P:(i + 1) * P], w2s[:, u, f, :],
                                                start=(f == 0), stop=(f == FC - 1))
                    if f == FC - 1:
                        last.then_inc(y_ps, 1)

                def exp_columns(t, j):
                    pe.wait_ge(e_ok, t + 1)
                    after(pe, ont_ok, t)
                    nc.tensor.transpose(pcol[:, 0, 0:P], e[:, j, 0:P], c["ident"][:])
                    nc.tensor.transpose(pcol[0:R1, 0, P:2 * P], e[:, j, P:P + R1], c["ident"][:]).then_inc(et_ps_ok, 1)

                def relative(t, j):
                    if isinstance(t, int) and t == 0:
                        pe.wait_ge(chain, 2)
                    pe.wait_ge(et_ok, t + 1)
                    after(pe, on_ok, t)
                    after(pe, res_ok, t)
                    nc.tensor.matmul(prow[:, 0, :], eT0[:, j, :], rvm[:, 0].rearrange("p h d -> p (h d)"), start=True, stop=False)
                    nc.tensor.matmul(prow[:, 0, :], eT1[:, j, :], rvm[0:R1, 1].rearrange("p h d -> p (h d)"),
                                     start=False, stop=True).then_inc(rv_ok, 1)

                def row_columns(t, j):
                    pe.wait_ge(on_ok, t + 1)
                    pe.wait_ge(et_ok, t + 1)
                    for k in range(KC):
                        last = nc.tensor.transpose(pcol[:, 1, k * P:(k + 1) * P], on[:, j, k * P:(k + 1) * P], c["ident"][:])
                    last.then_inc(on_ps_ok, 1)

                def project(t, j):
                    if isinstance(t, int) and t == 0:
                        pe.wait_ge(c_in, 16 * (2 + NM))
                    pe.wait_ge(ont_ok, t + 1)
                    for k in range(KC):
                        last = nc.tensor.matmul(prow[:, 1, :], onT[:, j, k, :], wo[:, k, :], start=(k == 0), stop=(k == KC - 1))
                    last.then_inc(att_ok, 1)

                def slot(s, u, k, tiles=True):
                    first, final = isinstance(s, int) and s == 0, isinstance(s, int) and s == NS - 1
                    if first:
                        columns(0, 0, 0)
                    pe.wait_ge(xl_ok, s + 1)
                    pe.wait_ge(wl_ok, 2 * NPC * (s + 1))
                    for f in range(FC):
                        hidden(s, u, f)
                        if f == LAG:
                            pe.wait_ge(w_in[u], 16 * (k + 1))
                        if f >= LAG:
                            outputs(s, u, f - LAG)
                        elif not first:
                            outputs(s - 1, 1 - u, FC - LAG + f)
                        if f == FC - 3 and not final:
                            columns(s + 1, 1 - u, k + u)
                        stages(s, u, f, tiles, {0: [(row_columns, 1)], 2: [(project, 1), (exp_columns, 0)],
                                                5: [(relative, 0)]})
                    if final:
                        for f in range(FC - LAG, FC):
                            outputs(s, u, f)
                nc.tensor.transpose(px[0:2 * X, 0, 0:P], wsum[:], c["ident"][:]).then_inc(wt_ok, 1)
                pe.wait_ge(setup, 2)
                pe.wait_ge(ones_ok, 1)
                nc.tensor.matmul(px[:, 1, 0:2 * X], ones[:], diag[:], start=True, stop=True).then_inc(wb_ok, 1)
                pe.wait_ge(setup, 3)
                slots(pe, slot)

            @block.scalar
            def _(act):
                def keep_columns(s, u):
                    act.wait_ge(xt_ps, s + 1)
                    nc.scalar.activation(xh[:, u], px[:], ACT.Copy, scale=XUP).then_inc(xt_ok, 1)

                def split_high(s, u, m, piece):
                    if piece == 0:
                        act.wait_ge(ws_in[m], 16 * (s + 1))
                    w = F // 2
                    k, cols = piece // 2, slice(piece % 2 * w, (piece % 2 + 1) * w)
                    nc.scalar.activation(wh[:, u, m, k, cols], ws[:, m, k, cols], ACT.Copy,
                                         scale=up[:, m, bass.ds(s, 1)]).then_inc(wh_ok, 1)

                def keep_outputs(s, u, k):
                    act.wait_ge(y_ps, s + 1)
                    after(act, y_out[u], 16 * k)
                    nc.scalar.copy(y[:, u], py[:, :, 0:E]).then_inc(y_ok, 1)

                def take_exps(t, u):
                    after(act, on_ok, t - 1)
                    nc.scalar.copy(e[:, u], band[:, t].rearrange("p m h -> p (m h)")).then_inc(e_ok, 1)

                def keep_exp_columns(t, j):
                    act.wait_ge(et_ps_ok, t + 1)
                    nc.scalar.copy(eT0[:, j, :], pcol[:, 0, 0:P])
                    nc.scalar.copy(eT1[:, j, :], pcol[0:R1, 0, P:2 * P]).then_inc(et_ok, 1)

                def keep_row_columns(t, j):
                    act.wait_ge(on_ps_ok, t + 1)
                    nc.scalar.copy(onT[:, j], pcol[:, 1, :].rearrange("p (k t) -> p k t", k=KC)).then_inc(ont_ok, 1)

                def slot(s, u, k, tiles=True):
                    first, final = isinstance(s, int) and s == 0, isinstance(s, int) and s == NS - 1
                    if first:
                        nc.scalar.activation(band[:].rearrange("p n m h -> p (n m h)"),
                                             band[:].rearrange("p n m h -> p (n m h)"), ACT.Exp).then_inc(band_ok, 1)
                        act.wait_ge(band_ok, 1)
                        act.wait_ge(setup, SETUP)
                        keep_columns(0, 0)
                        for n in range(2 * NPC):
                            split_high(0, 0, n // NPC, n % NPC)
                    for f in range(FC):
                        act.wait_ge(a_ok, s * FC + f + 1)
                        after(act, h_ok, s * FC + f - 1)
                        nc.scalar.activation(sg[:, f % 2, :], pa[:, f % PA, 0, :], ACT.Silu,
                                             scale=down[:, 0, bass.ds(s, 1)]).then_inc(g_ok, 1)
                        if not final:
                            for n in SPLITS[f]:
                                split_high(s + 1, 1 - u, n // NPC, n % NPC)
                        if f == 0 and tiles and not (isinstance(s, int) and s >= TSLOTS):
                            take_exps(s, u)
                        if f == LAG - 1 and not first:
                            keep_outputs(s - 1, 1 - u, k if u else k - 1)
                        if f == FC - 2 and not final:
                            keep_columns(s + 1, 1 - u)
                        stages(s, u, f, tiles, {1: [(keep_row_columns, 1)], 3: [(keep_exp_columns, 0)]})
                    if final:
                        keep_outputs(s, u, k)
                slots(act, slot)

            @block.vector
            def _(dve):
                BASE, STEPS = 2, 7

                def link(ins):
                    ins.then_inc(chain, 1)

                def linked(t, k):
                    dve.wait_ge(chain, t * STEPS + BASE + k)

                def totals(t, j):
                    dve.wait_ge(e_ok, t + 1)
                    link(nc.vector.tensor_reduce(es[:], e[:, j, :].rearrange("p (m h) -> p h m", h=H), AX.X, ALU.add))
                    linked(t, 1)
                    link(nc.vector.tensor_tensor(z[:], es[:], oa[:, t, :, D], ALU.add))
                    linked(t, 2)
                    link(nc.vector.reciprocal(rz[:], z[:]))

                def window_sum(t, j, part):
                    dve.wait_ge(prod_ok, t + 1)
                    cols = slice(part * P, (part + 1) * P)
                    link(nc.vector.tensor_reduce(o1[:, cols], prod[:, j, :, cols].rearrange("p m e -> p e m"), AX.X, ALU.add))

                def rows(t, j):
                    linked(t, 5)
                    link(nc.vector.tensor_tensor(o2[:].rearrange("p (h d) -> p h d", d=D), o1[:].rearrange("p (h d) -> p h d", d=D),
                                                 oa[:, t, :, 0:D], ALU.add))
                    dve.wait_ge(rv_ok, t + 1)
                    after(dve, att_ok, t)
                    linked(t, 6)
                    link(nc.vector.tensor_tensor(o3[:], o2[:], prow[:, 0, :], ALU.add))
                    linked(t, 7)
                    after(dve, on_ps_ok, t - 1)
                    nc.vector.tensor_tensor(on[:, j, :].rearrange("p (h d) -> p h d", d=D),
                                            o3[:].rearrange("p (h d) -> p h d", d=D),
                                            rz[:].rearrange("p (h o) -> p h o", o=1).broadcast_to([P, H, D]),
                                            ALU.mult).then_inc(on_ok, 1)

                def result(t, j):
                    dve.wait_ge(att_ok, t + 1)
                    nc.vector.tensor_tensor(res[:, t, :], prow[:, 1, :], xb[:, j, :], ALU.add).then_inc(res_ok, 1)

                def columns_low(s, u):
                    dve.wait_ge(xt_ok, s + 1)
                    nc.vector.scalar_tensor_tensor(out=xl[:, u], in0=px[:], scalar=XUP, in1=xh[:, u],
                                                   op0=ALU.mult, op1=ALU.subtract).then_inc(xl_ok, 1)

                def split_low(s, u, m, piece):
                    dve.wait_ge(wh_ok, 2 * NPC * s + NPC * m + piece + 1)
                    w = F // 2
                    k, cols = piece // 2, slice(piece % 2 * w, (piece % 2 + 1) * w)
                    nc.vector.scalar_tensor_tensor(out=wl[:, u, m, k, cols], in0=ws[:, m, k, cols], scalar=up[:, m, bass.ds(s, 1)],
                                                   in1=wh[:, u, m, k, cols], op0=ALU.mult, op1=ALU.subtract).then_inc(wl_ok, 1)

                def slot(s, u, k, tiles=True):
                    first, final = isinstance(s, int) and s == 0, isinstance(s, int) and s == NS - 1
                    for f in range(FC):
                        dve.wait_ge(g_ok, s * FC + f + 1)
                        nc.vector.scalar_tensor_tensor(out=hT[:, f, :], in0=pa[:, f % PA, 1, :], scalar=down[:, 1, bass.ds(s, 1)],
                                                       in1=sg[:, f % 2, :], op0=ALU.mult, op1=ALU.mult).then_inc(h_ok, 1)
                        if not final:
                            for n in SPLITS[f]:
                                split_low(s + 1, 1 - u, n // NPC, n % NPC)
                        if f == FC - 2 and not final:
                            columns_low(s + 1, 1 - u)
                        stages(s, u, f, tiles, {
                            3: [(result, 1), (totals, 0)], 4: [(lambda t, j: window_sum(t, j, 0), 0)],
                            5: [(lambda t, j: window_sum(t, j, 1), 0)], 7: [(rows, 0)]})
                steps = [0]

                def then(ins):
                    steps[0] += 1
                    ins.then_inc(setup, 1)
                    dve.wait_ge(setup, steps[0])
                dve.wait_ge(wt_ok, 1)
                then(nc.vector.tensor_reduce(wmax[:], px[0:2 * X, 0, 0:P], AX.X, ALU.max))
                then(nc.vector.tensor_scalar(diag[:], c["ident"][0:2 * X, 0:2 * X], wmax[:, 0:1], None, ALU.mult))
                dve.wait_ge(wb_ok, 1)
                then(nc.vector.tensor_scalar_max(bound[:].rearrange("p m e -> p (m e)"), px[:, 1, 0:2 * X], TINY))
                then(nc.vector.tensor_tensor(slot_is[:], iota_e[:].rearrange("p (o e) -> p o e", o=1).broadcast_to([P, NS, X]),
                                             slot_expert[:].rearrange("p (s o) -> p s o", o=1).broadcast_to([P, NS, X]),
                                             ALU.is_equal))
                for m in range(2):
                    then(nc.vector.tensor_tensor(picked[:], slot_is[:],
                                                 bound[:, m:m + 1, :].broadcast_to([P, NS, X]), ALU.mult))
                    then(nc.vector.tensor_reduce(slot_bound[:, m, :], picked[:], AX.X, ALU.add))
                then(nc.vector.reciprocal(up[:], slot_bound[:]))
                then(nc.vector.tensor_scalar(up[:], up[:], WUP, None, ALU.mult))
                then(nc.vector.tensor_scalar(down[:], slot_bound[:], 1.0 / (WUP * XUP), None, ALU.mult))
                assert steps[0] == SETUP
                columns_low(0, 0)
                for n in range(2 * NPC):
                    split_low(0, 0, n // NPC, n % NPC)
                dve.wait_ge(set_ok, 2)
                nc.vector.tensor_reduce(hsel[:], pick[:], AX.X, ALU.add).then_inc(chain, 1)
                dve.wait_ge(chain, 1)
                dve.wait_ge(c_in, 16 * (2 + NM))
                for k, rows_in in ((0, P), (1, R1)):
                    last = nc.vector.tensor_tensor(
                        rvm[0:rows_in, k], rv[0:rows_in, k, :].rearrange("p (o d) -> p o d", o=1).broadcast_to([rows_in, H, D]),
                        hsel[0:rows_in, :].rearrange("p (h o) -> p h o", o=1).broadcast_to([rows_in, H, D]), ALU.mult)
                last.then_inc(chain, 1)
                slots(dve, slot)


def combine(nc, dr, dst, gates, res, out):
    with ExitStack() as ctx:
        def sb(name, shape, dt=F32):
            return ctx.enter_context(nc.sbuf_tensor("c_" + name, shape, dt))

        def sem(name):
            return ctx.enter_context(nc.semaphore("c_" + name))
        BUF = 4
        y = sb("y", [P, BUF, 2, E])
        half = sb("half", [P, BUF, E])
        o = sb("o", [P, BUF, E])
        y_in, part_ok, o_ok, o_out = (
            [sem(f"y_in{i}") for i in range(BUF)], sem("part_ok"), sem("o_ok"), [sem(f"o_out{i}") for i in range(BUF)])
        out_v = out.rearrange("(n p) e -> n p e", p=P)
        with nc.Block() as block:
            @block.gpsimd
            def _(pool):
                for t in range(NT):
                    u = t % BUF
                    after(pool, o_ok, t - BUF + 1)
                    for k in range(2):
                        nc.gpsimd.indirect_dma_start(
                            out=y[:, u, k, :], out_offset=None, in_=dr["ys"],
                            in_offset=bass.IndirectOffsetOnAxis(ap=dst[:, t, k:k + 1], axis=0)).then_inc(y_in[u], 16)

            def tiles(eng, body):
                for u in range(BUF):
                    body(u, u, 0)
                with eng.Fori(1, NT // BUF) as r:
                    for u in range(BUF):
                        body(BUF * r + u, u, r)

            @block.vector
            def _(dve):
                def weigh(t, u, r):
                    dve.wait_ge(y_in[u], 32 * (r + 1))
                    after(dve, o_out[u], 16 * r)
                    nc.vector.scalar_tensor_tensor(out=half[:, u, :], in0=y[:, u, 0, :], scalar=gates[:, t, 0:1],
                                                   in1=res[:, t, :], op0=ALU.mult, op1=ALU.add).then_inc(part_ok, 1)
                    dve.wait_ge(part_ok, t + 1)
                    nc.vector.scalar_tensor_tensor(out=o[:, u, :], in0=y[:, u, 1, :], scalar=gates[:, t, 1:2],
                                                   in1=half[:, u, :], op0=ALU.mult, op1=ALU.add).then_inc(o_ok, 1)
                tiles(dve, weigh)

            @block.sync
            def _(sp):
                def store(t, u, r):
                    sp.wait_ge(o_ok, t + 1)
                    sp.dma_start(out_v[t], o[:, u, :]).then_inc(o_out[u], 16)
                tiles(sp, store)
                for u in range(BUF):
                    sp.wait_ge(o_out[u], 16 * NT // BUF)


def constants(nc, c):
    with ExitStack() as ctx:
        made = ctx.enter_context(nc.semaphore("const_made"))
        with nc.Block() as block:
            @block.gpsimd
            def _(pool):
                count = [0]

                def then(ins):
                    count[0] += 1
                    ins.then_inc(made, 1)
                    pool.wait_ge(made, count[0])
                for m in (c["ident"], c["ident16"]):
                    then(nc.gpsimd.memset(m[:], 0.0))
                    then(nc.gpsimd.affine_select(out=m[:], in_=m[:], compare_op=ALU.not_equal, fill=1.0, base=0,
                                                 pattern=[[-1, P]], channel_multiplier=1))
                then(nc.gpsimd.memset(c["far"][:], FAR))
                then(nc.gpsimd.affine_select(out=c["far"][:], in_=c["far"][:], compare_op=ALU.is_ge, fill=0.0, base=0,
                                             pattern=[[1, BW]], channel_multiplier=-1))
                then(nc.gpsimd.affine_select(out=c["far"][:], in_=c["far"][:], compare_op=ALU.is_ge, fill=0.0, base=2 * W,
                                             pattern=[[-1, BW]], channel_multiplier=1))
                then(nc.gpsimd.memset(c["edge"][:], 0.0))
                first = c["edge"][:].rearrange("p (b i) m -> p b i m", i=TB)[:, :, 0, :]
                final = c["edge"][:].rearrange("p (b i) m -> p b i m", i=TB)[:, :, TB - 1, :]
                then(nc.gpsimd.affine_select(out=first, in_=first, compare_op=ALU.is_ge, fill=FAR, base=-W,
                                             pattern=[[0, NB], [1, NM]], channel_multiplier=1))
                then(nc.gpsimd.affine_select(out=final, in_=final, compare_op=ALU.is_ge, fill=FAR, base=P - 1 + W,
                                             pattern=[[0, NB], [-1, NM]], channel_multiplier=-1))


def build(nc, x, Wq, bq, Wk, bk, Wv, bv, Wo, bo, rel_k, rel_v, gate_w, gate_b, w1, w3, w2, out):
    with ExitStack() as ctx:
        def sb(name, shape, dt=F32):
            return ctx.enter_context(nc.sbuf_tensor(name, shape, dt))
        c = dict(ident=sb("ident", [P, P]), ident16=sb("ident16", [P, P], BF16), far=sb("far", [P, BW], BF16),
                 edge=sb("edge", [P, NT, NM]))
        nc.disable_value_cache = True
        x = x.rearrange("b l e -> (b l) e")
        out = out.rearrange("b l e -> (b l) e")
        dr = scratch(nc)
        band = sb("band", [P, NT, NM, H])
        neg = sb("neg", [P, NT, H])
        oa = sb("oa", [P, NT, H, D + 1])
        dst = sb("dst", [P, NT, 2], mybir.dt.int32)
        gates = sb("gates", [P, NT, 2])
        table = sb("table", [1, NS], mybir.dt.int32)
        slot_expert = sb("slot_expert", [P, NS])
        iota_e = sb("iota_e", [P, X])
        wsum = sb("wsum", [P, 2 * X])
        constants(nc, c)
        with ExitStack() as early:
            def sb_early(name, shape, dt=F32):
                return early.enter_context(nc.sbuf_tensor(name, shape, dt))
            bmax = sb_early("bmax", [P, NT, H])
            norm_and_project(nc, c, dr, x, Wq, bq, Wk, bk, Wv, bv, rel_k, gate_w, gate_b, band, dst, gates, table, iota_e, slot_expert)
            attention(nc, c, dr, band, bmax, neg, oa, dst, w1, w3, wsum)
        finish_and_experts(nc, c, dr, x, Wo, bo, rel_v, band, oa, w1, w3, w2, table, iota_e, slot_expert, wsum)
        combine(nc, dr, dst, gates, oa[:].rearrange("p n h v -> p n (h v)")[:, :, 0:E], out)


_INS = ['L0_attn_hidden_states', 'L0_attn_Wq', 'L0_attn_bq', 'L0_attn_Wk', 'L0_attn_bk', 'L0_attn_Wv', 'L0_attn_bv',
        'L0_attn_Wo', 'L0_attn_bo', 'L0_attn_emb_rel_k', 'L0_attn_emb_rel_v', 'L0_ffn_gate_w', 'L0_ffn_gate_b',
        'L0_ffn_w1', 'L0_ffn_w3', 'L0_ffn_w2']


def kernel(**inputs):
    import numpy as _np
    import concourse.bacc as _bacc
    from concourse.bass_utils import run_bass_kernel_spmd as _run

    nc = _bacc.Bacc("TRN2", target_bir_lowering=False, num_devices=1)
    arrays, args = {}, []
    for name in _INS:
        a = _np.ascontiguousarray(inputs[name])
        arrays[f"in_{name}_dram"] = a
        args.append(nc.dram_tensor(f"in_{name}_dram", a.shape, mybir.dt.from_np(a.dtype), kind="ExternalInput").ap())
    args.append(nc.dram_tensor("out_0_dram", (NB, L, E), F32, kind="ExternalOutput").ap())
    build(nc, *args)
    r = _run(nc, [arrays], core_ids=[0])
    return r.results[0]["out_0_dram"]
```
